# Optimizing a Trainium2 kernel written in Bass

```python
import numpy as np
import jax
import jax.numpy as jnp

def _softmax(x, axis=-1):
    return jax.nn.softmax(x, axis=axis)

def _gelu(x):
    return jax.nn.gelu(x, approximate=True)

def _silu(x):
    return jax.nn.silu(x)

def _sigmoid(x):
    return jax.nn.sigmoid(x)

def _layernorm(x, axis=-1, eps=1e-05):
    m = jnp.mean(x, axis=axis, keepdims=True)
    v = jnp.var(x, axis=axis, keepdims=True)
    return (x - m) / jnp.sqrt(v + eps)

def _scatter_add(tgt, idx, src, axis=0):
    return tgt.at[idx].add(src)

def _segment_sum(src, seg, n):
    return jax.ops.segment_sum(src, seg, n)
kernel_name = 'mk_vit_tower_cls_d2_tok_img2048_r4_7a0588'

def setup_inputs(seed: int=0):
    np.random.seed(seed)
    _w = jnp.asarray

    def _rec_inputs():
        import jax
        import jax.numpy as jnp
        _rk = jax.random.key(seed)
        x = -0.00493535 + 1.00056 * jax.random.normal(jax.random.fold_in(_rk, 1), (16, 128, 64, 2), jnp.float32)
        cls_tok = 0.02 * jax.random.normal(jax.random.fold_in(_rk, 5), (1, 1, 512), jnp.float32)
        return (x, cls_tok)
    x, cls_tok = _rec_inputs()

    def _L0_tok_setup():
        import jax, jax.numpy as jnp
        import numpy as np
        H, N, C = (128, 64, 1)
        DT_MIN, DT_MAX = (0.001, 0.1)
        EPS = 1e-07

        def _hippo_skew_evals(n):
            i = np.arange(n, dtype=np.float64)
            x = 2 * i + 1
            Hm = np.sqrt(np.outer(x, x))
            Hm = np.tril(Hm, k=-1)
            Skew = (Hm - Hm.T) / 2
            ev = np.linalg.eigvals(Skew)
            return ev[np.argsort(-ev.imag)]
        key = jax.random.key(seed)
        k1, k2 = jax.random.split(key)
        w = _hippo_skew_evals(2 * N)[:N] - 0.5
        Lambda = jnp.stack([jnp.asarray(w.real, jnp.float32), jnp.asarray(w.imag, jnp.float32)], axis=-1)
        log_dt = np.log(DT_MIN) + jax.random.uniform(k1, (H,)) * (np.log(DT_MAX) - np.log(DT_MIN))
        log_dt = jnp.tile(log_dt[:, None], (1, 2)).astype(jnp.float32)
        W = jax.random.normal(k2, (C, H, N, 2), dtype=jnp.float32)
        return {'log_dt': log_dt, 'Lambda': Lambda, 'W': W, 'L': 512}
    _L0_tok_all = _L0_tok_setup()
    _L0_tok_in = {k: v for k, v in _L0_tok_all.items() if k in ('log_dt', 'Lambda')}
    del _L0_tok_all

    def _L0_attn_setup():
        import jax, jax.numpy as jnp
        import numpy as np
        B, L, D, DI = (4, 1024, 512, 64)
        LN_EPS = 1e-05

        def _scan_dir(z, Wp):
            d = z.shape[-1]
            o = jnp.einsum('bld,de->ble', z, Wp)
            delta = jax.nn.sigmoid(o[..., :d])
            gate = o[..., d:] * z

            def step(h, dg):
                dlt, g = dg
                h = h * dlt + g
                return (h, h)
            h0 = jnp.zeros_like(z[:, 0])
            _, hs = jax.lax.scan(step, h0, (jnp.swapaxes(delta, 0, 1), jnp.swapaxes(gate, 0, 1)))
            return jnp.swapaxes(hs, 0, 1)
        key = jax.random.key(seed)
        ks = jax.random.split(key, 5)
        x = jax.random.normal(ks[0], (B, L, D), jnp.float32)
        W_in = jax.random.normal(ks[1], (D, DI), jnp.float32) * np.float32(1.0 / np.sqrt(D))
        W_fwd = jax.random.normal(ks[2], (DI, 2 * DI), jnp.float32) * np.float32(0.01)
        W_bwd = jax.random.normal(ks[3], (DI, 2 * DI), jnp.float32) * np.float32(0.01)
        W_out = jax.random.normal(ks[4], (2 * DI, D), jnp.float32) * np.float32(1.0 / np.sqrt(2 * DI))
        gamma = jnp.ones((D,), jnp.float32)
        beta = jnp.zeros((D,), jnp.float32)
        return {'x': x, 'W_in': W_in, 'W_fwd': W_fwd, 'W_bwd': W_bwd, 'W_out': W_out, 'gamma': gamma, 'beta': beta}
    _L0_attn_all = _L0_attn_setup()
    _L0_attn_in = {k: v for k, v in _L0_attn_all.items() if k in ('W_in', 'W_fwd', 'W_bwd', 'W_out', 'gamma', 'beta')}
    del _L0_attn_all

    def _L0_ffn_setup():
        import jax, jax.numpy as jnp
        import numpy as np
        N_EXPERTS = 8
        TOP_K = 2
        C = 512
        H = 256
        HS = 512
        B, T = (1, 128)
        SCALE = 0.02
        key = jax.random.key(seed)
        ks = jax.random.split(key, 10)
        x = jax.random.normal(ks[0], (B, T, C), dtype=jnp.float32)
        gate_w = jax.random.normal(ks[1], (N_EXPERTS, C), dtype=jnp.float32) * SCALE
        w_gate = jax.random.normal(ks[2], (N_EXPERTS, H, C), dtype=jnp.float32) * SCALE
        w_up = jax.random.normal(ks[3], (N_EXPERTS, H, C), dtype=jnp.float32) * SCALE
        w_down = jax.random.normal(ks[4], (N_EXPERTS, C, H), dtype=jnp.float32) * SCALE
        sh_gate = jax.random.normal(ks[5], (HS, C), dtype=jnp.float32) * SCALE
        sh_up = jax.random.normal(ks[6], (HS, C), dtype=jnp.float32) * SCALE
        sh_down = jax.random.normal(ks[7], (C, HS), dtype=jnp.float32) * SCALE
        se_gate_w = jax.random.normal(ks[8], (1, C), dtype=jnp.float32) * SCALE
        return {'x': x, 'gate_w': gate_w, 'w_gate': w_gate, 'w_up': w_up, 'w_down': w_down, 'sh_gate': sh_gate, 'sh_up': sh_up, 'sh_down': sh_down, 'se_gate_w': se_gate_w}
    _L0_ffn_all = _L0_ffn_setup()
    _L0_ffn_in = {k: v for k, v in _L0_ffn_all.items() if k in ('gate_w', 'w_gate', 'w_up', 'w_down', 'sh_gate', 'sh_up', 'sh_down', 'se_gate_w')}
    del _L0_ffn_all

    def _L1_attn_setup():
        import jax, jax.numpy as jnp
        import numpy as np
        B, L, H, NH = (2, 512, 512, 16)
        K = H // NH
        EPS = 1e-05
        SCALE = K ** (-0.5)

        def _gla(q, k, v, g):

            def step(S, xs):
                q_t, k_t, v_t, g_t = xs
                S = jnp.exp(g_t)[:, :, None] * S + k_t[:, :, None] * v_t[:, None, :]
                o_t = jnp.einsum('bk,bkv->bv', q_t, S)
                return (S, o_t)
            S0 = jnp.zeros((q.shape[0], q.shape[2], v.shape[2]), dtype=q.dtype)
            xs = (jnp.swapaxes(q, 0, 1), jnp.swapaxes(k, 0, 1), jnp.swapaxes(v, 0, 1), jnp.swapaxes(g, 0, 1))
            _, o = jax.lax.scan(step, S0, xs)
            return jnp.swapaxes(o, 0, 1)
        key = jax.random.key(seed)
        k0, k1, k2, k3, k4 = jax.random.split(key, 5)
        std = 0.02
        return {'hidden_states': jax.random.normal(k0, (B, L, H), dtype=jnp.float32), 'Wq': jax.random.normal(k1, (K, H), dtype=jnp.float32) * std, 'Wk': jax.random.normal(k2, (K, H), dtype=jnp.float32) * std, 'Wog': jax.random.normal(k3, (H, H), dtype=jnp.float32) * std, 'Wig': jax.random.normal(k4, (H, H), dtype=jnp.float32) * std, 'g_weight': jnp.ones((H,), dtype=jnp.float32)}
    _L1_attn_all = _L1_attn_setup()
    _L1_attn_in = {k: v for k, v in _L1_attn_all.items() if k in ('Wq', 'Wk', 'Wog', 'Wig', 'g_weight')}
    del _L1_attn_all

    def _L1_ffn_setup():
        import jax, jax.numpy as jnp
        import numpy as np
        B, S, H = (2, 256, 512)
        E, K = (8, 2)
        I = 352
        IS = 1408
        WSCALE = 0.02
        key = jax.random.key(seed)
        ks = jax.random.split(key, 9)
        f32 = jnp.float32
        return {'hidden_states': jax.random.normal(ks[0], (B, S, H), dtype=f32), 'gate_w': jax.random.normal(ks[1], (E, H), dtype=f32) * WSCALE, 'w_gate': jax.random.normal(ks[2], (E, H, I), dtype=f32) * WSCALE, 'w_up': jax.random.normal(ks[3], (E, H, I), dtype=f32) * WSCALE, 'w_down': jax.random.normal(ks[4], (E, I, H), dtype=f32) * WSCALE, 'sw_gate': jax.random.normal(ks[5], (H, IS), dtype=f32) * WSCALE, 'sw_up': jax.random.normal(ks[6], (H, IS), dtype=f32) * WSCALE, 'sw_down': jax.random.normal(ks[7], (IS, H), dtype=f32) * WSCALE, 'shared_gate_w': jax.random.normal(ks[8], (H, 1), dtype=f32) * WSCALE}
    _L1_ffn_all = _L1_ffn_setup()
    _L1_ffn_in = {k: v for k, v in _L1_ffn_all.items() if k in ('gate_w', 'w_gate', 'w_up', 'w_down', 'sw_gate', 'sw_up', 'sw_down', 'shared_gate_w')}
    del _L1_ffn_all
    return {'x': x, 'cls_tok': cls_tok, 'L0_tok_log_dt': _L0_tok_in['log_dt'], 'L0_tok_Lambda': _L0_tok_in['Lambda'], 'L0_attn_W_in': _L0_attn_in['W_in'], 'L0_attn_W_fwd': _L0_attn_in['W_fwd'], 'L0_attn_W_bwd': _L0_attn_in['W_bwd'], 'L0_attn_W_out': _L0_attn_in['W_out'], 'L0_attn_gamma': _L0_attn_in['gamma'], 'L0_attn_beta': _L0_attn_in['beta'], 'L0_ffn_gate_w': _L0_ffn_in['gate_w'], 'L0_ffn_w_gate': _L0_ffn_in['w_gate'], 'L0_ffn_w_up': _L0_ffn_in['w_up'], 'L0_ffn_w_down': _L0_ffn_in['w_down'], 'L0_ffn_sh_gate': _L0_ffn_in['sh_gate'], 'L0_ffn_sh_up': _L0_ffn_in['sh_up'], 'L0_ffn_sh_down': _L0_ffn_in['sh_down'], 'L0_ffn_se_gate_w': _L0_ffn_in['se_gate_w'], 'L1_attn_Wq': _L1_attn_in['Wq'], 'L1_attn_Wk': _L1_attn_in['Wk'], 'L1_attn_Wog': _L1_attn_in['Wog'], 'L1_attn_Wig': _L1_attn_in['Wig'], 'L1_attn_g_weight': _L1_attn_in['g_weight'], 'L1_ffn_gate_w': _L1_ffn_in['gate_w'], 'L1_ffn_w_gate': _L1_ffn_in['w_gate'], 'L1_ffn_w_up': _L1_ffn_in['w_up'], 'L1_ffn_w_down': _L1_ffn_in['w_down'], 'L1_ffn_sw_gate': _L1_ffn_in['sw_gate'], 'L1_ffn_sw_up': _L1_ffn_in['sw_up'], 'L1_ffn_sw_down': _L1_ffn_in['sw_down'], 'L1_ffn_shared_gate_w': _L1_ffn_in['shared_gate_w']}

def reference(x, cls_tok, L0_tok_log_dt, L0_tok_Lambda, L0_attn_W_in, L0_attn_W_fwd, L0_attn_W_bwd, L0_attn_W_out, L0_attn_gamma, L0_attn_beta, L0_ffn_gate_w, L0_ffn_w_gate, L0_ffn_w_up, L0_ffn_w_down, L0_ffn_sh_gate, L0_ffn_sh_up, L0_ffn_sh_down, L0_ffn_se_gate_w, L1_attn_Wq, L1_attn_Wk, L1_attn_Wog, L1_attn_Wig, L1_attn_g_weight, L1_ffn_gate_w, L1_ffn_w_gate, L1_ffn_w_up, L1_ffn_w_down, L1_ffn_sw_gate, L1_ffn_sw_up, L1_ffn_sw_down, L1_ffn_shared_gate_w):
    import jax
    import jax.numpy as jnp

    def _L0_tok_ref(log_dt, Lambda, W, L):
        import jax, jax.numpy as jnp
        import numpy as np
        H, N, C = (128, 64, 1)
        DT_MIN, DT_MAX = (0.001, 0.1)
        EPS = 1e-07

        def _hippo_skew_evals(n):
            i = np.arange(n, dtype=np.float64)
            x = 2 * i + 1
            Hm = np.sqrt(np.outer(x, x))
            Hm = np.tril(Hm, k=-1)
            Skew = (Hm - Hm.T) / 2
            ev = np.linalg.eigvals(Skew)
            return ev[np.argsort(-ev.imag)]
        Lam = Lambda[:, 0] + 1j * Lambda[:, 1]
        dt = jnp.exp(log_dt)
        dtL = dt[:, None, :] * Lambda[None, :, :]
        dt_Lambda = dtL[..., 0] + 1j * dtL[..., 1]
        Wc = W[..., 0] + 1j * W[..., 1]
        t = jnp.arange(L, dtype=jnp.float32)
        P = dt_Lambda[..., None] * t
        pos = (Lam.real > 0).astype(jnp.float32)
        P_max = jax.lax.stop_gradient(dt_Lambda * (pos * (L - 1)))
        P = P - P_max[..., None]
        S = jnp.exp(P)
        dt_Lambda_neg = dt_Lambda * (1.0 - 2.0 * pos)
        num = jnp.exp(dt_Lambda_neg) - 1.0
        den = jnp.exp(dt_Lambda_neg * L) - 1.0
        x = den * Lam
        recip = jnp.conj(x) / (x * jnp.conj(x) + EPS)
        Wc = Wc * num * recip
        K = jnp.einsum('chn,hnl->chl', Wc, S).real.astype(jnp.float32)
        return K

    def _L0_attn_ref(x, W_in, W_fwd, W_bwd, W_out, gamma, beta):
        import jax, jax.numpy as jnp
        import numpy as np
        B, L, D, DI = (4, 1024, 512, 64)
        LN_EPS = 1e-05

        def _scan_dir(z, Wp):
            d = z.shape[-1]
            o = jnp.einsum('bld,de->ble', z, Wp)
            delta = jax.nn.sigmoid(o[..., :d])
            gate = o[..., d:] * z

            def step(h, dg):
                dlt, g = dg
                h = h * dlt + g
                return (h, h)
            h0 = jnp.zeros_like(z[:, 0])
            _, hs = jax.lax.scan(step, h0, (jnp.swapaxes(delta, 0, 1), jnp.swapaxes(gate, 0, 1)))
            return jnp.swapaxes(hs, 0, 1)
        z = jnp.einsum('bld,de->ble', x, W_in)
        h_fwd = _scan_dir(z, W_fwd)
        h_bwd = _scan_dir(z[:, ::-1], W_bwd)[:, ::-1]
        out = jnp.einsum('ble,ed->bld', jnp.concatenate([h_fwd, h_bwd], axis=-1), W_out)
        y = out + x
        mu = jnp.mean(y, axis=-1, keepdims=True)
        var = jnp.var(y, axis=-1, keepdims=True)
        return (y - mu) * jax.lax.rsqrt(var + LN_EPS) * gamma + beta

    def _L0_ffn_ref(x, gate_w, w_gate, w_up, w_down, sh_gate, sh_up, sh_down, se_gate_w):
        import jax, jax.numpy as jnp
        import numpy as np
        N_EXPERTS = 8
        TOP_K = 2
        C = 512
        H = 256
        HS = 512
        B, T = (1, 128)
        SCALE = 0.02
        Bb, Tt, Cc = x.shape
        xf = x.reshape(-1, Cc)
        scores = xf @ gate_w.T
        ew, ei = jax.lax.top_k(scores, TOP_K)
        ew = jax.nn.softmax(ew, axis=-1)
        x1 = jax.nn.silu(jnp.einsum('td,ehd->teh', xf, w_gate))
        x3 = jnp.einsum('td,ehd->teh', xf, w_up)
        expert_out = jnp.einsum('teh,edh->ted', x1 * x3, w_down)
        onehot = jax.nn.one_hot(ei, N_EXPERTS, dtype=ew.dtype)
        comb = jnp.einsum('ta,tae->te', ew, onehot)
        routed = jnp.einsum('te,ted->td', comb, expert_out)
        shared = jax.nn.silu(xf @ sh_gate.T) * (xf @ sh_up.T) @ sh_down.T
        sgate = jax.nn.sigmoid(xf @ se_gate_w.T)
        return (routed + sgate * shared).reshape(Bb, Tt, Cc)

    def _L1_attn_ref(hidden_states, Wq, Wk, Wog, Wig, g_weight):
        import jax, jax.numpy as jnp
        import numpy as np
        B, L, H, NH = (2, 512, 512, 16)
        K = H // NH
        EPS = 1e-05
        SCALE = K ** (-0.5)

        def _gla(q, k, v, g):

            def step(S, xs):
                q_t, k_t, v_t, g_t = xs
                S = jnp.exp(g_t)[:, :, None] * S + k_t[:, :, None] * v_t[:, None, :]
                o_t = jnp.einsum('bk,bkv->bv', q_t, S)
                return (S, o_t)
            S0 = jnp.zeros((q.shape[0], q.shape[2], v.shape[2]), dtype=q.dtype)
            xs = (jnp.swapaxes(q, 0, 1), jnp.swapaxes(k, 0, 1), jnp.swapaxes(v, 0, 1), jnp.swapaxes(g, 0, 1))
            _, o = jax.lax.scan(step, S0, xs)
            return jnp.swapaxes(o, 0, 1)
        x = hidden_states
        q = x @ Wq.T
        k_sig = jax.nn.sigmoid(x @ Wk.T)
        q = jax.nn.silu(q) * SCALE
        gf = jax.nn.log_sigmoid(-k_sig)
        o = _gla(q, k_sig, x, gf)
        go = o @ Wog.T + x @ Wig.T
        rms = o * jax.lax.rsqrt(jnp.mean(o * o, axis=-1, keepdims=True) + EPS) * g_weight
        return rms * go * jax.nn.sigmoid(go)

    def _L1_ffn_ref(hidden_states, gate_w, w_gate, w_up, w_down, sw_gate, sw_up, sw_down, shared_gate_w):
        import jax, jax.numpy as jnp
        import numpy as np
        B, S, H = (2, 256, 512)
        E, K = (8, 2)
        I = 352
        IS = 1408
        WSCALE = 0.02
        x = hidden_states
        logits = jnp.einsum('bsh,eh->bse', x, gate_w)
        probs = jax.nn.softmax(logits, axis=-1)
        top_w, top_i = jax.lax.top_k(probs, K)
        top_w = top_w / jnp.sum(top_w, axis=-1, keepdims=True)
        onehot = jax.nn.one_hot(top_i, E, dtype=x.dtype)
        combine = jnp.einsum('bsk,bske->bse', top_w, onehot)
        g = jnp.einsum('bsh,ehi->besi', x, w_gate)
        u = jnp.einsum('bsh,ehi->besi', x, w_up)
        h = jax.nn.silu(g) * u
        expert_out = jnp.einsum('besi,eih->besh', h, w_down)
        moe_out = jnp.einsum('besh,bse->bsh', expert_out, combine)
        sh = jax.nn.silu(x @ sw_gate) * (x @ sw_up)
        shared_out = sh @ sw_down
        shared_gate = jax.nn.sigmoid(x @ shared_gate_w)
        return moe_out + shared_out * shared_gate
    h = _L0_tok_ref(L0_tok_log_dt, L0_tok_Lambda, x, 512)
    h = jnp.concatenate([jnp.broadcast_to(cls_tok, (h.shape[0], 1, h.shape[2])), h], axis=1)
    h = h + _L0_attn_ref(_layernorm(h, axis=-1), L0_attn_W_in, L0_attn_W_fwd, L0_attn_W_bwd, L0_attn_W_out, L0_attn_gamma, L0_attn_beta)
    h = h + _L0_ffn_ref(_layernorm(h, axis=-1), L0_ffn_gate_w, L0_ffn_w_gate, L0_ffn_w_up, L0_ffn_w_down, L0_ffn_sh_gate, L0_ffn_sh_up, L0_ffn_sh_down, L0_ffn_se_gate_w)
    h = h + _L1_attn_ref(_layernorm(h, axis=-1), L1_attn_Wq, L1_attn_Wk, L1_attn_Wog, L1_attn_Wig, L1_attn_g_weight)
    h = h + _L1_ffn_ref(_layernorm(h, axis=-1), L1_ffn_gate_w, L1_ffn_w_gate, L1_ffn_w_up, L1_ffn_w_down, L1_ffn_sw_gate, L1_ffn_sw_up, L1_ffn_sw_down, L1_ffn_shared_gate_w)
    return h

_drawn_inputs = setup_inputs


def setup_inputs(seed=0):
    import zlib

    import numpy as np

    out = dict(_drawn_inputs(seed))
    spreads = {'L0_attn_gamma': (1.0, 0.2), 'L0_attn_beta': (0.0, 0.1), 'L1_attn_g_weight': (1.0, 0.2)}
    factors = {'L0_ffn_se_gate_w': 23.153, 'L1_ffn_shared_gate_w': 7.702}
    for name, (base, spread) in spreads.items():
        noise = np.random.default_rng([zlib.crc32(name.encode()), seed]).standard_normal(out[name].shape)
        drawn = base * np.exp(spread * noise) if base else spread * noise
        out[name] = jnp.asarray(drawn.astype(out[name].dtype))
    for name, factor in factors.items():
        out[name] = (out[name] * factor).astype(out[name].dtype)
    return out
```

```python
from contextlib import ExitStack

import concourse.bass as bass
import numpy as np
from concourse import mybir

F32 = mybir.dt.float32
I32 = mybir.dt.int32
U32 = mybir.dt.uint32
ALU = mybir.AluOpType
ACT = mybir.ActivationFunctionType
AX = mybir.AxisListType

P = 128
NB = 16
NH = 128
NS = 64
L = 512
D = 512
KD = D // P
T = NB + 1
NCOL = NB * NH
NTOK = NB * (NH + 1)
SEQ = NH + 1
NQ = 4
QC = 512
LN_EPS = 1e-5
SILU_SCALE = 32 ** -0.5

TB = 8
TI, TJ = 8, 64
HC = 16
NHC = NH // HC
NK = 3 * TB
MAGIC = 1.5 * 2.0 ** 23
TWO_PI = 2 * np.pi


class Chain:

    def __init__(self, eng, sem, base=0):
        self.eng, self.sem, self.base, self.n = eng, sem, base, 0

    def put(self, ins):
        self.n += 1
        ins.then_inc(self.sem, 1)

    def wait(self):
        self.eng.wait_ge(self.sem, self.base + self.n)

    def link(self, ins):
        self.put(ins)
        self.wait()


def looped(eng, n, body):
    body(0)
    if n > 1:
        with eng.Fori(1, n) as i:
            body(i)


def is_first(i):
    return isinstance(i, int) and i == 0


def bc(ap, dim, n):
    shape = list(ap.shape)
    shape[dim] = n
    return ap.to_broadcast(shape)


class Arena:

    def __init__(self, tensor, at=0):
        self.tensor, self.at = tensor, at

    def take(self, *shape, rows=P, dt=F32):
        size = int(np.prod(shape))
        flat = self.tensor[0:rows, self.at:self.at + size]
        self.at += size + size % 2
        assert self.at <= self.tensor.shape[1], self.at
        if dt != F32:
            flat = flat.bitcast(dt)
        if len(shape) == 1:
            return flat
        names = [f"d{k}" for k in range(len(shape))]
        return flat.rearrange(f"p ({' '.join(names)}) -> p {' '.join(names)}",
                              **{n: s for n, s in zip(names[1:], shape[1:])})


def tokenizer(nc, sem, sb, ps, d, h0, arena_at):
    a = Arena(sb, arena_at)
    lam = a.take(2)
    ld = a.take(2, NH)
    kc = a.take(2, NK + 4)
    wre, wim = a.take(NH, NB), a.take(NH, NB)
    pos, sig, sgn = a.take(1), a.take(1), a.take(1)
    kt, kt2 = a.take(NK), a.take(4)
    ex, en, er, ep, es = (a.take(4, NH) for _ in range(5))
    eni = a.take(4 * NH, dt=I32)
    dt = a.take(2, NH)
    dre, dim = a.take(NH), a.take(NH)
    em = a.take(2, NH)
    fa, fb, p1, q, t0, fhi, flo = (a.take(NH) for _ in range(7))
    sm = [a.take(NH, 4) for _ in range(6)]
    nr, ni, dr, di, xr, xi, s0, s1, inv = (a.take(NH) for _ in range(9))
    cr, ci, c1, c2 = (a.take(NH) for _ in range(4))
    m, kl, ke, mk, re, im = (a.take(NH, NK) for _ in range(6))
    a1, a2 = a.take(2, HC, TI), a.take(2, HC, TI)
    d1, d2 = a.take(2, HC, TB), a.take(2, HC, TB)
    ta, tb = a.take(HC, TB), a.take(HC, TB)
    u1, u2 = a.take(2, HC, TI * NB), a.take(2, HC, TI * NB)
    bb, bt = a.take(2, HC, TJ), a.take(HC, TJ)
    ob = a.take(2, HC * TJ)
    LO, HI = slice(0, NS), slice(NS, P)
    INV = 1.0 / TWO_PI

    def top12(x):
        return float((np.array([x], np.float32).view(np.uint32) & np.uint32(0xFFFFF000)).view(np.float32)[0])

    V1 = top12(INV)
    V2 = top12(INV - V1)
    V3 = float(np.float32(INV - V1 - V2))
    LN2H = 355.0 / 512.0
    LN2L = float(np.log(2.0) - LN2H)

    par_in, w_in = sem("tok_params_loaded"), sem("tok_weights_loaded")
    dch, pch = sem("tok_dve_chain"), sem("tok_pool_chain")
    phase = sem("tok_phase_split")
    lin = sem("tok_linear_ready")
    sm_in, sm_out = sem("tok_small_args"), sem("tok_small_sines")
    arg, sines = sem("tok_sine_args"), sem("tok_sines")
    expd = sem("tok_decays")
    scaled = sem("tok_tables_scaled")
    ab, uw, u2r = sem("tok_factors"), sem("tok_u1_and_b"), sem("tok_u2")
    prod, evac, stored = sem("tok_products"), sem("tok_evacuated"), [sem(f"tok_stored{k}") for k in range(2)]
    H2 = NH // 2
    hs = [slice(0, H2), slice(H2, NH)]
    cch = sem("tok_step_chain")

    def sync(sp):
        for half in (LO, HI):
            sp.dma_start(lam[half, :], d["lam"]).then_inc(par_in, 16)
        for k in range(2):
            sp.dma_start(ld[:, k, :], d["log_dt"][k].partition_broadcast(P)).then_inc(par_in, 16)
            sp.dma_start(kc[:, k, :], d["kconst"][k].partition_broadcast(P)).then_inc(par_in, 16)
        for w, k in ((wre, 0), (wim, 1)):
            for half in (LO, HI):
                sp.dma_start(w[half, :, :].rearrange("p h c -> p (h c)"), d["x"][k]).then_inc(w_in, 16)
        h0v = h0.rearrange("c (g h) (i j) -> i c g h j", j=TJ, h=HC)

        def store(k, u):
            sp.wait_ge(evac, 2 * k + 2)
            for i in range(TI):
                sp.dma_start(h0v[i, :, k, :, :],
                             ob[i * NB:(i + 1) * NB, u, :].rearrange("c (h j) -> c h j", j=TJ)).then_inc(stored[u], 16)

        def pair(i):
            for u in range(2):
                store(2 * i + u, u)

        looped(sp, NHC // 2, pair)
    def all_stored(sp):
        for u in range(2):
            sp.wait_ge(stored[u], 16 * TI * NHC // 2)

    def vector(v):
        c = Chain(v, dch)
        v.wait_ge(par_in, 6 * 16)

        def exp_parts(x, w):
            X, N, R, PM, S = (t[:, 0:w, :] for t in (x, en, er, ep, es))
            NI = eni[:, 0:w * NH].rearrange("p (a b) -> p a b", b=NH)
            c.link(v.tensor_scalar(X, X, -87.0, 88.0, ALU.max, ALU.min))
            c.link(v.tensor_scalar(N, X, float(1 / np.log(2.0)), MAGIC, ALU.mult, ALU.add))
            c.link(v.tensor_scalar(N, N, -MAGIC, None, ALU.add))
            c.link(v.scalar_tensor_tensor(out=R, in0=N, scalar=-LN2H, in1=X, op0=ALU.mult, op1=ALU.add))
            c.link(v.scalar_tensor_tensor(out=R, in0=N, scalar=-LN2L, in1=R, op0=ALU.mult, op1=ALU.add))
            c.link(v.tensor_scalar(PM, R, 1.0 / 40320, None, ALU.mult))
            for f in (5040, 720, 120, 24, 6, 2, 1):
                c.link(v.scalar_tensor_tensor(out=PM, in0=PM, scalar=1.0 / f, in1=R, op0=ALU.add, op1=ALU.mult))
            c.link(v.tensor_scalar(NI, N, 127.0, None, ALU.add))
            c.link(v.tensor_scalar(S.bitcast(I32), NI, 23, None, ALU.logical_shift_left))

        c.link(v.tensor_copy(ex[:, 0:2, :], ld[:, :, :]))
        exp_parts(ex, 2)
        c.link(v.scalar_tensor_tensor(out=dt, in0=ep[:, 0:2, :], scalar=1.0, in1=es[:, 0:2, :], op0=ALU.add, op1=ALU.mult))
        c.link(v.tensor_scalar(dre, dt[:, 0, :], lam[:, 0:1], None, ALU.mult))
        c.link(v.tensor_scalar(dim, dt[:, 1, :], lam[:, 1:2], None, ALU.mult))
        c.link(v.tensor_scalar(pos, lam[:, 0:1], 0.0, None, ALU.is_gt))
        c.link(v.tensor_scalar(sig, pos, -2.0, 1.0, ALU.mult, ALU.add))
        c.link(v.memset(sgn[LO, :], 1.0))
        c.link(v.memset(sgn[HI, :], -1.0))
        c.link(v.scalar_tensor_tensor(out=kt, in0=kc[:, 1, 0:NK], scalar=pos[:, 0:1], in1=kc[:, 0, 0:NK], op0=ALU.mult, op1=ALU.add))
        c.link(v.tensor_copy(kt2, kc[:, 0, NK:NK + 4]))
        c.link(v.tensor_scalar(fa.bitcast(U32), dim.bitcast(U32), 0xFFFFF000, None, ALU.bitwise_and))
        c.link(v.tensor_tensor(fb, dim, fa, ALU.subtract))
        c.link(v.tensor_scalar(p1, fa, V1, None, ALU.mult))
        c.link(v.tensor_scalar(t0, p1, MAGIC, None, ALU.add))
        c.link(v.scalar_tensor_tensor(out=t0, in0=t0, scalar=-MAGIC, in1=p1, op0=ALU.add, op1=ALU.subtract))
        c.link(v.tensor_scalar(p1, t0, -1.0, None, ALU.mult))
        c.link(v.tensor_scalar(q, fb, V2, None, ALU.mult))
        c.link(v.scalar_tensor_tensor(out=q, in0=fa, scalar=V3, in1=q, op0=ALU.mult, op1=ALU.add))
        c.link(v.tensor_scalar(t0, fb, V1, None, ALU.mult))
        c.link(v.scalar_tensor_tensor(out=t0, in0=fa, scalar=V2, in1=t0, op0=ALU.mult, op1=ALU.add))
        c.link(v.tensor_tensor(q, q, t0, ALU.add))
        c.link(v.tensor_tensor(t0, p1, q, ALU.add))
        c.link(v.tensor_scalar(t0, t0, MAGIC / 32768, None, ALU.add))
        c.link(v.tensor_scalar(fhi, t0, -MAGIC / 32768, None, ALU.add))
        c.link(v.tensor_tensor(flo, p1, fhi, ALU.subtract))
        v.tensor_tensor(flo, flo, q, ALU.add).then_inc(phase, 1)
        v.wait_ge(phase, 1)
        c.link(v.tensor_scalar(t0, fhi, MAGIC, None, ALU.add))
        c.link(v.tensor_scalar(t0, t0, -MAGIC, None, ALU.add))
        c.link(v.tensor_tensor(fhi, fhi, t0, ALU.subtract))

        def args(out, mm, mmk, kk, ph):
            c.link(v.tensor_scalar(out, mmk, ph, MAGIC, ALU.add, ALU.add))
            c.link(v.scalar_tensor_tensor(out=out, in0=out, scalar=-MAGIC, in1=mm, op0=ALU.add, op1=ALU.subtract))
            c.link(v.scalar_tensor_tensor(out=out, in0=out, scalar=-ph, in1=kk, op0=ALU.add, op1=ALU.subtract))
            return v.tensor_scalar(out, out, -0.5, 0.5, ALU.max, ALU.min)

        def spread(x, w):
            return bc(x.unsqueeze(2), 2, w)

        k4 = bc(kt2.unsqueeze(1), 1, NH)
        ms, ks, mks, co, si, _ = sm
        c.link(v.tensor_tensor(ms, k4, spread(fhi, 4), ALU.mult))
        c.link(v.tensor_tensor(ks, k4, spread(flo, 4), ALU.mult))
        c.link(v.tensor_tensor(mks, ms, ks, ALU.add))
        args(si, ms, mks, ks, 0.0).then_inc(sm_in, 1)
        args(co, ms, mks, ks, 0.25).then_inc(sm_in, 1)
        k24 = bc(kt.unsqueeze(1), 1, H2)
        for n, h in enumerate(hs):
            c.link(v.tensor_tensor(m[:, h, :], k24, spread(fhi[:, h], NK), ALU.mult))
            v.wait_ge(lin, 2 * n + 2)
            c.link(v.tensor_tensor(mk[:, h, :], m[:, h, :], kl[:, h, :], ALU.add))
            args(re[:, h, :], m[:, h, :], mk[:, h, :], kl[:, h, :], 0.25).then_inc(arg, 1)
            args(im[:, h, :], m[:, h, :], mk[:, h, :], kl[:, h, :], 0.0).then_inc(arg, 1)
        c.link(v.tensor_scalar(ex[:, 0, :], dre, sig[:, 0:1], None, ALU.mult))
        c.link(v.tensor_scalar(ex[:, 1, :], ex[:, 0, :], float(L), None, ALU.mult))
        exp_parts(ex, 2)
        c.link(v.tensor_tensor(em, ep[:, 0:2, :], es[:, 0:2, :], ALU.mult))
        c.link(v.scalar_tensor_tensor(out=em, in0=es[:, 0:2, :], scalar=-1.0, in1=em, op0=ALU.add, op1=ALU.add))
        v.wait_ge(sm_out, 2)
        for out_r, out_i, e, kk in ((nr, ni, em[:, 0, :], 1), (dr, di, em[:, 1, :], 3)):
            c.link(v.tensor_tensor(s0, si[:, :, kk - 1], si[:, :, kk - 1], ALU.mult))
            c.link(v.tensor_tensor(out_r, e, co[:, :, kk], ALU.mult))
            c.link(v.scalar_tensor_tensor(out=out_r, in0=s0, scalar=-2.0, in1=out_r, op0=ALU.mult, op1=ALU.add))
            c.link(v.scalar_tensor_tensor(out=out_i, in0=e, scalar=1.0, in1=si[:, :, kk], op0=ALU.add, op1=ALU.mult))
            c.link(v.tensor_scalar(out_i, out_i, sig[:, 0:1], None, ALU.mult))
        c.link(v.tensor_scalar(s0, di, lam[:, 1:2], None, ALU.mult))
        c.link(v.scalar_tensor_tensor(out=xr, in0=dr, scalar=lam[:, 0:1], in1=s0, op0=ALU.mult, op1=ALU.subtract))
        c.link(v.tensor_scalar(s0, di, lam[:, 0:1], None, ALU.mult))
        c.link(v.scalar_tensor_tensor(out=xi, in0=dr, scalar=lam[:, 1:2], in1=s0, op0=ALU.mult, op1=ALU.add))
        c.link(v.tensor_tensor(s0, xr, xr, ALU.mult))
        c.link(v.tensor_tensor(s1, xi, xi, ALU.mult))
        c.link(v.scalar_tensor_tensor(out=s0, in0=s0, scalar=1e-7, in1=s1, op0=ALU.add, op1=ALU.add))
        c.link(v.reciprocal(inv, s0))
        for out, g, h, w, x, op in ((cr, nr, xr, ni, xi, ALU.add), (ci, ni, xr, nr, xi, ALU.subtract)):
            c.link(v.tensor_tensor(s0, g, h, ALU.mult))
            c.link(v.tensor_tensor(s1, w, x, ALU.mult))
            c.link(v.tensor_tensor(s0, s0, s1, op))
            c.link(v.tensor_tensor(out, s0, inv, ALU.mult))
        c.link(v.tensor_copy(c1[LO, :], cr[LO, :]))
        c.link(v.tensor_copy(c1[HI, :], ci[HI, :]))
        c.link(v.tensor_scalar(c2[LO, :], ci[LO, :], -1.0, None, ALU.mult))
        c.link(v.tensor_copy(c2[HI, :], cr[HI, :]))
        v.wait_ge(w_in, 64)
        v.wait_ge(scaled, 4)

        PER = 22

        def pair(i):
            s = Chain(v, cch, i * PER)
            for u in range(2):
                k = 2 * i + u
                hh = bass.ds(k * HC, HC)
                AR, AI = re[:, hh, 2 * TB:3 * TB], im[:, hh, 2 * TB:3 * TB]
                R1, I1 = re[:, hh, 0:TB], im[:, hh, 0:TB]
                R2, I2 = re[:, hh, TB:2 * TB], im[:, hh, TB:2 * TB]
                C1, C2 = spread(c1[:, hh], TI), spread(c2[:, hh], TI)
                if not is_first(i):
                    v.wait_ge(prod, 2 * (k - 1))
                s.put(v.tensor_tensor(a1[:, u], C1, AR, ALU.mult))
                s.put(v.tensor_tensor(ta, C2, AI, ALU.mult))
                s.put(v.tensor_tensor(a2[:, u], C2, AR, ALU.mult))
                s.link(v.tensor_tensor(tb, C1, AI, ALU.mult))
                s.put(v.tensor_tensor(a1[:, u], a1[:, u], ta, ALU.add))
                v.tensor_tensor(a2[:, u], a2[:, u], tb, ALU.subtract).then_inc(ab, 1)
                s.put(v.tensor_copy(d1[LO, u], R2[LO]))
                s.put(v.tensor_scalar(d1[HI, u], I2[HI], -1.0, None, ALU.mult))
                s.put(v.tensor_scalar(d2[LO, u], I2[LO], -1.0, None, ALU.mult))
                s.link(v.tensor_scalar(d2[HI, u], R2[HI], -1.0, None, ALU.mult))
                B4 = bb[:, u].rearrange("p h (b c) -> p h b c", c=TB)
                T4 = bt.rearrange("p h (b c) -> p h b c", c=TB)

                def outer(small, big):
                    return bc(small.unsqueeze(2), 2, TB), bc(big.unsqueeze(3), 3, TB)

                x, y = outer(R1, d1[:, u])
                s.put(v.tensor_tensor(B4, x, y, ALU.mult))
                x, y = outer(I1, d2[:, u])
                s.link(v.tensor_tensor(T4, x, y, ALU.mult))
                v.tensor_tensor(bb[:, u], bb[:, u], bt, ALU.add).then_inc(uw, 1)
                U4 = u1[:, u].rearrange("p h (i c) -> p h i c", c=NB)
                v.tensor_tensor(U4, bc(wre[:, hh, :].unsqueeze(2), 2, TI), bc(a1[:, u].unsqueeze(3), 3, NB), ALU.mult).then_inc(uw, 1)
            assert s.n == PER

        looped(v, NHC // 2, pair)

    def gpsimd(g):
        g.wait_ge(phase, 1)
        for n, h in enumerate(hs):
            k24 = bc(kt.unsqueeze(1), 1, H2)
            g.tensor_tensor(kl[:, h, :], k24, bc(flo[:, h].unsqueeze(2), 2, NK), ALU.mult).then_inc(lin, 1)
            g.tensor_tensor(ke[:, h, :], k24, bc(dre[:, h].unsqueeze(2), 2, NK), ALU.mult).then_inc(lin, 1)
        for n, h in enumerate(hs):
            g.wait_ge(expd, n + 1)
            for j, t in enumerate((re, im)):
                g.wait_ge(sines, 2 * n + j + 1)
                g.tensor_tensor(t[:, h, :], t[:, h, :], ke[:, h, :], ALU.mult).then_inc(scaled, 1)
        g.wait_ge(w_in, 64)

        def pair(i):
            for u in range(2):
                k = 2 * i + u
                hh = bass.ds(k * HC, HC)
                g.wait_ge(ab, k + 1)
                if not is_first(i):
                    g.wait_ge(prod, 2 * (k - 1))
                U4 = u2[:, u].rearrange("p h (i c) -> p h i c", c=NB)
                g.tensor_tensor(U4, bc(wim[:, hh, :].unsqueeze(2), 2, TI), bc(a2[:, u].unsqueeze(3), 3, NB), ALU.mult).then_inc(u2r, 1)

        looped(g, NHC // 2, pair)

    def scalar(s):
        for n, h in enumerate(hs):
            s.wait_ge(lin, 2 * n + 2)
            s.activation(ke[:, h, :], ke[:, h, :], ACT.Exp).then_inc(expd, 1)
        for j in (3, 4):
            t = sm[4] if j == 3 else sm[3]
            s.wait_ge(sm_in, j - 2)
            s.activation(t, t, ACT.Sin, scale=-TWO_PI).then_inc(sm_out, 1)
        for n, h in enumerate(hs):
            for j, t in enumerate((re, im)):
                s.wait_ge(arg, 2 * n + j + 1)
                s.activation(t[:, h, :], t[:, h, :], ACT.Sin, scale=-TWO_PI).then_inc(sines, 1)

        def pair(i):
            for u in range(2):
                k = 2 * i + u
                if not is_first(i):
                    s.wait_ge(stored[u], 16 * TI * i)
                for b in range(2):
                    s.wait_ge(prod, 2 * k + b + 1)
                    s.activation(ob[:, u, b * QC:(b + 1) * QC], ps[:, 2 * u + b, :], ACT.Copy).then_inc(evac, 1)

        looped(s, NHC // 2, pair)

    def tensor(t):
        def pair(i):
            for u in range(2):
                k = 2 * i + u
                t.wait_ge(uw, 2 * k + 2)
                t.wait_ge(u2r, k + 1)
                for b in range(2):
                    if not is_first(i):
                        t.wait_ge(evac, 2 * (k - 2) + b + 1)
                    for h in range(8):
                        hh = 8 * b + h
                        o = ps[:, 2 * u + b, h * TJ:(h + 1) * TJ]
                        t.matmul(o, u1[:, u, hh, :], bb[:, u, hh, :], start=True, stop=False)
                        mm = t.matmul(o, u2[:, u, hh, :], bb[:, u, hh, :], start=False, stop=True)
                    mm.then_inc(prod, 1)

        looped(t, NHC // 2, pair)

    return sync, vector, gpsimd, scalar, tensor, all_stored


def tile_rows(t):
    return NB if isinstance(t, int) and t == T - 1 else P


def over_tiles(eng, body):
    def pair(i):
        for u in range(2):
            body(2 * i + u, u)

    looped(eng, NB // 2, pair)
    body(T - 1, 0)


def each_tile(body):
    for t in range(T):
        body(t, t % 2)


def early(t):
    return isinstance(t, int) and t < 2


class Norm:

    def __init__(self, arena, chain_sem):
        self.stats = arena.take(T, 6)
        self.mv = arena.take(T, 2)
        self.rstd = arena.take(T)
        self.half = arena.take(T, 2)
        self.sem = chain_sem
        self.count = 0

    def chain(self, v):
        return Chain(v, self.sem, self.count)

    def closed(self, c):
        self.count += c.n

    def take_stats(self, v, x, t):
        r = tile_rows(t)
        v.bn_stats(self.stats[0:r, t, :], x[0:r, t, :]).then_inc(self.sem, 1)

    def clear(self, v):
        c = self.chain(v)
        c.link(v.memset(self.mv, 1.0))
        self.closed(c)

    def solve(self, v, eps=LN_EPS):
        c = self.chain(v)
        c.n += T
        c.wait()
        for t in range(T):
            r = tile_rows(t)
            c.put(v.bn_aggr(self.mv[0:r, t, :], self.stats[0:r, t, :]))
        c.wait()
        self.newton(v, c, self.mv[:, :, 1], 1.0, eps)
        self.closed(c)

    def newton(self, v, c, var, scale, eps):
        y, a, b = self.rstd, self.half[:, :, 0], self.half[:, :, 1]
        c.link(v.tensor_scalar(b, var, scale, eps, ALU.mult, ALU.add))
        c.link(v.tensor_copy(a, b))
        c.link(v.tensor_scalar(y.bitcast(I32), a.bitcast(I32), 1, None, ALU.arith_shift_right))
        c.link(v.tensor_scalar(y.bitcast(I32), y.bitcast(I32), -1.0, float(0x5F3759DF), ALU.mult, ALU.add))
        for _ in range(4):
            c.link(v.tensor_tensor(a, y, y, ALU.mult))
            c.link(v.scalar_tensor_tensor(out=a, in0=a, scalar=-0.5, in1=b, op0=ALU.mult, op1=ALU.mult))
            c.link(v.scalar_tensor_tensor(out=y, in0=a, scalar=1.5, in1=y, op0=ALU.add, op1=ALU.mult))

    def apply(self, v, out, x, t):
        r = tile_rows(t)
        return v.tensor_scalar(out[0:r, t, :], x[0:r, t, :], self.mv[0:r, t, 0:1], self.rstd[0:r, bass.ds(t, 1)],
                               ALU.subtract, ALU.mult)


def turn_tile(t_eng, ps_bank, xn, t, ident):
    r = tile_rows(t)
    for k in range(KD):
        ins = t_eng.transpose(ps_bank[:, k * r:(k + 1) * r], xn[0:r, t, k * P:(k + 1) * P], ident[0:r, 0:r])
    return ins


def turned_out(s_eng, ps_bank, xnT, t):
    r = tile_rows(t)
    dst = xnT[:, :, NCOL:NTOK] if r == NB else xnT[:, :, bass.ds(t * P, P)]
    return s_eng.activation(dst, ps_bank[:, 0:KD * r].rearrange("p (k n) -> p k n", k=KD), ACT.Copy)


def scan_layer(nc, sem, sb, ps, d, h0, tok_stored, g, at):
    a = Arena(sb, at)
    hb, xn, xnT, yb, ident, norm = g.h, g.xn, g.xnT, g.y, g.ident, g.norm
    win = a.take(KD, P)
    wd, wg = a.take(P), a.take(P)
    wout, gam, bet = a.take(D), a.take(D), a.take(D)
    zb, db, gb, hs = (a.take(NB, SEQ) for _ in range(4))
    tmp = a.take(2, D)
    F = (lambda x: x.rearrange("p b s -> p (b s)"))
    zf, df, gf, hf = F(zb), F(db), F(gb), F(hs)
    NC, CW = 6, NTOK // 6
    HALF = P // 2

    h_in = [sem(f"h_loaded{q}") for q in range(NQ + 1)]
    wz, w_in, w_fb = sem("scan_zeroed"), sem("scan_weights_loaded"), sem("scan_block_weights_loaded")
    xr, turned, tev = sem("scan_xn_ready"), sem("scan_turned"), sem("scan_xnT_ready")
    zp, zr = sem("scan_z_products"), sem("scan_z_ready")
    op, dr, gr = sem("scan_gate_products"), sem("scan_delta_ready"), sem("scan_gate_ready")
    rst, sc = sem("scan_resets"), sem("scan_states")
    outp, yr = sem("scan_out_products"), sem("scan_y_ready")
    hbr, hr, tch = sem("scan_h_plus_beta"), g.h_ready, sem("scan_vector_chain")

    def sync(sp):
        tok_stored(sp)
        for q in range(NQ):
            sp.dma_start(hb[:, 4 * q:4 * q + 4, :], h0[4 * q:4 * q + 4].rearrange("b p d -> p b d")).then_inc(h_in[q], 16)
        sp.dma_start(hb[0:NB, NB, :], d["cls"]).then_inc(h_in[NQ], 16)
        sp.dma_start(ident, d["ident"]).then_inc(w_in, 16)
        for k in range(2):
            sp.dma_start(win[:, :, k * HALF:(k + 1) * HALF], d["W_in"].rearrange("(k p) n -> p k n", p=P)).then_inc(w_in, 16)
        sp.wait_ge(wz, 2)
        for k, w in enumerate((d["W_fwd"], d["W_bwd"])):
            s = slice(k * HALF, (k + 1) * HALF)
            sp.dma_start(wd[s, s], w[:, 0:HALF]).then_inc(w_fb, 16)
            sp.dma_start(wg[s, s], w[:, HALF:P]).then_inc(w_fb, 16)
        sp.dma_start(wout, d["W_out"]).then_inc(w_fb, 16)
        sp.dma_start(gam, d["gamma"].partition_broadcast(P)).then_inc(w_fb, 16)
        sp.dma_start(bet, d["beta"].partition_broadcast(P)).then_inc(w_fb, 16)

    def vector(v):
        v.wait_ge(h_in[0], 16)
        norm.clear(v)
        for q in range(NQ):
            v.wait_ge(h_in[q], 16)
            for t in range(4 * q, 4 * q + 4):
                norm.take_stats(v, hb, t)
        v.wait_ge(h_in[NQ], 16)
        norm.take_stats(v, hb, NB)
        norm.solve(v)
        over_tiles(v, lambda t, u: norm.apply(v, xn, hb, t).then_inc(xr, 1))

        def gates(c):
            v.wait_ge(op, c + 1)
            cols = bass.ds(c * CW, CW)
            b = 6
            v.tensor_tensor(gf[:, cols], ps[:, b, 0:CW], zf[:, cols], ALU.mult).then_inc(gr, 1)

        looped(v, NC, gates)
        v.wait_ge(gr, NC)
        v.wait_ge(rst, 2)
        v.tensor_tensor_scan(hf[0:HALF, :], df[0:HALF, :], gf[0:HALF, :], 0.0, ALU.mult, ALU.add).then_inc(sc, 1)
        v.tensor_tensor_scan(hf[HALF:P, ::-1], df[HALF:P, ::-1], gf[HALF:P, ::-1], 0.0, ALU.mult, ALU.add).then_inc(sc, 1)

        v.wait_ge(xr, T)

        def add(t, u):
            r = tile_rows(t)
            v.wait_ge(outp, t + 1)
            v.tensor_tensor(yb[0:r, t, :], ps[0:r, 2 + u, :], xn[0:r, t, :], ALU.add).then_inc(yr, 1)
            v.wait_ge(yr, t + 1)
            norm.take_stats(v, yb, t)

        over_tiles(v, add)
        norm.solve(v)
        v.wait_ge(hbr, 2)

        def post(t, u):
            r = tile_rows(t)
            v.scalar_tensor_tensor(out=tmp[0:r, u], in0=yb[0:r, t, :], scalar=norm.mv[0:r, t, 0:1], in1=gam[0:r], op0=ALU.subtract, op1=ALU.mult).then_inc(tch, 1)
            v.wait_ge(tch, t + 1)
            v.scalar_tensor_tensor(out=hb[0:r, t, :], in0=tmp[0:r, u], scalar=norm.rstd[0:r, bass.ds(t, 1)], in1=hb[0:r, t, :], op0=ALU.mult, op1=ALU.add).then_inc(hr, 1)
            v.wait_ge(hr, t + 1)
            norm.take_stats(v, hb, t)

        over_tiles(v, post)

    def gpsimd(p):
        p.wait_ge(h_in[0], 16)
        p.memset(wd, 0.0).then_inc(wz, 1)
        p.memset(wg, 0.0).then_inc(wz, 1)
        p.wait_ge(dr, NC)
        p.memset(db[0:HALF, :, 0], 0.0).then_inc(rst, 1)
        p.memset(db[HALF:P, :, SEQ - 1], 0.0).then_inc(rst, 1)
        p.wait_ge(rst, 2)
        p.wait_ge(w_fb, 16 * 7)
        p.wait_ge(xr, T)
        p.tensor_tensor(hb[:, 0:NB, :], hb[:, 0:NB, :], bc(bet.unsqueeze(1), 1, NB), ALU.add).then_inc(hbr, 1)
        p.wait_ge(hbr, 1)
        p.tensor_tensor(hb[0:NB, NB, :], hb[0:NB, NB, :], bet[0:NB], ALU.add).then_inc(hbr, 1)

    def scalar(s):
        def quarter(q):
            for j in range(4):
                s.wait_ge(turned, 4 * q + j + 1)
                turned_out(s, ps[:, j % 2, :], xnT, 4 * q + j).then_inc(tev, 1)
            s.wait_ge(zp, q + 1)
            s.activation(zb[:, bass.ds(4 * q, 4), 1:SEQ], ps[:, 2, :].rearrange("p (b n) -> p b n", b=4), ACT.Copy).then_inc(zr, 1)

        looped(s, NQ, quarter)
        s.wait_ge(turned, T)
        turned_out(s, ps[:, 0, :], xnT, NB).then_inc(tev, 1)
        s.wait_ge(zp, NQ + 1)
        s.activation(zb[:, :, 0], ps[:, 3, 0:NB], ACT.Copy).then_inc(zr, 1)

        def deltas(c):
            s.wait_ge(op, c + 1)
            s.activation(df[:, bass.ds(c * CW, CW)], ps[:, 4, 0:CW], ACT.Sigmoid).then_inc(dr, 1)

        looped(s, NC, deltas)

    def tensor(t):
        t.wait_ge(w_in, 3 * 16)

        def quarter(q):
            for j in range(4):
                n = 4 * q + j
                t.wait_ge(xr, n + 1)
                if not (is_first(q) and j < 2):
                    t.wait_ge(tev, n - 1)
                turn_tile(t, ps[:, j % 2, :], xn, n, ident).then_inc(turned, 1)
            t.wait_ge(tev, 4 * q + 4)
            if not is_first(q):
                t.wait_ge(zr, q)
            for k in range(KD):
                mm = t.matmul(ps[:, 2, :], win[:, k, :], xnT[:, k, bass.ds(q * QC, QC)], start=(k == 0), stop=(k == KD - 1))
            mm.then_inc(zp, 1)

        for q in range(NQ):
            quarter(q)
        t.wait_ge(xr, T)
        turn_tile(t, ps[:, 0, :], xn, NB, ident).then_inc(turned, 1)
        t.wait_ge(tev, T)
        for k in range(KD):
            mm = t.matmul(ps[:, 3, 0:NB], win[:, k, :], xnT[:, k, NCOL:NTOK], start=(k == 0), stop=(k == KD - 1))
        mm.then_inc(zp, 1)
        t.wait_ge(zr, NQ + 1)
        t.wait_ge(w_fb, 16 * 7)

        def gates(c):
            if not is_first(c):
                t.wait_ge(dr, c)
                t.wait_ge(gr, c)
            cols = bass.ds(c * CW, CW)
            t.matmul(ps[:, 4, 0:CW], wd, zf[:, cols], start=True, stop=True)
            t.matmul(ps[:, 6, 0:CW], wg, zf[:, cols], start=True, stop=True).then_inc(op, 1)

        looped(t, NC, gates)
        t.wait_ge(sc, 2)

        def outs(n, u):
            if not early(n):
                t.wait_ge(yr, n - 1)
            r = tile_rows(n)
            lhs = hs[:, :, 0] if r == NB else hs[:, n, 1:SEQ]
            t.matmul(ps[0:r, 2 + u, :], lhs, wout, start=True, stop=True).then_inc(outp, 1)

        each_tile(outs)

    return sync, vector, gpsimd, scalar, tensor


def ffn_layer(nc, sem, sb, ps, d, g, at, name, F, NBLK, SH, stats_after, before):
    a = Arena(sb, at)
    hb, xn, xnT, ident, norm = g.h, g.xn, g.xnT, g.ident, g.norm
    NE = 8
    NF = -(-F // P)
    FR = [min(P, F - P * f) for f in range(NF)]
    NU = NQ + 1
    wr = a.take(KD, NE + 1)
    wgu, wdn = a.take(2, KD, 2 * F), a.take(2, NF, D)
    hid = a.take(2, NF, QC)
    sil = a.take(2, QC)
    lg, oh0, oh1, t8 = (a.take(T, NE) for _ in range(4))
    sg, m1, m2, wt = a.take(T), a.take(T), a.take(T), a.take(2, T)
    iota = a.take(NE)
    sc = a.take(T, NBLK)

    xr, turned, tev = sem(name + "_xn_ready"), sem(name + "_turned"), sem(name + "_xnT_ready")
    r_in, rp, rch, sgm = sem(name + "_router_loaded"), sem(name + "_scores"), sem(name + "_router_chain"), sem(name + "_sigmoids")
    need_s = sem(name + "_differences")
    w_in = [sem(f"{name}_weights_loaded{u}") for u in range(2)]
    gu, silr, hidr = sem(name + "_gate_up"), sem(name + "_silu"), sem(name + "_hidden")
    dn, acc = sem(name + "_down"), sem(name + "_added")
    WD = 1 + (1 if FR[-1] == P else 2)

    def sync(sp):
        before(sp)
        sp.dma_start(wr, d[name + "_router"]).then_inc(r_in, 16)
        sp.dma_start(iota, d["iota8"].partition_broadcast(P)).then_inc(r_in, 16)

        def pair(i):
            for u in range(2):
                b = 2 * i + u
                if not is_first(i):
                    sp.wait_ge(dn, (b - 1) * T)
                sp.dma_start(wgu[:, u], d[name + "_gate_up"][b]).then_inc(w_in[u], 16)
                full = NF if FR[-1] == P else NF - 1
                sp.dma_start(wdn[:, u, 0:full, :], d[name + "_down"][b, 0:full * P, :].rearrange("(f p) n -> p f n", p=P)).then_inc(w_in[u], 16)
                if full < NF:
                    sp.dma_start(wdn[0:FR[-1], u, full, :], d[name + "_down"][b, full * P:F, :]).then_inc(w_in[u], 16)

        looped(sp, NBLK // 2, pair)

    def order():
        steps = [("gu", 0)]
        for m in range(1, NU):
            steps += [("gu", m), ("dn", m - 1)]
        return steps + [("dn", NU - 1)]

    def unit_cols(m):
        return (slice(NCOL, NTOK), NB) if m == 0 else (slice((m - 1) * QC, m * QC), QC)

    def unit_tiles(m):
        return [NB] if m == 0 else list(range(4 * (m - 1), 4 * m))

    def sums_before(tile, u, first):
        r = 0 if tile == NB else tile + 1
        at0 = u * T
        if r == 0:
            n = at0 - 3
        elif r <= 4:
            n = at0 + 1 if r == 1 else at0 - 4 + r
        else:
            n = at0 + r - 3
        return None if first and n <= 0 else n

    def downs_through(k):
        if k < 0:
            return 0 if k == -1 else -len(unit_tiles(NU - 1))
        return sum(len(unit_tiles(j % NU)) for j in range(k + 1))

    def vector(v):
        norm.solve(v)
        over_tiles(v, lambda t, u: norm.apply(v, xn, hb, t).then_inc(xr, 1))
        c = Chain(v, rch)
        c.link(v.memset(lg, 0.0))
        c.put(v.memset(sg, 0.0))
        v.wait_ge(rp, T)
        s3 = ps[:, 2, 0:T * 16].rearrange("p (t e) -> p t e", e=16)
        c.put(v.tensor_copy(lg[:, 0:NB, :], s3[:, 0:NB, 0:NE]))
        c.put(v.tensor_copy(lg[0:NB, NB, :], s3[0:NB, NB, 0:NE]))
        c.wait()
        c.put(v.tensor_copy(sg[:, 0:NB], s3[:, 0:NB, NE]))
        c.link(v.tensor_copy(sg[0:NB, NB:T], s3[0:NB, NB, NE:NE + 1]))
        v.wait_ge(r_in, 32)
        io = bc(iota.unsqueeze(1), 1, T)
        wide = (lambda x: bc(x.unsqueeze(2), 2, NE))
        for m, oh in ((m1, oh0), (m2, oh1)):
            c.link(v.tensor_reduce(m, lg, AX.X, ALU.max))
            c.link(v.tensor_tensor(t8, lg, wide(m), ALU.is_ge))
            c.link(v.scalar_tensor_tensor(out=t8, in0=t8, scalar=-16.0, in1=io, op0=ALU.mult, op1=ALU.add))
            c.link(v.tensor_reduce(wt[:, 0, :], t8, AX.X, ALU.min))
            c.link(v.tensor_tensor(oh, t8, wide(wt[:, 0, :]), ALU.is_equal))
            c.link(v.scalar_tensor_tensor(out=lg, in0=oh, scalar=-3.0e38, in1=lg, op0=ALU.mult, op1=ALU.add))
        c.link(v.tensor_tensor(wt[:, 0, :], m1, m2, ALU.subtract))
        v.tensor_tensor(wt[:, 1, :], m2, m1, ALU.subtract).then_inc(need_s, 1)
        v.wait_ge(sgm, 2)
        c.put(v.tensor_tensor(oh0, oh0, wide(wt[:, 0, :]), ALU.mult))
        c.link(v.tensor_tensor(oh1, oh1, wide(wt[:, 1, :]), ALU.mult))
        c.put(v.tensor_tensor(sc[:, :, 0:NE], oh0, oh1, ALU.add))
        c.link(v.tensor_copy(sc[:, :, NE:NBLK], bc(sg.unsqueeze(2), 2, SH)))

        def pair(i):
            n = 0
            r = 0
            for u in range(2):
                b = 2 * i + u
                for what, m in order():
                    if what == "gu":
                        cols, w = unit_cols(m)
                        for f in range(NF):
                            v.wait_ge(silr, i * (2 * NU * NF) + n + 1)
                            slot = (u * NU + m) % 2
                            if f == 0 and not (is_first(i) and u == 0 and m < 2):
                                v.wait_ge(dn, i * 2 * T + downs_through(u * NU + m - 2))
                            v.tensor_tensor(hid[0:FR[f], slot, f, 0:w], sil[0:FR[f], n % 2, 0:w],
                                            ps[0:FR[f], 2 * (n % 2) + 1, 0:w], ALU.mult).then_inc(hidr, 1)
                            n += 1
                    else:
                        for t in unit_tiles(m):
                            rows = tile_rows(t)
                            v.wait_ge(dn, i * 2 * T + r + 1)
                            if not (is_first(i) and u == 0):
                                v.wait_ge(acc, i * 2 * T + r - T + 1)
                            bank = 4 if t == NB else 4 + t % 4
                            v.scalar_tensor_tensor(out=hb[0:rows, t, :], in0=ps[0:rows, bank, :], scalar=sc[0:rows, t, bass.ds(b, 1)],
                                                   in1=hb[0:rows, t, :], op0=ALU.mult, op1=ALU.add).then_inc(acc, 1)
                            r += 1

        looped(v, NBLK // 2, pair)
        v.wait_ge(acc, T * NBLK)
        if stats_after:
            over_tiles(v, lambda t, u: norm.take_stats(v, hb, t))

    def gpsimd(p):
        pass

    def scalar(s):
        def turn(t, u):
            s.wait_ge(turned, t + 1)
            turned_out(s, ps[:, u, :], xnT, t).then_inc(tev, 1)

        over_tiles(s, turn)
        s.wait_ge(need_s, 1)
        s.activation(wt, wt, ACT.Sigmoid).then_inc(sgm, 1)
        s.activation(sg, sg, ACT.Sigmoid).then_inc(sgm, 1)

        def pair(i):
            n = 0
            for u in range(2):
                for m in range(NU):
                    cols, w = unit_cols(m)
                    for f in range(NF):
                        s.wait_ge(gu, i * (2 * NU * NF) + n + 1)
                        if not (is_first(i) and n < 2):
                            s.wait_ge(hidr, i * (2 * NU * NF) + n - 1)
                        s.activation(sil[0:FR[f], n % 2, 0:w], ps[0:FR[f], 2 * (n % 2), 0:w], ACT.Silu).then_inc(silr, 1)
                        n += 1

        looped(s, NBLK // 2, pair)

    def tensor(t):
        def turn(n, u):
            t.wait_ge(xr, n + 1)
            if n >= 2:
                t.wait_ge(tev, n - 1)
            turn_tile(t, ps[:, u, :], xn, n, ident).then_inc(turned, 1)

        each_tile(turn)
        t.wait_ge(tev, T)
        t.wait_ge(r_in, 32)

        def score(n, u):
            r = tile_rows(n)
            cols = slice(NCOL, NTOK) if r == NB else slice(n * P, (n + 1) * P)
            for k in range(KD):
                mm = t.matmul(ps[0:r, 2, 16 * n:16 * n + NE + 1], xnT[:, k, cols], wr[:, k, :], start=(k == 0), stop=(k == KD - 1))
            mm.then_inc(rp, 1)

        each_tile(score)
        t.wait_ge(sgm, 2)

        def pair(i):
            n = 0
            for u in range(2):
                t.wait_ge(w_in[u], 16 * WD * (i + 1))
                for what, m in order():
                    slot = (u * NU + m) % 2
                    if what == "gu":
                        cols, w = unit_cols(m)
                        for f in range(NF):
                            if not (is_first(i) and n < 2):
                                t.wait_ge(hidr, i * (2 * NU * NF) + n - 1)
                            for j in range(2):
                                for k in range(KD):
                                    mm = t.matmul(ps[0:FR[f], 2 * (n % 2) + j, 0:w],
                                                  wgu[:, u, k, j * F + f * P:j * F + f * P + FR[f]], xnT[:, k, cols],
                                                  start=(k == 0), stop=(k == KD - 1))
                            mm.then_inc(gu, 1)
                            n += 1
                    else:
                        t.wait_ge(hidr, i * (2 * NU * NF) + (u * NU + m + 1) * NF)
                        for j, tile in enumerate(unit_tiles(m)):
                            rows = tile_rows(tile)
                            bank = 4 if tile == NB else 4 + tile % 4
                            before_n = sums_before(tile, u, is_first(i))
                            if before_n is not None:
                                t.wait_ge(acc, i * 2 * T + before_n)
                            for f in range(NF):
                                mm = t.matmul(ps[0:rows, bank, :], hid[0:FR[f], slot, f, j * P:j * P + rows], wdn[0:FR[f], u, f, :],
                                              start=(f == 0), stop=(f == NF - 1))
                            mm.then_inc(dn, 1)

        looped(t, NBLK // 2, pair)

    return sync, vector, gpsimd, scalar, tensor, acc


def gla_layer(nc, sem, sb, ps, d, g, at, before):
    a = Arena(sb, at)
    hb, xn, xnT, ident, norm = g.h, g.xn, g.xnT, g.ident, g.norm
    KH, BL, NBL = 32, 32, 4
    wqk, wog, wig = a.take(KD, 2 * KH), a.take(KD, D), a.take(KD, D)
    gw, mask = a.take(D), a.take(P)
    ats, ots = a.take(2, P), a.take(2, KD, P)
    atc = a.take(NB, NH, rows=NB)
    sg, pb, junk = a.take(2, D), a.take(2, D), a.take(D)
    ss = a.take(T)
    qs, kb3, = (a.take(NB, SEQ, rows=KH) for _ in range(2))
    b = Arena(sb, g.y_at)
    kb0, kb1, kb2, pv = (b.take(NB, SEQ, rows=KH) for _ in range(4))
    av, bv = kb2, kb1
    sq = a.take(NB, SEQ, rows=KH)
    kb = [kb0, kb1, kb2, kb3]
    F = (lambda x: x.rearrange("p b s -> p (b s)"))

    w_in = sem("gla_weights_loaded")
    xr, turned, tev = sem("gla_xn_ready"), sem("gla_turned"), sem("gla_xnT_ready")
    qk, qsig, ksig, asig, qkr = sem("gla_qk_products"), sem("gla_q_sigmoid"), sem("gla_k_ready"), sem("gla_a_ready"), sem("gla_q_ready")
    kch, kbr, cp = sem("gla_decay_chain"), sem("gla_keys_scaled"), sem("gla_keys_copied")
    acp, atcr = sem("gla_cls_products"), sem("gla_cls_attention")
    ap, atr, ob, otr, ssr = sem("gla_attention_products"), sem("gla_attention_masked"), sem("gla_o_products"), sem("gla_oT_ready"), sem("gla_squares")
    gor, sgr, t1r, pr, gwr = sem("gla_gate_products"), sem("gla_gate_sigmoid"), sem("gla_gated"), sem("gla_gated_o"), sem("gla_weighted")
    hr = sem("gla_h_ready")
    zr = sem("gla_cleared")

    def sync(sp):
        before(sp)
        sp.dma_start(wqk, d["Wqk"]).then_inc(w_in, 16)
        sp.dma_start(wog, d["Wog"].rearrange("(k p) n -> p k n", p=P)).then_inc(w_in, 16)
        sp.dma_start(wig, d["Wig"].rearrange("(k p) n -> p k n", p=P)).then_inc(w_in, 16)
        sp.dma_start(gw, d["g_weight"].partition_broadcast(P)).then_inc(w_in, 16)
        sp.dma_start(mask, d["causal"]).then_inc(w_in, 16)

    def vector(v):
        norm.solve(v)
        over_tiles(v, lambda t, u: norm.apply(v, xn, hb, t).then_inc(xr, 1))
        c = Chain(v, kch)
        c.put(v.memset(ss, 1.0))

        def queries(q):
            v.wait_ge(qsig, q + 1)
            src = ps[0:KH, 2, :].rearrange("p (b n) -> p b n", b=4)
            bs = bass.ds(4 * q, 4)
            v.scalar_tensor_tensor(out=qs[:, bs, 1:SEQ], in0=src, scalar=SILU_SCALE, in1=sq[:, bs, 1:SEQ], op0=ALU.mult, op1=ALU.mult).then_inc(qkr, 1)

        looped(v, NQ, queries)
        v.wait_ge(qsig, NQ + 1)
        v.scalar_tensor_tensor(out=qs[:, :, 0], in0=ps[0:KH, 3, 0:NB], scalar=SILU_SCALE, in1=sq[:, :, 0], op0=ALU.mult, op1=ALU.mult).then_inc(qkr, 1)
        v.wait_ge(asig, NQ + 1)
        c.link(v.memset(bv, 0.0))
        starts = slice(1, SEQ, BL)
        c.put(v.tensor_copy(bv[:, :, starts], av[:, :, starts]))
        c.put(v.memset(bv[:, :, 0], 1.0))
        c.wait()
        c.put(v.memset(av[:, :, starts], 0.0))
        c.link(v.memset(av[:, :, 0], 0.0))
        c.link(v.tensor_tensor_scan(F(pv), F(av), F(bv), 0.0, ALU.mult, ALU.add))
        v.wait_ge(qkr, NQ + 1)
        c.link(v.reciprocal(F(av), F(pv)))
        c.put(v.tensor_tensor(F(qs), F(qs), F(pv), ALU.mult))
        v.wait_ge(ksig, NQ + 1)
        v.tensor_tensor(F(kb0), F(kb0), F(av), ALU.mult).then_inc(kbr, 1)
        v.wait_ge(kbr, 1)
        c.wait()
        for n in range(1, NBL):
            w = 1 + BL * n
            total = pv[:, :, BL * n:BL * n + 1]
            if n > 1:
                v.wait_ge(cp, n - 1)
            v.tensor_tensor(kb[n][:, :, 0:w], kb[n - 1][:, :, 0:w], bc(total, 2, w), ALU.mult).then_inc(kbr, 1)
            v.wait_ge(kbr, n + 1)
        v.wait_ge(w_in, 5 * 16)
        own = ident[0:NB, 0:NB].unsqueeze(2)
        for n in range(NBL):
            v.wait_ge(acp, n + 1)
            v.tensor_tensor(atc[:, :, n * BL:(n + 1) * BL], ps[0:NB, n, :].rearrange("p (b n) -> p b n", b=NB), bc(own, 2, BL), ALU.mult).then_inc(atcr, 1)

        def masked(t, u):
            v.wait_ge(ap, t + 1)
            if not early(t):
                v.wait_ge(ob, t - 1)
            if tile_rows(t) == NB:
                v.tensor_tensor(ats[0:NB, u, 0:NB], ps[0:NB, u, 0:NB], ident[0:NB, 0:NB], ALU.mult).then_inc(atr, 1)
            else:
                v.tensor_tensor(ats[:, u], ps[:, u, 0:P], mask, ALU.mult).then_inc(atr, 1)

        def gated(t, u):
            r = tile_rows(t)
            v.wait_ge(sgr, t + 1)
            v.tensor_tensor(sg[0:r, u], ps[0:r, 6 + u, :], sg[0:r, u], ALU.mult).then_inc(t1r, 1)
            v.wait_ge(t1r, t + 1)
            if not early(t):
                v.wait_ge(gwr, t - 1)
            v.wait_ge(ssr, t + 1)
            v.tensor_tensor(pb[0:r, u], ps[0:r, 2 + u, :], sg[0:r, u], ALU.mult).then_inc(pr, 1)

        masked(0, 0)
        masked(1, 1)
        gated_loop(v, lambda t, u: (masked(t + 1, 1 - u), gated(t - 1, 1 - u)))
        masked(NB, 0)
        gated(NB - 2, 0)
        gated(NB - 1, 1)
        gated(NB, 0)
        v.wait_ge(ssr, T)
        c2 = norm.chain(v)
        norm.newton(v, c2, ss, 1.0 / D, LN_EPS)
        norm.closed(c2)

        def add(t, u):
            r = tile_rows(t)
            v.wait_ge(gwr, t + 1)
            v.scalar_tensor_tensor(out=hb[0:r, t, :], in0=xn[0:r, t, :], scalar=norm.rstd[0:r, bass.ds(t, 1)], in1=hb[0:r, t, :], op0=ALU.mult, op1=ALU.add).then_inc(hr, 1)
            v.wait_ge(hr, t + 1)
            norm.take_stats(v, hb, t)

        over_tiles(v, add)

    def gated_loop(eng, body):
        def pair(i):
            for u in range(2):
                body(2 * i + 1 + u, 1 - u)

        looped(eng, NB // 2 - 1, pair)

    def gpsimd(p):
        p.wait_ge(w_in, 5 * 16)

        def weigh(t, u):
            r = tile_rows(t)
            p.wait_ge(pr, t + 1)
            if isinstance(t, int) and t == NB:
                p.wait_ge(ob, T)
            p.tensor_tensor(xn[0:r, t, :], pb[0:r, u], gw[0:r], ALU.mult).then_inc(gwr, 1)

        over_tiles(p, weigh)

    def scalar(s):
        def sigmoids(q, src_q, src_k, w, out):
            s.wait_ge(qk, q + 1)
            s.activation(out(sq), src_q, ACT.Sigmoid).then_inc(qsig, 1)
            s.activation(out(kb0), src_k, ACT.Sigmoid).then_inc(ksig, 1)
            s.wait_ge(ksig, q + 1)
            s.activation(out(av), out(kb0), ACT.Sigmoid, scale=-1.0).then_inc(asig, 1)

        def quarter(q):
            for j in range(4):
                s.wait_ge(turned, 4 * q + j + 1)
                turned_out(s, ps[:, j % 2, :], xnT, 4 * q + j).then_inc(tev, 1)
            split = (lambda x: x.rearrange("p (b n) -> p b n", b=4))
            sigmoids(q, split(ps[0:KH, 2, :]), split(ps[KH:2 * KH, 2, :]), QC, lambda x: x[:, bass.ds(4 * q, 4), 1:SEQ])

        looped(s, NQ, quarter)
        s.wait_ge(turned, T)
        turned_out(s, ps[:, 0, :], xnT, NB).then_inc(tev, 1)
        sigmoids(NQ, ps[0:KH, 3, 0:NB], ps[KH:2 * KH, 3, 0:NB], NB, lambda x: x[:, :, 0])
        for n in range(1, NBL):
            s.wait_ge(kbr, n)
            w = 1 + BL * n
            s.activation(kb[n][:, :, w:SEQ], kb0[:, :, w:SEQ], ACT.Copy).then_inc(cp, 1)

        def outs(t, u):
            r = tile_rows(t)
            s.wait_ge(ob, t + 1)
            if not early(t):
                s.wait_ge(gor, t - 1)
            s.activation(ots[:, u, :, 0:r], ps[:, 4 + u, 0:KD * r].rearrange("p (k n) -> p k n", k=KD), ACT.Copy).then_inc(otr, 1)
            if not (isinstance(t, int) and t == 0):
                s.wait_ge(ssr, t)
            s.activation(junk[0:r], ps[0:r, 2 + u, :], ACT.Square, accum_out=ss[0:r, bass.ds(t, 1)]).then_inc(ssr, 1)

        def gate(t, u):
            r = tile_rows(t)
            s.wait_ge(gor, t + 1)
            if not early(t):
                s.wait_ge(pr, t - 1)
            s.activation(sg[0:r, u], ps[0:r, 6 + u, :], ACT.Sigmoid).then_inc(sgr, 1)

        outs(0, 0)
        gated_loop(s, lambda t, u: (outs(t, u), gate(t - 1, 1 - u)))
        outs(NB - 1, 1)
        gate(NB - 2, 0)
        outs(NB, 0)
        gate(NB - 1, 1)
        gate(NB, 0)

    def tensor(t):
        t.wait_ge(w_in, 5 * 16)

        def project(q, cols, w, bank):
            for k in range(KD):
                mm = t.matmul(ps[0:2 * KH, bank, 0:w], wqk[:, k, :], xnT[:, k, cols], start=(k == 0), stop=(k == KD - 1))
            mm.then_inc(qk, 1)

        for q in range(NQ):
            for j in range(4):
                n = 4 * q + j
                t.wait_ge(xr, n + 1)
                if n >= 2:
                    t.wait_ge(tev, n - 1)
                turn_tile(t, ps[:, j % 2, :], xn, n, ident).then_inc(turned, 1)
            t.wait_ge(tev, 4 * q + 4)
            if q:
                t.wait_ge(qkr, q)
                t.wait_ge(ksig, q)
            project(q, slice(q * QC, (q + 1) * QC), QC, 2)
        t.wait_ge(xr, T)
        turn_tile(t, ps[:, 0, :], xn, NB, ident).then_inc(turned, 1)
        t.wait_ge(tev, T)
        project(NQ, slice(NCOL, NTOK), NB, 3)
        t.wait_ge(cp, NBL - 1)
        t.wait_ge(kbr, NBL)
        t.wait_ge(qkr, NQ + 1)
        for n in range(NBL):
            t.matmul(ps[0:NB, n, :], kb[n][:, :, 0], qs[:, :, 1 + n * BL:1 + (n + 1) * BL], start=True, stop=True).then_inc(acp, 1)
        t.wait_ge(atcr, NBL)

        def attend(n):
            u = n % 2
            if n >= 2:
                t.wait_ge(atr, n - 1)
            if n == NB:
                t.matmul(ps[0:NB, u, 0:NB], kb0[:, :, 0], qs[:, :, 0], start=True, stop=True).then_inc(ap, 1)
                return
            for m in range(NBL):
                mm = t.matmul(ps[:, u, m * BL:(m + 1) * BL], kb[m][:, n, 1:SEQ], qs[:, n, 1 + m * BL:1 + (m + 1) * BL], start=True, stop=True)
            mm.then_inc(ap, 1)

        def outs(n):
            u, r = n % 2, tile_rows(n)
            t.wait_ge(atr, n + 1)
            if n >= 2:
                t.wait_ge(pr, n - 1)
                t.wait_ge(otr, n - 1)
            last = n == NB
            t.matmul(ps[0:r, 2 + u, :], ats[0:r, u, 0:r], xn[0:r, n, :], start=True, stop=last)
            if not last:
                t.matmul(ps[0:r, 2 + u, :], atc[:, n, :], xn[0:NB, NB, :], start=False, stop=True)
            for k in range(KD):
                ks = slice(k * P, (k + 1) * P)
                mm = t.matmul(ps[:, 4 + u, k * r:(k + 1) * r], xn[0:r, n, ks], ats[0:r, u, 0:r], start=True, stop=last)
                if not last:
                    mm = t.matmul(ps[:, 4 + u, k * r:(k + 1) * r], xn[0:NB, NB, ks], atc[:, n, :], start=False, stop=True)
            mm.then_inc(ob, 1)

        def gate(n):
            u, r = n % 2, tile_rows(n)
            cols = slice(NCOL, NTOK) if n == NB else slice(n * P, (n + 1) * P)
            t.wait_ge(otr, n + 1)
            if n >= 2:
                t.wait_ge(pr, n - 1)
            for k in range(KD):
                t.matmul(ps[0:r, 6 + u, :], xnT[:, k, cols], wig[:, k, :], start=(k == 0), stop=False)
            for k in range(KD):
                mm = t.matmul(ps[0:r, 6 + u, :], ots[:, u, k, 0:r], wog[:, k, :], start=False, stop=(k == KD - 1))
            mm.then_inc(gor, 1)

        attend(0)
        for n in range(T):
            if n + 1 < T:
                attend(n + 1)
            outs(n)
            if n:
                gate(n - 1)
        gate(NB)

    return sync, vector, gpsimd, scalar, tensor, hr


class Shared:

    def __init__(self, nc, sem, arena):
        self.h, self.xn = arena.take(T, D), arena.take(T, D)
        self.y_at = arena.at
        self.y = arena.take(T, D)
        self.xnT = arena.take(KD, NTOK)
        self.ident = arena.take(P)
        self.norm = Norm(arena, sem("norm_chain"))
        self.h_ready = sem("h_after_scan")


def tower(nc, d, out):
    with ExitStack() as ctx:
        def sem(name):
            return ctx.enter_context(nc.semaphore(name))

        sb = ctx.enter_context(nc.sbuf_tensor("sb", [P, 51 * 1024], F32))
        ps = ctx.enter_context(nc.psum_tensor("ps", [P, 8, 512], F32))
        h0 = nc.dram_tensor("tokens", (NB, NH, D), F32).ap()
        arena = Arena(sb)
        g = Shared(nc, sem, arena)
        tok = tokenizer(nc, sem, sb, ps, d, h0, 0)
        scan = scan_layer(nc, sem, sb, ps, d, h0, tok[5], g, arena.at)
        ffn0 = ffn_layer(nc, sem, sb, ps, d, g, arena.at, "ffn0", 256, 10, 2, True, lambda sp: sp.wait_ge(g.h_ready, T))
        gla = gla_layer(nc, sem, sb, ps, d, g, arena.at, lambda sp: sp.wait_ge(ffn0[5], T * 10))
        ffn1 = ffn_layer(nc, sem, sb, ps, d, g, arena.at, "ffn1", 352, 12, 4, False, lambda sp: sp.wait_ge(gla[5], T))
        h_out = sem("h_stored")
        block = ctx.enter_context(nc.Block())

        @block.sync
        def _(sp):
            tok[0](sp)
            scan[0](sp)
            ffn0[0](sp)
            gla[0](sp)
            ffn1[0](sp)
            sp.wait_ge(ffn1[5], T * 12)
            sp.dma_start(out[:, 1:SEQ, :].rearrange("b p d -> p b d"), g.h[:, 0:NB, :]).then_inc(h_out, 16)
            sp.dma_start(out[:, 0, :], g.h[0:NB, NB, :]).then_inc(h_out, 16)
            sp.wait_ge(h_out, 32)

        @block.vector
        def _(v):
            tok[1](v)
            scan[1](v)
            ffn0[1](v)
            gla[1](v)
            ffn1[1](v)

        @block.gpsimd
        def _(p):
            tok[2](p)
            scan[2](p)
            ffn0[2](p)
            gla[2](p)
            ffn1[2](p)

        @block.scalar
        def _(s):
            tok[3](s)
            scan[3](s)
            ffn0[3](s)
            gla[3](s)
            ffn1[3](s)

        @block.tensor
        def _(t):
            tok[4](t)
            scan[4](t)
            ffn0[4](t)
            gla[4](t)
            ffn1[4](t)


def laid_out(i):
    f = {k: np.asarray(v) for k, v in i.items()}
    t8 = np.arange(TB)
    k0 = np.concatenate([t8, TB * t8, TJ * t8, [0.5, 1, L // 2, L]])
    km = np.concatenate([np.repeat([TB - 1, TB * (TB - 1), TJ * (TB - 1)], TB), [0, 0, 0, 0]])

    def gate_up(gate, up):
        w = np.concatenate([gate, up], axis=2)
        n, _, c = w.shape
        return w.reshape(n, KD, P, c).transpose(0, 2, 1, 3)

    def cut(w, n):
        return w.reshape(w.shape[0], n, -1).transpose(1, 0, 2)

    def router(gate, shared):
        return np.concatenate([gate.T, shared.reshape(D, 1)], axis=1).reshape(KD, P, -1).transpose(1, 0, 2)

    T01 = (0, 2, 1)
    a = {
        "kconst": np.stack([k0, -km]).astype(np.float32),
        "lam": f["L0_tok_Lambda"],
        "log_dt": f["L0_tok_log_dt"].T,
        "x": f["x"].transpose(3, 2, 1, 0).reshape(2, NS, NH * NB),
        "ident": np.eye(P, dtype=np.float32),
        "W_in": f["L0_attn_W_in"], "W_fwd": f["L0_attn_W_fwd"], "W_bwd": f["L0_attn_W_bwd"], "W_out": f["L0_attn_W_out"],
        "gamma": f["L0_attn_gamma"], "beta": f["L0_attn_beta"],
        "iota8": np.arange(8, dtype=np.float32),
        "ffn0_router": router(f["L0_ffn_gate_w"], f["L0_ffn_se_gate_w"]),
        "ffn0_gate_up": gate_up(np.concatenate([f["L0_ffn_w_gate"].transpose(T01), cut(f["L0_ffn_sh_gate"].T, 2)]),
                                np.concatenate([f["L0_ffn_w_up"].transpose(T01), cut(f["L0_ffn_sh_up"].T, 2)])),
        "ffn0_down": np.concatenate([f["L0_ffn_w_down"].transpose(T01), f["L0_ffn_sh_down"].T.reshape(2, 256, D)]),
        "Wqk": np.concatenate([f["L1_attn_Wq"].T, f["L1_attn_Wk"].T], axis=1).reshape(KD, P, -1).transpose(1, 0, 2),
        "Wog": f["L1_attn_Wog"].T, "Wig": f["L1_attn_Wig"].T, "g_weight": f["L1_attn_g_weight"],
        "causal": np.triu(np.ones((P, P), np.float32)),
        "ffn1_router": router(f["L1_ffn_gate_w"], f["L1_ffn_shared_gate_w"]),
        "ffn1_gate_up": gate_up(np.concatenate([f["L1_ffn_w_gate"], cut(f["L1_ffn_sw_gate"], 4)]),
                                np.concatenate([f["L1_ffn_w_up"], cut(f["L1_ffn_sw_up"], 4)])),
        "ffn1_down": np.concatenate([f["L1_ffn_w_down"], f["L1_ffn_sw_down"].reshape(4, 352, D)]),
        "cls": np.broadcast_to(f["cls_tok"][0], (NB, D)),
    }
    return {k: np.ascontiguousarray(v) for k, v in a.items()}


def kernel(**inputs):
    import concourse.bacc as _bacc
    from concourse.bass_utils import run_bass_kernel_spmd as _run

    nc = _bacc.Bacc("TRN2", target_bir_lowering=False, num_devices=1)
    arrays, d = {}, {}
    for name, a in laid_out(inputs).items():
        arrays[f"in_{name}"] = a
        d[name] = nc.dram_tensor(f"in_{name}", a.shape, F32, kind="ExternalInput").ap()
    out = nc.dram_tensor("out", (NB, SEQ, D), F32, kind="ExternalOutput").ap()
    tower(nc, d, out)
    r = _run(nc, [arrays], core_ids=[0])
    return r.results[0]["out"]
```

```python
from contextlib import ExitStack

import concourse.bass as bass
import numpy as np
from concourse import mybir

F32 = mybir.dt.float32
I32 = mybir.dt.int32
U32 = mybir.dt.uint32
ALU = mybir.AluOpType
ACT = mybir.ActivationFunctionType
AX = mybir.AxisListType

P = 128
NB = 16
NH = 128
NS = 64
L = 512
D = 512
KD = D // P
T = NB + 1
NCOL = NB * NH
NTOK = NB * (NH + 1)
SEQ = NH + 1
NQ = 4
QC = 512
LN_EPS = 1e-5
SILU_SCALE = 32 ** -0.5

TB = 8
TI, TJ = 8, 64
HC = 16
NHC = NH // HC
NK = 3 * TB
MAGIC = 1.5 * 2.0 ** 23
TWO_PI = 2 * np.pi


class Chain:

    def __init__(self, eng, sem, base=0):
        self.eng, self.sem, self.base, self.n = eng, sem, base, 0

    def put(self, ins):
        self.n += 1
        ins.then_inc(self.sem, 1)

    def wait(self):
        self.eng.wait_ge(self.sem, self.base + self.n)

    def link(self, ins):
        self.put(ins)
        self.wait()


def looped(eng, n, body):
    body(0)
    if n > 1:
        with eng.Fori(1, n) as i:
            body(i)


def is_first(i):
    return isinstance(i, int) and i == 0


def bc(ap, dim, n):
    shape = list(ap.shape)
    shape[dim] = n
    return ap.to_broadcast(shape)


class Arena:

    def __init__(self, tensor, at=0):
        self.tensor, self.at = tensor, at

    def take(self, *shape, rows=P, dt=F32):
        size = int(np.prod(shape))
        flat = self.tensor[0:rows, self.at:self.at + size]
        self.at += size + size % 2
        assert self.at <= self.tensor.shape[1], self.at
        if dt != F32:
            flat = flat.bitcast(dt)
        if len(shape) == 1:
            return flat
        names = [f"d{k}" for k in range(len(shape))]
        return flat.rearrange(f"p ({' '.join(names)}) -> p {' '.join(names)}",
                              **{n: s for n, s in zip(names[1:], shape[1:])})


def tokenizer(nc, sem, sb, ps, d, h0, arena_at):
    a = Arena(sb, arena_at)
    lam = a.take(2)
    ld = a.take(2, NH)
    kc = a.take(2, NK + 4)
    wre, wim = a.take(NH, NB), a.take(NH, NB)
    pos, sig, sgn = a.take(1), a.take(1), a.take(1)
    kt, kt2 = a.take(NK), a.take(4)
    ex, en, er, ep, es = (a.take(4, NH) for _ in range(5))
    eni = a.take(4 * NH, dt=I32)
    dt = a.take(2, NH)
    dre, dim = a.take(NH), a.take(NH)
    em = a.take(2, NH)
    fa, fb, p1, q, t0, fhi, flo = (a.take(NH) for _ in range(7))
    sm = [a.take(NH, 4) for _ in range(6)]
    nr, ni, dr, di, xr, xi, s0, s1, inv = (a.take(NH) for _ in range(9))
    cr, ci, c1, c2 = (a.take(NH) for _ in range(4))
    m, kl, ke, mk, re, im = (a.take(NH, NK) for _ in range(6))
    a1, a2 = a.take(2, HC, TI), a.take(2, HC, TI)
    d1, d2 = a.take(2, HC, TB), a.take(2, HC, TB)
    ta, tb = a.take(HC, TB), a.take(HC, TB)
    u1, u2 = a.take(2, HC, TI * NB), a.take(2, HC, TI * NB)
    bb, bt = a.take(2, HC, TJ), a.take(HC, TJ)
    ob = a.take(2, HC * TJ)
    LO, HI = slice(0, NS), slice(NS, P)
    INV = 1.0 / TWO_PI

    def top12(x):
        return float((np.array([x], np.float32).view(np.uint32) & np.uint32(0xFFFFF000)).view(np.float32)[0])

    V1 = top12(INV)
    V2 = top12(INV - V1)
    V3 = float(np.float32(INV - V1 - V2))
    LN2H = 355.0 / 512.0
    LN2L = float(np.log(2.0) - LN2H)

    par_in, w_in = sem("tok_params_loaded"), sem("tok_weights_loaded")
    dch, pch = sem("tok_dve_chain"), sem("tok_pool_chain")
    phase = sem("tok_phase_split")
    lin = sem("tok_linear_ready")
    sm_in, sm_out = sem("tok_small_args"), sem("tok_small_sines")
    arg, sines = sem("tok_sine_args"), sem("tok_sines")
    expd = sem("tok_decays")
    scaled = sem("tok_tables_scaled")
    ab, uw, u2r = sem("tok_factors"), sem("tok_u1_and_b"), sem("tok_u2")
    prod, evac, stored = sem("tok_products"), sem("tok_evacuated"), [sem(f"tok_stored{k}") for k in range(2)]
    H2 = NH // 2
    hs = [slice(0, H2), slice(H2, NH)]
    cch = sem("tok_step_chain")

    def sync(sp):
        for half in (LO, HI):
            sp.dma_start(lam[half, :], d["lam"]).then_inc(par_in, 16)
        for k in range(2):
            sp.dma_start(ld[:, k, :], d["log_dt"][k].partition_broadcast(P)).then_inc(par_in, 16)
            sp.dma_start(kc[:, k, :], d["kconst"][k].partition_broadcast(P)).then_inc(par_in, 16)
        for w, k in ((wre, 0), (wim, 1)):
            for half in (LO, HI):
                sp.dma_start(w[half, :, :].rearrange("p h c -> p (h c)"), d["x"][k]).then_inc(w_in, 16)
        h0v = h0.rearrange("c (g h) (i j) -> i c g h j", j=TJ, h=HC)

        def store(k, u):
            sp.wait_ge(evac, 2 * k + 2)
            for i in range(TI):
                sp.dma_start(h0v[i, :, k, :, :],
                             ob[i * NB:(i + 1) * NB, u, :].rearrange("c (h j) -> c h j", j=TJ)).then_inc(stored[u], 16)

        def pair(i):
            for u in range(2):
                store(2 * i + u, u)

        looped(sp, NHC // 2, pair)
    def all_stored(sp):
        for u in range(2):
            sp.wait_ge(stored[u], 16 * TI * NHC // 2)

    def vector(v):
        c = Chain(v, dch)
        v.wait_ge(par_in, 6 * 16)

        def exp_parts(x, w):
            X, N, R, PM, S = (t[:, 0:w, :] for t in (x, en, er, ep, es))
            NI = eni[:, 0:w * NH].rearrange("p (a b) -> p a b", b=NH)
            c.link(v.tensor_scalar(X, X, -87.0, 88.0, ALU.max, ALU.min))
            c.link(v.tensor_scalar(N, X, float(1 / np.log(2.0)), MAGIC, ALU.mult, ALU.add))
            c.link(v.tensor_scalar(N, N, -MAGIC, None, ALU.add))
            c.link(v.scalar_tensor_tensor(out=R, in0=N, scalar=-LN2H, in1=X, op0=ALU.mult, op1=ALU.add))
            c.link(v.scalar_tensor_tensor(out=R, in0=N, scalar=-LN2L, in1=R, op0=ALU.mult, op1=ALU.add))
            c.link(v.tensor_scalar(PM, R, 1.0 / 40320, None, ALU.mult))
            for f in (5040, 720, 120, 24, 6, 2, 1):
                c.link(v.scalar_tensor_tensor(out=PM, in0=PM, scalar=1.0 / f, in1=R, op0=ALU.add, op1=ALU.mult))
            c.link(v.tensor_scalar(NI, N, 127.0, None, ALU.add))
            c.link(v.tensor_scalar(S.bitcast(I32), NI, 23, None, ALU.logical_shift_left))

        c.link(v.tensor_copy(ex[:, 0:2, :], ld[:, :, :]))
        exp_parts(ex, 2)
        c.link(v.scalar_tensor_tensor(out=dt, in0=ep[:, 0:2, :], scalar=1.0, in1=es[:, 0:2, :], op0=ALU.add, op1=ALU.mult))
        c.link(v.tensor_scalar(dre, dt[:, 0, :], lam[:, 0:1], None, ALU.mult))
        c.link(v.tensor_scalar(dim, dt[:, 1, :], lam[:, 1:2], None, ALU.mult))
        c.link(v.tensor_scalar(pos, lam[:, 0:1], 0.0, None, ALU.is_gt))
        c.link(v.tensor_scalar(sig, pos, -2.0, 1.0, ALU.mult, ALU.add))
        c.link(v.memset(sgn[LO, :], 1.0))
        c.link(v.memset(sgn[HI, :], -1.0))
        c.link(v.scalar_tensor_tensor(out=kt, in0=kc[:, 1, 0:NK], scalar=pos[:, 0:1], in1=kc[:, 0, 0:NK], op0=ALU.mult, op1=ALU.add))
        c.link(v.tensor_copy(kt2, kc[:, 0, NK:NK + 4]))
        c.link(v.tensor_scalar(fa.bitcast(U32), dim.bitcast(U32), 0xFFFFF000, None, ALU.bitwise_and))
        c.link(v.tensor_tensor(fb, dim, fa, ALU.subtract))
        c.link(v.tensor_scalar(p1, fa, V1, None, ALU.mult))
        c.link(v.tensor_scalar(t0, p1, MAGIC, None, ALU.add))
        c.link(v.scalar_tensor_tensor(out=t0, in0=t0, scalar=-MAGIC, in1=p1, op0=ALU.add, op1=ALU.subtract))
        c.link(v.tensor_scalar(p1, t0, -1.0, None, ALU.mult))
        c.link(v.tensor_scalar(q, fb, V2, None, ALU.mult))
        c.link(v.scalar_tensor_tensor(out=q, in0=fa, scalar=V3, in1=q, op0=ALU.mult, op1=ALU.add))
        c.link(v.tensor_scalar(t0, fb, V1, None, ALU.mult))
        c.link(v.scalar_tensor_tensor(out=t0, in0=fa, scalar=V2, in1=t0, op0=ALU.mult, op1=ALU.add))
        c.link(v.tensor_tensor(q, q, t0, ALU.add))
        c.link(v.tensor_tensor(t0, p1, q, ALU.add))
        c.link(v.tensor_scalar(t0, t0, MAGIC / 32768, None, ALU.add))
        c.link(v.tensor_scalar(fhi, t0, -MAGIC / 32768, None, ALU.add))
        c.link(v.tensor_tensor(flo, p1, fhi, ALU.subtract))
        v.tensor_tensor(flo, flo, q, ALU.add).then_inc(phase, 1)
        v.wait_ge(phase, 1)
        c.link(v.tensor_scalar(t0, fhi, MAGIC, None, ALU.add))
        c.link(v.tensor_scalar(t0, t0, -MAGIC, None, ALU.add))
        c.link(v.tensor_tensor(fhi, fhi, t0, ALU.subtract))

        def args(out, mm, mmk, kk, ph):
            c.link(v.tensor_scalar(out, mmk, ph, MAGIC, ALU.add, ALU.add))
            c.link(v.scalar_tensor_tensor(out=out, in0=out, scalar=-MAGIC, in1=mm, op0=ALU.add, op1=ALU.subtract))
            c.link(v.scalar_tensor_tensor(out=out, in0=out, scalar=-ph, in1=kk, op0=ALU.add, op1=ALU.subtract))
            return v.tensor_scalar(out, out, -0.5, 0.5, ALU.max, ALU.min)

        def spread(x, w):
            return bc(x.unsqueeze(2), 2, w)

        k4 = bc(kt2.unsqueeze(1), 1, NH)
        ms, ks, mks, co, si, _ = sm
        c.link(v.tensor_tensor(ms, k4, spread(fhi, 4), ALU.mult))
        c.link(v.tensor_tensor(ks, k4, spread(flo, 4), ALU.mult))
        c.link(v.tensor_tensor(mks, ms, ks, ALU.add))
        args(si, ms, mks, ks, 0.0).then_inc(sm_in, 1)
        args(co, ms, mks, ks, 0.25).then_inc(sm_in, 1)
        k24 = bc(kt.unsqueeze(1), 1, H2)
        for n, h in enumerate(hs):
            c.link(v.tensor_tensor(m[:, h, :], k24, spread(fhi[:, h], NK), ALU.mult))
            v.wait_ge(lin, 2 * n + 2)
            c.link(v.tensor_tensor(mk[:, h, :], m[:, h, :], kl[:, h, :], ALU.add))
            args(re[:, h, :], m[:, h, :], mk[:, h, :], kl[:, h, :], 0.25).then_inc(arg, 1)
            args(im[:, h, :], m[:, h, :], mk[:, h, :], kl[:, h, :], 0.0).then_inc(arg, 1)
        c.link(v.tensor_scalar(ex[:, 0, :], dre, sig[:, 0:1], None, ALU.mult))
        c.link(v.tensor_scalar(ex[:, 1, :], ex[:, 0, :], float(L), None, ALU.mult))
        exp_parts(ex, 2)
        c.link(v.tensor_tensor(em, ep[:, 0:2, :], es[:, 0:2, :], ALU.mult))
        c.link(v.scalar_tensor_tensor(out=em, in0=es[:, 0:2, :], scalar=-1.0, in1=em, op0=ALU.add, op1=ALU.add))
        v.wait_ge(sm_out, 2)
        for out_r, out_i, e, kk in ((nr, ni, em[:, 0, :], 1), (dr, di, em[:, 1, :], 3)):
            c.link(v.tensor_tensor(s0, si[:, :, kk - 1], si[:, :, kk - 1], ALU.mult))
            c.link(v.tensor_tensor(out_r, e, co[:, :, kk], ALU.mult))
            c.link(v.scalar_tensor_tensor(out=out_r, in0=s0, scalar=-2.0, in1=out_r, op0=ALU.mult, op1=ALU.add))
            c.link(v.scalar_tensor_tensor(out=out_i, in0=e, scalar=1.0, in1=si[:, :, kk], op0=ALU.add, op1=ALU.mult))
            c.link(v.tensor_scalar(out_i, out_i, sig[:, 0:1], None, ALU.mult))
        c.link(v.tensor_scalar(s0, di, lam[:, 1:2], None, ALU.mult))
        c.link(v.scalar_tensor_tensor(out=xr, in0=dr, scalar=lam[:, 0:1], in1=s0, op0=ALU.mult, op1=ALU.subtract))
        c.link(v.tensor_scalar(s0, di, lam[:, 0:1], None, ALU.mult))
        c.link(v.scalar_tensor_tensor(out=xi, in0=dr, scalar=lam[:, 1:2], in1=s0, op0=ALU.mult, op1=ALU.add))
        c.link(v.tensor_tensor(s0, xr, xr, ALU.mult))
        c.link(v.tensor_tensor(s1, xi, xi, ALU.mult))
        c.link(v.scalar_tensor_tensor(out=s0, in0=s0, scalar=1e-7, in1=s1, op0=ALU.add, op1=ALU.add))
        c.link(v.reciprocal(inv, s0))
        for out, g, h, w, x, op in ((cr, nr, xr, ni, xi, ALU.add), (ci, ni, xr, nr, xi, ALU.subtract)):
            c.link(v.tensor_tensor(s0, g, h, ALU.mult))
            c.link(v.tensor_tensor(s1, w, x, ALU.mult))
            c.link(v.tensor_tensor(s0, s0, s1, op))
            c.link(v.tensor_tensor(out, s0, inv, ALU.mult))
        c.link(v.tensor_copy(c1[LO, :], cr[LO, :]))
        c.link(v.tensor_copy(c1[HI, :], ci[HI, :]))
        c.link(v.tensor_scalar(c2[LO, :], ci[LO, :], -1.0, None, ALU.mult))
        c.link(v.tensor_copy(c2[HI, :], cr[HI, :]))
        v.wait_ge(w_in, 64)
        v.wait_ge(scaled, 4)

        PER = 22

        def pair(i):
            s = Chain(v, cch, i * PER)
            for u in range(2):
                k = 2 * i + u
                hh = bass.ds(k * HC, HC)
                AR, AI = re[:, hh, 2 * TB:3 * TB], im[:, hh, 2 * TB:3 * TB]
                R1, I1 = re[:, hh, 0:TB], im[:, hh, 0:TB]
                R2, I2 = re[:, hh, TB:2 * TB], im[:, hh, TB:2 * TB]
                C1, C2 = spread(c1[:, hh], TI), spread(c2[:, hh], TI)
                if not is_first(i):
                    v.wait_ge(prod, 2 * (k - 1))
                s.put(v.tensor_tensor(a1[:, u], C1, AR, ALU.mult))
                s.put(v.tensor_tensor(ta, C2, AI, ALU.mult))
                s.put(v.tensor_tensor(a2[:, u], C2, AR, ALU.mult))
                s.link(v.tensor_tensor(tb, C1, AI, ALU.mult))
                s.put(v.tensor_tensor(a1[:, u], a1[:, u], ta, ALU.add))
                v.tensor_tensor(a2[:, u], a2[:, u], tb, ALU.subtract).then_inc(ab, 1)
                s.put(v.tensor_copy(d1[LO, u], R2[LO]))
                s.put(v.tensor_scalar(d1[HI, u], I2[HI], -1.0, None, ALU.mult))
                s.put(v.tensor_scalar(d2[LO, u], I2[LO], -1.0, None, ALU.mult))
                s.link(v.tensor_scalar(d2[HI, u], R2[HI], -1.0, None, ALU.mult))
                B4 = bb[:, u].rearrange("p h (b c) -> p h b c", c=TB)
                T4 = bt.rearrange("p h (b c) -> p h b c", c=TB)

                def outer(small, big):
                    return bc(small.unsqueeze(2), 2, TB), bc(big.unsqueeze(3), 3, TB)

                x, y = outer(R1, d1[:, u])
                s.put(v.tensor_tensor(B4, x, y, ALU.mult))
                x, y = outer(I1, d2[:, u])
                s.link(v.tensor_tensor(T4, x, y, ALU.mult))
                v.tensor_tensor(bb[:, u], bb[:, u], bt, ALU.add).then_inc(uw, 1)
                U4 = u1[:, u].rearrange("p h (i c) -> p h i c", c=NB)
                v.tensor_tensor(U4, bc(wre[:, hh, :].unsqueeze(2), 2, TI), bc(a1[:, u].unsqueeze(3), 3, NB), ALU.mult).then_inc(uw, 1)
            assert s.n == PER

        looped(v, NHC // 2, pair)

    def gpsimd(g):
        g.wait_ge(phase, 1)
        for n, h in enumerate(hs):
            k24 = bc(kt.unsqueeze(1), 1, H2)
            g.tensor_tensor(kl[:, h, :], k24, bc(flo[:, h].unsqueeze(2), 2, NK), ALU.mult).then_inc(lin, 1)
            g.tensor_tensor(ke[:, h, :], k24, bc(dre[:, h].unsqueeze(2), 2, NK), ALU.mult).then_inc(lin, 1)
        for n, h in enumerate(hs):
            g.wait_ge(expd, n + 1)
            for j, t in enumerate((re, im)):
                g.wait_ge(sines, 2 * n + j + 1)
                g.tensor_tensor(t[:, h, :], t[:, h, :], ke[:, h, :], ALU.mult).then_inc(scaled, 1)
        g.wait_ge(w_in, 64)

        def pair(i):
            for u in range(2):
                k = 2 * i + u
                hh = bass.ds(k * HC, HC)
                g.wait_ge(ab, k + 1)
                if not is_first(i):
                    g.wait_ge(prod, 2 * (k - 1))
                U4 = u2[:, u].rearrange("p h (i c) -> p h i c", c=NB)
                g.tensor_tensor(U4, bc(wim[:, hh, :].unsqueeze(2), 2, TI), bc(a2[:, u].unsqueeze(3), 3, NB), ALU.mult).then_inc(u2r, 1)

        looped(g, NHC // 2, pair)

    def scalar(s):
        for n, h in enumerate(hs):
            s.wait_ge(lin, 2 * n + 2)
            s.activation(ke[:, h, :], ke[:, h, :], ACT.Exp).then_inc(expd, 1)
        for j in (3, 4):
            t = sm[4] if j == 3 else sm[3]
            s.wait_ge(sm_in, j - 2)
            s.activation(t, t, ACT.Sin, scale=-TWO_PI).then_inc(sm_out, 1)
        for n, h in enumerate(hs):
            for j, t in enumerate((re, im)):
                s.wait_ge(arg, 2 * n + j + 1)
                s.activation(t[:, h, :], t[:, h, :], ACT.Sin, scale=-TWO_PI).then_inc(sines, 1)

        def pair(i):
            for u in range(2):
                k = 2 * i + u
                if not is_first(i):
                    s.wait_ge(stored[u], 16 * TI * i)
                for b in range(2):
                    s.wait_ge(prod, 2 * k + b + 1)
                    s.activation(ob[:, u, b * QC:(b + 1) * QC], ps[:, 2 * u + b, :], ACT.Copy).then_inc(evac, 1)

        looped(s, NHC // 2, pair)

    def tensor(t):
        def pair(i):
            for u in range(2):
                k = 2 * i + u
                t.wait_ge(uw, 2 * k + 2)
                t.wait_ge(u2r, k + 1)
                for b in range(2):
                    if not is_first(i):
                        t.wait_ge(evac, 2 * (k - 2) + b + 1)
                    for h in range(8):
                        hh = 8 * b + h
                        o = ps[:, 2 * u + b, h * TJ:(h + 1) * TJ]
                        t.matmul(o, u1[:, u, hh, :], bb[:, u, hh, :], start=True, stop=False)
                        mm = t.matmul(o, u2[:, u, hh, :], bb[:, u, hh, :], start=False, stop=True)
                    mm.then_inc(prod, 1)

        looped(t, NHC // 2, pair)

    return sync, vector, gpsimd, scalar, tensor, all_stored


def tile_rows(t):
    return NB if isinstance(t, int) and t == T - 1 else P


def over_tiles(eng, body):
    def pair(i):
        for u in range(2):
            body(2 * i + u, u)

    looped(eng, NB // 2, pair)
    body(T - 1, 0)


def each_tile(body):
    for t in range(T):
        body(t, t % 2)


def early(t):
    return isinstance(t, int) and t < 2


class Norm:

    def __init__(self, arena, chain_sem):
        self.stats = arena.take(T, 6)
        self.mv = arena.take(T, 2)
        self.rstd = arena.take(T)
        self.half = arena.take(T, 2)
        self.sem = chain_sem
        self.count = 0

    def chain(self, v):
        return Chain(v, self.sem, self.count)

    def closed(self, c):
        self.count += c.n

    def take_stats(self, v, x, t):
        r = tile_rows(t)
        v.bn_stats(self.stats[0:r, t, :], x[0:r, t, :]).then_inc(self.sem, 1)

    def clear(self, v):
        c = self.chain(v)
        c.link(v.memset(self.mv, 1.0))
        self.closed(c)

    def solve(self, v, eps=LN_EPS):
        c = self.chain(v)
        c.n += T
        c.wait()
        for t in range(T):
            r = tile_rows(t)
            c.put(v.bn_aggr(self.mv[0:r, t, :], self.stats[0:r, t, :]))
        c.wait()
        self.newton(v, c, self.mv[:, :, 1], 1.0, eps)
        self.closed(c)

    def newton(self, v, c, var, scale, eps):
        y, a, b = self.rstd, self.half[:, :, 0], self.half[:, :, 1]
        c.link(v.tensor_scalar(b, var, scale, eps, ALU.mult, ALU.add))
        c.link(v.tensor_copy(a, b))
        c.link(v.tensor_scalar(y.bitcast(I32), a.bitcast(I32), 1, None, ALU.arith_shift_right))
        c.link(v.tensor_scalar(y.bitcast(I32), y.bitcast(I32), -1.0, float(0x5F3759DF), ALU.mult, ALU.add))
        for _ in range(4):
            c.link(v.tensor_tensor(a, y, y, ALU.mult))
            c.link(v.scalar_tensor_tensor(out=a, in0=a, scalar=-0.5, in1=b, op0=ALU.mult, op1=ALU.mult))
            c.link(v.scalar_tensor_tensor(out=y, in0=a, scalar=1.5, in1=y, op0=ALU.add, op1=ALU.mult))

    def apply(self, v, out, x, t):
        r = tile_rows(t)
        return v.tensor_scalar(out[0:r, t, :], x[0:r, t, :], self.mv[0:r, t, 0:1], self.rstd[0:r, bass.ds(t, 1)],
                               ALU.subtract, ALU.mult)


def turn_tile(t_eng, ps_bank, xn, t, ident):
    r = tile_rows(t)
    for k in range(KD):
        ins = t_eng.transpose(ps_bank[:, k * r:(k + 1) * r], xn[0:r, t, k * P:(k + 1) * P], ident[0:r, 0:r])
    return ins


def turned_out(s_eng, ps_bank, xnT, t):
    r = tile_rows(t)
    dst = xnT[:, :, NCOL:NTOK] if r == NB else xnT[:, :, bass.ds(t * P, P)]
    return s_eng.activation(dst, ps_bank[:, 0:KD * r].rearrange("p (k n) -> p k n", k=KD), ACT.Copy)


def scan_layer(nc, sem, sb, ps, d, h0, tok_stored, g, at):
    a = Arena(sb, at)
    hb, xn, xnT, yb, ident, norm = g.h, g.xn, g.xnT, g.y, g.ident, g.norm
    win = a.take(KD, P)
    wd, wg = a.take(P), a.take(P)
    wout, gam, bet = a.take(D), a.take(D), a.take(D)
    zb, db, gb, hs = (a.take(NB, SEQ) for _ in range(4))
    tmp = a.take(2, D)
    F = (lambda x: x.rearrange("p b s -> p (b s)"))
    zf, df, gf, hf = F(zb), F(db), F(gb), F(hs)
    NC, CW = 6, NTOK // 6
    HALF = P // 2

    h_in = [sem(f"h_loaded{q}") for q in range(NQ + 1)]
    wz, w_in, w_fb = sem("scan_zeroed"), sem("scan_weights_loaded"), sem("scan_block_weights_loaded")
    xr, turned, tev = sem("scan_xn_ready"), sem("scan_turned"), sem("scan_xnT_ready")
    zp, zr = sem("scan_z_products"), sem("scan_z_ready")
    op, dr, gr = sem("scan_gate_products"), sem("scan_delta_ready"), sem("scan_gate_ready")
    rst, sc = sem("scan_resets"), sem("scan_states")
    outp, yr = sem("scan_out_products"), sem("scan_y_ready")
    hbr, hr, tch = sem("scan_h_plus_beta"), g.h_ready, sem("scan_vector_chain")

    def sync(sp):
        tok_stored(sp)
        for q in range(NQ):
            sp.dma_start(hb[:, 4 * q:4 * q + 4, :], h0[4 * q:4 * q + 4].rearrange("b p d -> p b d")).then_inc(h_in[q], 16)
        sp.dma_start(hb[0:NB, NB, :], d["cls"]).then_inc(h_in[NQ], 16)
        sp.dma_start(ident, d["ident"]).then_inc(w_in, 16)
        for k in range(2):
            sp.dma_start(win[:, :, k * HALF:(k + 1) * HALF], d["W_in"].rearrange("(k p) n -> p k n", p=P)).then_inc(w_in, 16)
        sp.wait_ge(wz, 2)
        for k, w in enumerate((d["W_fwd"], d["W_bwd"])):
            s = slice(k * HALF, (k + 1) * HALF)
            sp.dma_start(wd[s, s], w[:, 0:HALF]).then_inc(w_fb, 16)
            sp.dma_start(wg[s, s], w[:, HALF:P]).then_inc(w_fb, 16)
        sp.dma_start(wout, d["W_out"]).then_inc(w_fb, 16)
        sp.dma_start(gam, d["gamma"].partition_broadcast(P)).then_inc(w_fb, 16)
        sp.dma_start(bet, d["beta"].partition_broadcast(P)).then_inc(w_fb, 16)

    def vector(v):
        v.wait_ge(h_in[0], 16)
        norm.clear(v)
        for q in range(NQ):
            v.wait_ge(h_in[q], 16)
            for t in range(4 * q, 4 * q + 4):
                norm.take_stats(v, hb, t)
        v.wait_ge(h_in[NQ], 16)
        norm.take_stats(v, hb, NB)
        norm.solve(v)
        over_tiles(v, lambda t, u: norm.apply(v, xn, hb, t).then_inc(xr, 1))

        def gates(c):
            v.wait_ge(op, c + 1)
            cols = bass.ds(c * CW, CW)
            b = 6
            v.tensor_tensor(gf[:, cols], ps[:, b, 0:CW], zf[:, cols], ALU.mult).then_inc(gr, 1)

        looped(v, NC, gates)
        v.wait_ge(gr, NC)
        v.wait_ge(rst, 2)
        v.tensor_tensor_scan(hf[0:HALF, :], df[0:HALF, :], gf[0:HALF, :], 0.0, ALU.mult, ALU.add).then_inc(sc, 1)
        v.tensor_tensor_scan(hf[HALF:P, ::-1], df[HALF:P, ::-1], gf[HALF:P, ::-1], 0.0, ALU.mult, ALU.add).then_inc(sc, 1)

        v.wait_ge(xr, T)

        def add(t, u):
            r = tile_rows(t)
            v.wait_ge(outp, t + 1)
            v.tensor_tensor(yb[0:r, t, :], ps[0:r, 2 + u, :], xn[0:r, t, :], ALU.add).then_inc(yr, 1)
            v.wait_ge(yr, t + 1)
            norm.take_stats(v, yb, t)

        over_tiles(v, add)
        norm.solve(v)
        v.wait_ge(hbr, 2)

        def post(t, u):
            r = tile_rows(t)
            v.scalar_tensor_tensor(out=tmp[0:r, u], in0=yb[0:r, t, :], scalar=norm.mv[0:r, t, 0:1], in1=gam[0:r], op0=ALU.subtract, op1=ALU.mult).then_inc(tch, 1)
            v.wait_ge(tch, t + 1)
            v.scalar_tensor_tensor(out=hb[0:r, t, :], in0=tmp[0:r, u], scalar=norm.rstd[0:r, bass.ds(t, 1)], in1=hb[0:r, t, :], op0=ALU.mult, op1=ALU.add).then_inc(hr, 1)
            v.wait_ge(hr, t + 1)
            norm.take_stats(v, hb, t)

        over_tiles(v, post)

    def gpsimd(p):
        p.wait_ge(h_in[0], 16)
        p.memset(wd, 0.0).then_inc(wz, 1)
        p.memset(wg, 0.0).then_inc(wz, 1)
        p.wait_ge(dr, NC)
        p.memset(db[0:HALF, :, 0], 0.0).then_inc(rst, 1)
        p.memset(db[HALF:P, :, SEQ - 1], 0.0).then_inc(rst, 1)
        p.wait_ge(rst, 2)
        p.wait_ge(w_fb, 16 * 7)
        p.wait_ge(xr, T)
        p.tensor_tensor(hb[:, 0:NB, :], hb[:, 0:NB, :], bc(bet.unsqueeze(1), 1, NB), ALU.add).then_inc(hbr, 1)
        p.wait_ge(hbr, 1)
        p.tensor_tensor(hb[0:NB, NB, :], hb[0:NB, NB, :], bet[0:NB], ALU.add).then_inc(hbr, 1)

    def scalar(s):
        def quarter(q):
            for j in range(4):
                s.wait_ge(turned, 4 * q + j + 1)
                turned_out(s, ps[:, j % 2, :], xnT, 4 * q + j).then_inc(tev, 1)
            s.wait_ge(zp, q + 1)
            s.activation(zb[:, bass.ds(4 * q, 4), 1:SEQ], ps[:, 2, :].rearrange("p (b n) -> p b n", b=4), ACT.Copy).then_inc(zr, 1)

        looped(s, NQ, quarter)
        s.wait_ge(turned, T)
        turned_out(s, ps[:, 0, :], xnT, NB).then_inc(tev, 1)
        s.wait_ge(zp, NQ + 1)
        s.activation(zb[:, :, 0], ps[:, 3, 0:NB], ACT.Copy).then_inc(zr, 1)

        def deltas(c):
            s.wait_ge(op, c + 1)
            s.activation(df[:, bass.ds(c * CW, CW)], ps[:, 4, 0:CW], ACT.Sigmoid).then_inc(dr, 1)

        looped(s, NC, deltas)

    def tensor(t):
        t.wait_ge(w_in, 3 * 16)

        def quarter(q):
            for j in range(4):
                n = 4 * q + j
                t.wait_ge(xr, n + 1)
                if not (is_first(q) and j < 2):
                    t.wait_ge(tev, n - 1)
                turn_tile(t, ps[:, j % 2, :], xn, n, ident).then_inc(turned, 1)
            t.wait_ge(tev, 4 * q + 4)
            if not is_first(q):
                t.wait_ge(zr, q)
            for k in range(KD):
                mm = t.matmul(ps[:, 2, :], win[:, k, :], xnT[:, k, bass.ds(q * QC, QC)], start=(k == 0), stop=(k == KD - 1))
            mm.then_inc(zp, 1)

        for q in range(NQ):
            quarter(q)
        t.wait_ge(xr, T)
        turn_tile(t, ps[:, 0, :], xn, NB, ident).then_inc(turned, 1)
        t.wait_ge(tev, T)
        for k in range(KD):
            mm = t.matmul(ps[:, 3, 0:NB], win[:, k, :], xnT[:, k, NCOL:NTOK], start=(k == 0), stop=(k == KD - 1))
        mm.then_inc(zp, 1)
        t.wait_ge(zr, NQ + 1)
        t.wait_ge(w_fb, 16 * 7)

        def gates(c):
            if not is_first(c):
                t.wait_ge(dr, c)
                t.wait_ge(gr, c)
            cols = bass.ds(c * CW, CW)
            t.matmul(ps[:, 4, 0:CW], wd, zf[:, cols], start=True, stop=True)
            t.matmul(ps[:, 6, 0:CW], wg, zf[:, cols], start=True, stop=True).then_inc(op, 1)

        looped(t, NC, gates)
        t.wait_ge(sc, 2)

        def outs(n, u):
            if not early(n):
                t.wait_ge(yr, n - 1)
            r = tile_rows(n)
            lhs = hs[:, :, 0] if r == NB else hs[:, n, 1:SEQ]
            t.matmul(ps[0:r, 2 + u, :], lhs, wout, start=True, stop=True).then_inc(outp, 1)

        each_tile(outs)

    return sync, vector, gpsimd, scalar, tensor


NE = 8
NTILE = (2 * NTOK + NE * (P - 1)) // P
NSLOT = NTILE * P


def ffn_layer(nc, sem, sb, ps, d, dram, g, name, F, NSH, stats_after, before):
    hb, xn, xnT, ident, norm = g.h, g.xn, g.xnT, g.ident, g.norm
    NF = -(-F // P)
    FR = [min(P, F - P * f) for f in range(NF)]
    NU = NQ + 1
    GW, DW = KD * 2 * F, NF * D
    EW = GW + DW
    ex = sb[:, g.xn_at:g.xn_at + NE * EW].rearrange("p (e w) -> p e w", e=NE)
    exg, exd = (lambda e, k, j, w: ex[:, e, k * 2 * F + j:k * 2 * F + j + w]), (lambda e, f, r: ex[0:r, e, GW + f * D:GW + (f + 1) * D])
    w = Arena(sb, g.scratch_at)
    wgu, wdn = w.take(2, KD, 2 * F), w.take(2, NF, D)
    a = Arena(sb, max(w.at, g.xn_at + NE * EW))
    hid_at = a.at
    hid, sil = a.take(2, NF, QC), a.take(2, QC)
    b = Arena(sb, hid_at)
    xgT, esil, ehid, ehT = b.take(2, KD, P), b.take(2, F), b.take(2, F), b.take(2, NF, P)
    assert b.at <= a.at
    ey = a.take(2, D)
    xg = a.take(2, D)
    wr = a.take(KD, NE + 1)
    lg, oh0, oh1, t8, mm8 = (a.take(T, NE) for _ in range(5))
    sg, m1, m2, wt = a.take(T), a.take(T), a.take(T), a.take(2, T)
    iota, iot, valid = a.take(NE), a.take(NTILE), a.take(T)
    tri, ones = xg[:, 0, 0:P], xg[:, 0, P:2 * P]
    mt, cnt, base, incl, one8 = (a.take(NE) for _ in range(5))
    cni = a.take(NE, dt=I32)
    slot_u, pos_u, tmp_u = a.take(2, T, dt=U32), a.take(2, T, dt=U32), a.take(T, dt=U32)
    tok_u, idx_u, zero_u = a.take(T, dt=U32), a.take(NTILE, dt=U32), a.take(NTILE, dt=U32)
    cmp = sb[:, hid_at:hid_at + NTILE * NE].rearrange("p (t e) -> p t e", e=NE)
    etab = a.take(NTILE)
    eti = a.take(NTILE, dt=I32)
    assert a.at <= g.top_at, (a.at, g.top_at)
    xd, slots, yd = dram["xn"], dram["slots"], dram["expert_out"]

    xr, turned, tev = sem(name + "_xn_ready"), sem(name + "_turned"), sem(name + "_xnT_ready")
    r_in, rp, rch, sgm = sem(name + "_router_loaded"), sem(name + "_scores"), sem(name + "_router_chain"), sem(name + "_sigmoids")
    need_s = sem(name + "_differences")
    w_in = [sem(f"{name}_weights_loaded{u}") for u in range(2)]
    gu, silr, hidr = sem(name + "_gate_up"), sem(name + "_silu"), sem(name + "_hidden")
    dn, acc = sem(name + "_down"), sem(name + "_added")
    WD = 1 + (1 if FR[-1] == P else 2)
    cntm, rankm = sem(name + "_choices_ready"), sem(name + "_ranks")
    zs, xs, rt, scat, ix = sem(name + "_slots_cleared"), sem(name + "_xn_stored"), sem(name + "_routed"), sem(name + "_slots_filled"), sem(name + "_slots_loaded")
    e_in = [sem(f"{name}_experts_loaded{k}") for k in range(2)]
    g_in = [sem(f"{name}_rows_gathered{u}") for u in range(2)]
    tx, txr = sem(name + "_rows_turned"), sem(name + "_rowsT_ready")
    eg, esr, ehr = sem(name + "_e_gate_up"), sem(name + "_e_silu"), sem(name + "_e_hidden")
    th, thr = sem(name + "_e_hidden_turned"), sem(name + "_e_hiddenT_ready")
    ed, eyr = sem(name + "_e_down"), sem(name + "_e_out_ready")
    yst = [sem(f"{name}_e_out_stored{u}") for u in range(2)]
    cg = [sem(f"{name}_out_gathered{u}") for u in range(2)]
    cadd = sem(name + "_combined")

    def load_block(sp, name2, dst_g, dst_d, b, s):
        sp.dma_start(dst_g, d[name2 + "_gate_up"][b].rearrange("p k f -> p (k f)")).then_inc(s, 16)
        full = NF if FR[-1] == P else NF - 1
        sp.dma_start(dst_d(slice(0, P), 0, full), d[name2 + "_down"][b, 0:full * P, :].rearrange("(f p) n -> p f n", p=P)).then_inc(s, 16)
        if full < NF:
            sp.dma_start(dst_d(slice(0, FR[-1]), full, NF), d[name2 + "_down"][b, full * P:F, :].unsqueeze(1)).then_inc(s, 16)

    def load_expert(sp, e, s):
        load_block(sp, name, ex[:, e, 0:GW], lambda r, f0, f1: ex[r, e, GW + f0 * D:GW + f1 * D].rearrange("p (f n) -> p f n", n=D), e, s)

    def sync(sp):
        before(sp)
        sp.dma_start(wr, d[name + "_router"]).then_inc(r_in, 16)
        for dst, src in ((iota, d["iota8"]), (iot, d["iota_tiles"])):
            sp.dma_start(dst, src.partition_broadcast(P)).then_inc(r_in, 16)
        for dst, src in ((valid, d["valid"]), (tri, d["before"]), (ones, d["ones"])):
            sp.dma_start(dst, src).then_inc(r_in, 16)
        sp.dma_start(tok_u, d["token_ids"].bitcast(U32)).then_inc(r_in, 16)
        def shared(b, u):
            load_block(sp, name + "_sh", wgu[:, u].rearrange("p k f -> p (k f)"), lambda r, f0, f1: wdn[r, u, f0:f1, :], b, w_in[u])

        for u in range(2):
            shared(u, u)
        sp.wait_ge(zs, 1)
        sp.dma_start(slots.rearrange("(p t) o -> p (t o)", t=NTILE), zero_u).then_inc(zs, 16)
        sp.wait_ge(xr, T)
        sp.dma_start(xd[0:NCOL, :].rearrange("(t p) n -> p t n", p=P), xn[:, 0:NB, :]).then_inc(xs, 16)
        sp.dma_start(xd[NCOL:NTOK, :], xn[0:NB, NB, :]).then_inc(xs, 16)
        sp.wait_ge(xs, 32)
        sp.wait_ge(tev, T)
        for e in range(4):
            load_expert(sp, e, e_in[0])
        for b in range(2, NSH):
            sp.wait_ge(dn, (b - 1) * T)
            shared(b, b % 2)
        sp.wait_ge(scat, 2 * T * 16)
        sp.dma_start(idx_u, slots.rearrange("(p t) o -> p (t o)", t=NTILE)).then_inc(ix, 16)
        sp.wait_ge(dn, NSH * T)
        for e in range(4, NE):
            load_expert(sp, e, e_in[1])

        def store(i):
            for u in range(2):
                t = 2 * i + u
                sp.wait_ge(eyr, t + 1)
                sp.dma_start(yd[bass.ds(t * P, P), :], ey[:, u]).then_inc(yst[u], 16)

        looped(sp, NTILE // 2, store)

    def order():
        steps = [("gu", 0)]
        for m in range(1, NU):
            steps += [("gu", m), ("dn", m - 1)]
        return steps + [("dn", NU - 1)]

    def unit_cols(m):
        return (slice(NCOL, NTOK), NB) if m == 0 else (slice((m - 1) * QC, m * QC), QC)

    def unit_tiles(m):
        return [NB] if m == 0 else list(range(4 * (m - 1), 4 * m))

    def sums_before(tile, u, first):
        r = 0 if tile == NB else tile + 1
        at0 = u * T
        if r == 0:
            n = at0 - 3
        elif r <= 4:
            n = at0 + 1 if r == 1 else at0 - 4 + r
        else:
            n = at0 + r - 3
        return None if first and n <= 0 else n

    def downs_through(k):
        if k < 0:
            return 0 if k == -1 else -len(unit_tiles(NU - 1))
        return sum(len(unit_tiles(j % NU)) for j in range(k + 1))

    def vector(v):
        norm.solve(v)
        over_tiles(v, lambda t, u: norm.apply(v, xn, hb, t).then_inc(xr, 1))
        c = Chain(v, rch)
        c.link(v.memset(lg, 0.0))
        c.put(v.memset(sg, 0.0))
        v.memset(zero_u, 0).then_inc(zs, 1)
        v.wait_ge(rp, T)
        s3 = ps[:, 2, 0:T * 16].rearrange("p (t e) -> p t e", e=16)
        c.put(v.tensor_copy(lg[:, 0:NB, :], s3[:, 0:NB, 0:NE]))
        c.put(v.tensor_copy(lg[0:NB, NB, :], s3[0:NB, NB, 0:NE]))
        c.wait()
        c.put(v.tensor_copy(sg[:, 0:NB], s3[:, 0:NB, NE]))
        c.link(v.tensor_copy(sg[0:NB, NB:T], s3[0:NB, NB, NE:NE + 1]))
        v.wait_ge(r_in, 7 * 16)
        io = bc(iota.unsqueeze(1), 1, T)
        wide = (lambda x: bc(x.unsqueeze(2), 2, NE))
        for m, oh in ((m1, oh0), (m2, oh1)):
            c.link(v.tensor_reduce(m, lg, AX.X, ALU.max))
            c.link(v.tensor_tensor(t8, lg, wide(m), ALU.is_ge))
            c.link(v.scalar_tensor_tensor(out=t8, in0=t8, scalar=-16.0, in1=io, op0=ALU.mult, op1=ALU.add))
            c.link(v.tensor_reduce(wt[:, 0, :], t8, AX.X, ALU.min))
            c.link(v.tensor_tensor(oh, t8, wide(wt[:, 0, :]), ALU.is_equal))
            c.link(v.scalar_tensor_tensor(out=lg, in0=oh, scalar=-3.0e38, in1=lg, op0=ALU.mult, op1=ALU.add))
        c.link(v.tensor_tensor(wt[:, 0, :], m1, m2, ALU.subtract))
        v.tensor_tensor(wt[:, 1, :], m2, m1, ALU.subtract).then_inc(need_s, 1)
        for oh in (oh0, oh1):
            c.put(v.tensor_tensor(oh, oh, wide(valid), ALU.mult))
        c.wait()
        c.link(v.tensor_tensor(mm8, oh0, oh1, ALU.add))
        v.tensor_reduce(mt, mm8.rearrange("p t e -> p e t"), AX.X, ALU.add).then_inc(cntm, 1)
        c.put(v.memset(one8, 1.0))
        c.wait()
        v.wait_ge(rankm, 2)
        c.link(v.tensor_scalar(cni, ps[:, 3, 256:256 + NE], float(P - 1), None, ALU.add))
        c.link(v.tensor_scalar(cni, cni, 7, None, ALU.arith_shift_right))
        c.link(v.tensor_copy(cnt, cni))
        c.link(v.tensor_tensor_scan(incl, one8, cnt, 0.0, ALU.mult, ALU.add))
        c.link(v.tensor_tensor(base, incl, cnt, ALU.subtract))
        c.link(v.tensor_scalar(base, base, float(P), None, ALU.mult))
        c.link(v.tensor_tensor(mm8, ps[:, 3, 0:T * NE].rearrange("p (t e) -> p t e", e=NE), bc(base.unsqueeze(1), 1, T), ALU.add))
        for j, oh in enumerate((oh0, oh1)):
            c.link(v.tensor_tensor(t8, oh, mm8, ALU.mult))
            c.link(v.tensor_reduce(m1, t8, AX.X, ALU.add))
            c.link(v.tensor_copy(slot_u[:, j], m1))
            c.link(v.tensor_scalar(tmp_u, slot_u[:, j], P - 1, None, ALU.bitwise_and))
            c.link(v.tensor_scalar(pos_u[:, j], slot_u[:, j], 7, None, ALU.logical_shift_right))
            c.link(v.scalar_tensor_tensor(out=pos_u[:, j], in0=tmp_u, scalar=float(NTILE), in1=pos_u[:, j], op0=ALU.mult, op1=ALU.add))
        c.link(v.tensor_tensor(cmp, bc(iot.unsqueeze(2), 2, NE), bc(incl.unsqueeze(1), 1, NTILE), ALU.is_ge))
        c.link(v.tensor_reduce(etab, cmp, AX.X, ALU.add))
        v.tensor_scalar(eti, etab, float(NE - 1), None, ALU.min).then_inc(rt, 1)
        v.wait_ge(sgm, 2)

        def pair(i):
            n = 0
            r = 0
            for u in range(2):
                b = 2 * i + u
                for what, m in order():
                    if what == "gu":
                        cols, w = unit_cols(m)
                        for f in range(NF):
                            v.wait_ge(silr, i * (2 * NU * NF) + n + 1)
                            slot = (u * NU + m) % 2
                            if f == 0 and not (is_first(i) and u == 0 and m < 2):
                                v.wait_ge(dn, i * 2 * T + downs_through(u * NU + m - 2))
                            v.tensor_tensor(hid[0:FR[f], slot, f, 0:w], sil[0:FR[f], n % 2, 0:w],
                                            ps[0:FR[f], 2 * (n % 2) + 1, 0:w], ALU.mult).then_inc(hidr, 1)
                            n += 1
                    else:
                        for t in unit_tiles(m):
                            rows = tile_rows(t)
                            v.wait_ge(dn, i * 2 * T + r + 1)
                            if not (is_first(i) and u == 0):
                                v.wait_ge(acc, i * 2 * T + r - T + 1)
                            bank = 4 if t == NB else 4 + t % 4
                            v.scalar_tensor_tensor(out=hb[0:rows, t, :], in0=ps[0:rows, bank, :], scalar=sg[0:rows, t:t + 1],
                                                   in1=hb[0:rows, t, :], op0=ALU.mult, op1=ALU.add).then_inc(acc, 1)
                            r += 1

        looped(v, NSH // 2, pair)

        def hidden(t, u):
            v.wait_ge(esr, t + 1)
            if not early(t):
                v.wait_ge(th, t - 1)
            v.tensor_tensor(ehid[:, u], esil[:, u], e_up(u), ALU.mult).then_inc(ehr, 1)

        def out_rows(t, u):
            v.wait_ge(ed, t + 1)
            if not early(t):
                v.wait_ge(yst[u], 16 * halves(t))
            v.tensor_copy(ey[:, u], ps[:, 6 + u, :]).then_inc(eyr, 1)

        def hidden_turned(t, u):
            v.wait_ge(th, t + 1)
            if not early(t):
                v.wait_ge(ed, t - 1)
            for f in range(NF):
                ins = v.tensor_copy(ehT[0:FR[f], u, f, :], ps[0:FR[f], 5, f * P:(f + 1) * P])
            ins.then_inc(thr, 1)

        hidden(0, 0)
        hidden_turned(0, 0)
        tiles_1_on(v, lambda t, u: (hidden(t, u), out_rows(t - 1, 1 - u), hidden_turned(t, u)))
        hidden(NTILE - 1, 1)
        out_rows(NTILE - 2, 0)
        hidden_turned(NTILE - 1, 1)
        out_rows(NTILE - 1, 1)

        v.wait_ge(acc, T * NSH)

        def combine(t, u):
            r = tile_rows(t)
            v.wait_ge(cg[u], 32 * (halves(t) + 1))
            v.scalar_tensor_tensor(out=hb[0:r, t, :], in0=cy[0:r, u, 0], scalar=wt[0:r, 0, bass.ds(t, 1)], in1=hb[0:r, t, :], op0=ALU.mult, op1=ALU.add).then_inc(cadd, 1)
            v.wait_ge(cadd, 2 * t + 1)
            v.scalar_tensor_tensor(out=hb[0:r, t, :], in0=cy[0:r, u, 1], scalar=wt[0:r, 1, bass.ds(t, 1)], in1=hb[0:r, t, :], op0=ALU.mult, op1=ALU.add).then_inc(cadd, 1)
            if stats_after:
                v.wait_ge(cadd, 2 * t + 2)
                norm.take_stats(v, hb, t)

        over_tiles(v, combine)

    def halves(t):
        return t // 2

    cy = sb[:, hid_at:hid_at + 4 * D].rearrange("p (u j n) -> p u j n", u=2, j=2)

    def e_up(u):
        return ps[:, u, F:2 * F] if 2 * F <= QC else ps[:, 2 * u + 1, 0:F]

    def e_gate(u):
        return ps[:, u, 0:F] if 2 * F <= QC else ps[:, 2 * u, 0:F]

    def tiles_1_on(eng, body):
        def pair(i):
            for u in range(2):
                body(2 * i + 1 + u, 1 - u)

        looped(eng, NTILE // 2 - 1, pair)

    def gpsimd(p):
        p.wait_ge(rt, 1)
        p.wait_ge(zs, 17)

        def scatter(t, u):
            r = tile_rows(t)
            for j in range(2):
                p.indirect_dma_start(out=slots, out_offset=bass.IndirectOffsetOnAxis(ap=pos_u[0:r, j, t:t + 1], axis=0),
                                     in_=tok_u[0:r, t:t + 1], in_offset=None).then_inc(scat, 16)

        each_tile(scatter)
        p.wait_ge(xs, 32)
        p.wait_ge(ix, 16)
        p.wait_ge(rankm, 2)

        for t in range(NTILE):
            if t >= 2:
                p.wait_ge(tx, t - 1)
            p.indirect_dma_start(out=xg[:, t % 2], out_offset=None, in_=xd,
                                 in_offset=bass.IndirectOffsetOnAxis(ap=idx_u[:, t:t + 1], axis=0)).then_inc(g_in[t % 2], 16)
        for u in range(2):
            p.wait_ge(yst[u], 16 * (NTILE // 2))
        p.wait_ge(ed, NTILE)

        def fetch(t, u):
            r = tile_rows(t)
            if not early(t):
                p.wait_ge(cadd, 2 * t - 2)
            for j in range(2):
                p.indirect_dma_start(out=cy[0:r, u, j], out_offset=None, in_=yd,
                                     in_offset=bass.IndirectOffsetOnAxis(ap=slot_u[0:r, j, t:t + 1], axis=0)).then_inc(cg[u], 16)

        each_tile(fetch)

    def scalar(s):
        def turn(t, u):
            s.wait_ge(turned, t + 1)
            turned_out(s, ps[:, u, :], xnT, t).then_inc(tev, 1)

        over_tiles(s, turn)
        s.wait_ge(need_s, 1)
        s.activation(wt, wt, ACT.Sigmoid).then_inc(sgm, 1)
        s.activation(sg, sg, ACT.Sigmoid).then_inc(sgm, 1)

        def pair(i):
            n = 0
            for u in range(2):
                for m in range(NU):
                    cols, w = unit_cols(m)
                    for f in range(NF):
                        s.wait_ge(gu, i * (2 * NU * NF) + n + 1)
                        if not (is_first(i) and n < 2):
                            s.wait_ge(hidr, i * (2 * NU * NF) + n - 1)
                        s.activation(sil[0:FR[f], n % 2, 0:w], ps[0:FR[f], 2 * (n % 2), 0:w], ACT.Silu).then_inc(silr, 1)
                        n += 1

        looped(s, NSH // 2, pair)

        def rows_turned(t, u):
            s.wait_ge(tx, t + 1)
            if not early(t):
                s.wait_ge(eg, t - 1)
            s.activation(xgT[:, u].rearrange("p k n -> p (k n)"), ps[:, 4, :], ACT.Copy).then_inc(txr, 1)

        def silu(t, u):
            s.wait_ge(eg, t + 1)
            if not early(t):
                s.wait_ge(ehr, t - 1)
            s.activation(esil[:, u], e_gate(u), ACT.Silu).then_inc(esr, 1)

        rows_turned(0, 0)
        silu(0, 0)
        rows_turned(1, 1)
        tiles_1_on(s, lambda t, u: (silu(t, u), rows_turned(t + 1, 1 - u)))
        silu(NTILE - 1, 1)

    def tensor(t):
        def turn(n, u):
            t.wait_ge(xr, n + 1)
            if n >= 2:
                t.wait_ge(tev, n - 1)
            turn_tile(t, ps[:, u, :], xn, n, ident).then_inc(turned, 1)

        each_tile(turn)
        t.wait_ge(tev, T)
        t.wait_ge(r_in, 7 * 16)

        def score(n, u):
            r = tile_rows(n)
            cols = slice(NCOL, NTOK) if r == NB else slice(n * P, (n + 1) * P)
            for k in range(KD):
                mm = t.matmul(ps[0:r, 2, 16 * n:16 * n + NE + 1], xnT[:, k, cols], wr[:, k, :], start=(k == 0), stop=(k == KD - 1))
            mm.then_inc(rp, 1)

        each_tile(score)
        t.wait_ge(cntm, 1)
        t.matmul(ps[:, 3, 256:256 + NE], ones, mt, start=True, stop=True).then_inc(rankm, 1)
        flat = mm8.rearrange("p t e -> p (t e)")
        t.matmul(ps[:, 3, 0:T * NE], tri, flat, start=True, stop=False)
        for n in range(1, T):
            mm = t.matmul(ps[:, 3, n * NE:T * NE], ones, flat[:, 0:(T - n) * NE], start=False, stop=(n == T - 1))
        mm.then_inc(rankm, 1)
        t.wait_ge(rt, 1)
        t.wait_ge(sgm, 2)

        def pair(i):
            n = 0
            for u in range(2):
                t.wait_ge(w_in[u], 16 * WD * (i + 1))
                for what, m in order():
                    slot = (u * NU + m) % 2
                    if what == "gu":
                        cols, w = unit_cols(m)
                        for f in range(NF):
                            if not (is_first(i) and n < 2):
                                t.wait_ge(hidr, i * (2 * NU * NF) + n - 1)
                            for j in range(2):
                                for k in range(KD):
                                    mm = t.matmul(ps[0:FR[f], 2 * (n % 2) + j, 0:w],
                                                  wgu[:, u, k, j * F + f * P:j * F + f * P + FR[f]], xnT[:, k, cols],
                                                  start=(k == 0), stop=(k == KD - 1))
                            mm.then_inc(gu, 1)
                            n += 1
                    else:
                        t.wait_ge(hidr, i * (2 * NU * NF) + (u * NU + m + 1) * NF)
                        for j, tile in enumerate(unit_tiles(m)):
                            rows = tile_rows(tile)
                            bank = 4 if tile == NB else 4 + tile % 4
                            before_n = sums_before(tile, u, is_first(i))
                            if before_n is not None:
                                t.wait_ge(acc, i * 2 * T + before_n)
                            for f in range(NF):
                                mm = t.matmul(ps[0:rows, bank, :], hid[0:FR[f], slot, f, j * P:j * P + rows], wdn[0:FR[f], u, f, :],
                                              start=(f == 0), stop=(f == NF - 1))
                            mm.then_inc(dn, 1)

        looped(t, NSH // 2, pair)

        def turn_rows(n, u):
            t.wait_ge(g_in[u], 16 * (halves(n) + 1))
            if not (isinstance(n, int) and n == 0):
                t.wait_ge(txr, n)
            for k in range(KD):
                ins = t.transpose(ps[:, 4, k * P:(k + 1) * P], xg[:, u, k * P:(k + 1) * P], ident)
            ins.then_inc(tx, 1)

        def gate_up(n, u):
            e = t.value_load(eti[0:1, bass.ds(n, 1)], min_val=0, max_val=NE - 1)
            t.wait_ge(txr, n + 1)
            if not early(n):
                t.wait_ge(ehr, n - 1)
            if 2 * F <= QC:
                for k in range(KD):
                    mm = t.matmul(ps[:, u, 0:2 * F], xgT[:, u, k], exg(e, k, 0, 2 * F), start=(k == 0), stop=(k == KD - 1))
            else:
                for j in range(2):
                    for k in range(KD):
                        mm = t.matmul(ps[:, 2 * u + j, 0:F], xgT[:, u, k], exg(e, k, j * F, F), start=(k == 0), stop=(k == KD - 1))
            mm.then_inc(eg, 1)

        def turn_hidden(n, u):
            t.wait_ge(ehr, n + 1)
            if not (isinstance(n, int) and n == 0):
                t.wait_ge(thr, n)
            for f in range(NF):
                ins = t.transpose(ps[0:FR[f], 5, f * P:(f + 1) * P], ehid[:, u, f * P:f * P + FR[f]], ident)
            ins.then_inc(th, 1)

        def down(n, u):
            e = t.value_load(eti[0:1, bass.ds(n, 1)], min_val=0, max_val=NE - 1)
            t.wait_ge(thr, n + 1)
            if not early(n):
                t.wait_ge(eyr, n - 1)
            for f in range(NF):
                mm = t.matmul(ps[:, 6 + u, :], ehT[0:FR[f], u, f, :], exd(e, f, FR[f]), start=(f == 0), stop=(f == NF - 1))
            mm.then_inc(ed, 1)

        t.wait_ge(acc, NSH * T)
        turn_rows(0, 0)
        for k in range(2):
            t.wait_ge(e_in[k], 16 * WD * 4)
        gate_up(0, 0)
        turn_rows(1, 1)
        turn_hidden(0, 0)

        def body(n, u):
            gate_up(n, u)
            turn_rows(n + 1, 1 - u)
            down(n - 1, 1 - u)
            turn_hidden(n, u)

        tiles_1_on(t, body)
        gate_up(NTILE - 1, 1)
        down(NTILE - 2, 0)
        turn_hidden(NTILE - 1, 1)
        down(NTILE - 1, 1)

    return sync, vector, gpsimd, scalar, tensor, cadd


def gla_layer(nc, sem, sb, ps, d, g, at, before):
    a = Arena(sb, at)
    hb, xn, xnT, ident, norm = g.h, g.xn, g.xnT, g.ident, g.norm
    KH, BL, NBL = 32, 32, 4
    wqk, wog, wig = a.take(KD, 2 * KH), a.take(KD, D), a.take(KD, D)
    gw, mask = a.take(D), a.take(P)
    ats, ots = a.take(2, P), a.take(2, KD, P)
    atc = a.take(NB, NH, rows=NB)
    sg, pb, junk = a.take(2, D), a.take(2, D), a.take(D)
    ss = a.take(T)
    qs, kb3, = (a.take(NB, SEQ, rows=KH) for _ in range(2))
    b = Arena(sb, g.y_at)
    kb0, kb1, kb2, pv = (b.take(NB, SEQ, rows=KH) for _ in range(4))
    av, bv = kb2, kb1
    sq = a.take(NB, SEQ, rows=KH)
    kb = [kb0, kb1, kb2, kb3]
    F = (lambda x: x.rearrange("p b s -> p (b s)"))

    w_in = sem("gla_weights_loaded")
    xr, turned, tev = sem("gla_xn_ready"), sem("gla_turned"), sem("gla_xnT_ready")
    qk, qsig, ksig, asig, qkr = sem("gla_qk_products"), sem("gla_q_sigmoid"), sem("gla_k_ready"), sem("gla_a_ready"), sem("gla_q_ready")
    kch, kbr, cp = sem("gla_decay_chain"), sem("gla_keys_scaled"), sem("gla_keys_copied")
    acp, atcr = sem("gla_cls_products"), sem("gla_cls_attention")
    ap, atr, ob, otr, ssr = sem("gla_attention_products"), sem("gla_attention_masked"), sem("gla_o_products"), sem("gla_oT_ready"), sem("gla_squares")
    gor, sgr, t1r, pr, gwr = sem("gla_gate_products"), sem("gla_gate_sigmoid"), sem("gla_gated"), sem("gla_gated_o"), sem("gla_weighted")
    hr = sem("gla_h_ready")
    zr = sem("gla_cleared")

    def sync(sp):
        before(sp)
        sp.dma_start(wqk, d["Wqk"]).then_inc(w_in, 16)
        sp.dma_start(wog, d["Wog"].rearrange("(k p) n -> p k n", p=P)).then_inc(w_in, 16)
        sp.dma_start(wig, d["Wig"].rearrange("(k p) n -> p k n", p=P)).then_inc(w_in, 16)
        sp.dma_start(gw, d["g_weight"].partition_broadcast(P)).then_inc(w_in, 16)
        sp.dma_start(mask, d["causal"]).then_inc(w_in, 16)

    def vector(v):
        norm.solve(v)
        over_tiles(v, lambda t, u: norm.apply(v, xn, hb, t).then_inc(xr, 1))
        c = Chain(v, kch)
        c.put(v.memset(ss, 1.0))

        def queries(q):
            v.wait_ge(qsig, q + 1)
            src = ps[0:KH, 2, :].rearrange("p (b n) -> p b n", b=4)
            bs = bass.ds(4 * q, 4)
            v.scalar_tensor_tensor(out=qs[:, bs, 1:SEQ], in0=src, scalar=SILU_SCALE, in1=sq[:, bs, 1:SEQ], op0=ALU.mult, op1=ALU.mult).then_inc(qkr, 1)

        looped(v, NQ, queries)
        v.wait_ge(qsig, NQ + 1)
        v.scalar_tensor_tensor(out=qs[:, :, 0], in0=ps[0:KH, 3, 0:NB], scalar=SILU_SCALE, in1=sq[:, :, 0], op0=ALU.mult, op1=ALU.mult).then_inc(qkr, 1)
        v.wait_ge(asig, NQ + 1)
        c.link(v.memset(bv, 0.0))
        starts = slice(1, SEQ, BL)
        c.put(v.tensor_copy(bv[:, :, starts], av[:, :, starts]))
        c.put(v.memset(bv[:, :, 0], 1.0))
        c.wait()
        c.put(v.memset(av[:, :, starts], 0.0))
        c.link(v.memset(av[:, :, 0], 0.0))
        c.link(v.tensor_tensor_scan(F(pv), F(av), F(bv), 0.0, ALU.mult, ALU.add))
        v.wait_ge(qkr, NQ + 1)
        c.link(v.reciprocal(F(av), F(pv)))
        c.put(v.tensor_tensor(F(qs), F(qs), F(pv), ALU.mult))
        v.wait_ge(ksig, NQ + 1)
        v.tensor_tensor(F(kb0), F(kb0), F(av), ALU.mult).then_inc(kbr, 1)
        v.wait_ge(kbr, 1)
        c.wait()
        for n in range(1, NBL):
            w = 1 + BL * n
            total = pv[:, :, BL * n:BL * n + 1]
            if n > 1:
                v.wait_ge(cp, n - 1)
            v.tensor_tensor(kb[n][:, :, 0:w], kb[n - 1][:, :, 0:w], bc(total, 2, w), ALU.mult).then_inc(kbr, 1)
            v.wait_ge(kbr, n + 1)
        v.wait_ge(w_in, 5 * 16)
        own = ident[0:NB, 0:NB].unsqueeze(2)
        for n in range(NBL):
            v.wait_ge(acp, n + 1)
            v.tensor_tensor(atc[:, :, n * BL:(n + 1) * BL], ps[0:NB, n, :].rearrange("p (b n) -> p b n", b=NB), bc(own, 2, BL), ALU.mult).then_inc(atcr, 1)

        def masked(t, u):
            v.wait_ge(ap, t + 1)
            if not early(t):
                v.wait_ge(ob, t - 1)
            if tile_rows(t) == NB:
                v.tensor_tensor(ats[0:NB, u, 0:NB], ps[0:NB, u, 0:NB], ident[0:NB, 0:NB], ALU.mult).then_inc(atr, 1)
            else:
                v.tensor_tensor(ats[:, u], ps[:, u, 0:P], mask, ALU.mult).then_inc(atr, 1)

        def gated(t, u):
            r = tile_rows(t)
            v.wait_ge(sgr, t + 1)
            v.tensor_tensor(sg[0:r, u], ps[0:r, 6 + u, :], sg[0:r, u], ALU.mult).then_inc(t1r, 1)
            v.wait_ge(t1r, t + 1)
            if not early(t):
                v.wait_ge(gwr, t - 1)
            v.wait_ge(ssr, t + 1)
            v.tensor_tensor(pb[0:r, u], ps[0:r, 2 + u, :], sg[0:r, u], ALU.mult).then_inc(pr, 1)

        masked(0, 0)
        masked(1, 1)
        gated_loop(v, lambda t, u: (masked(t + 1, 1 - u), gated(t - 1, 1 - u)))
        masked(NB, 0)
        gated(NB - 2, 0)
        gated(NB - 1, 1)
        gated(NB, 0)
        v.wait_ge(ssr, T)
        c2 = norm.chain(v)
        norm.newton(v, c2, ss, 1.0 / D, LN_EPS)
        norm.closed(c2)

        def add(t, u):
            r = tile_rows(t)
            v.wait_ge(gwr, t + 1)
            v.scalar_tensor_tensor(out=hb[0:r, t, :], in0=xn[0:r, t, :], scalar=norm.rstd[0:r, bass.ds(t, 1)], in1=hb[0:r, t, :], op0=ALU.mult, op1=ALU.add).then_inc(hr, 1)
            v.wait_ge(hr, t + 1)
            norm.take_stats(v, hb, t)

        over_tiles(v, add)

    def gated_loop(eng, body):
        def pair(i):
            for u in range(2):
                body(2 * i + 1 + u, 1 - u)

        looped(eng, NB // 2 - 1, pair)

    def gpsimd(p):
        p.wait_ge(w_in, 5 * 16)

        def weigh(t, u):
            r = tile_rows(t)
            p.wait_ge(pr, t + 1)
            if isinstance(t, int) and t == NB:
                p.wait_ge(ob, T)
            p.tensor_tensor(xn[0:r, t, :], pb[0:r, u], gw[0:r], ALU.mult).then_inc(gwr, 1)

        over_tiles(p, weigh)

    def scalar(s):
        def sigmoids(q, src_q, src_k, w, out):
            s.wait_ge(qk, q + 1)
            s.activation(out(sq), src_q, ACT.Sigmoid).then_inc(qsig, 1)
            s.activation(out(kb0), src_k, ACT.Sigmoid).then_inc(ksig, 1)
            s.wait_ge(ksig, q + 1)
            s.activation(out(av), out(kb0), ACT.Sigmoid, scale=-1.0).then_inc(asig, 1)

        def quarter(q):
            for j in range(4):
                s.wait_ge(turned, 4 * q + j + 1)
                turned_out(s, ps[:, j % 2, :], xnT, 4 * q + j).then_inc(tev, 1)
            split = (lambda x: x.rearrange("p (b n) -> p b n", b=4))
            sigmoids(q, split(ps[0:KH, 2, :]), split(ps[KH:2 * KH, 2, :]), QC, lambda x: x[:, bass.ds(4 * q, 4), 1:SEQ])

        looped(s, NQ, quarter)
        s.wait_ge(turned, T)
        turned_out(s, ps[:, 0, :], xnT, NB).then_inc(tev, 1)
        sigmoids(NQ, ps[0:KH, 3, 0:NB], ps[KH:2 * KH, 3, 0:NB], NB, lambda x: x[:, :, 0])
        for n in range(1, NBL):
            s.wait_ge(kbr, n)
            w = 1 + BL * n
            s.activation(kb[n][:, :, w:SEQ], kb0[:, :, w:SEQ], ACT.Copy).then_inc(cp, 1)

        def outs(t, u):
            r = tile_rows(t)
            s.wait_ge(ob, t + 1)
            if not early(t):
                s.wait_ge(gor, t - 1)
            s.activation(ots[:, u, :, 0:r], ps[:, 4 + u, 0:KD * r].rearrange("p (k n) -> p k n", k=KD), ACT.Copy).then_inc(otr, 1)
            if not (isinstance(t, int) and t == 0):
                s.wait_ge(ssr, t)
            s.activation(junk[0:r], ps[0:r, 2 + u, :], ACT.Square, accum_out=ss[0:r, bass.ds(t, 1)]).then_inc(ssr, 1)

        def gate(t, u):
            r = tile_rows(t)
            s.wait_ge(gor, t + 1)
            if not early(t):
                s.wait_ge(pr, t - 1)
            s.activation(sg[0:r, u], ps[0:r, 6 + u, :], ACT.Sigmoid).then_inc(sgr, 1)

        outs(0, 0)
        gated_loop(s, lambda t, u: (outs(t, u), gate(t - 1, 1 - u)))
        outs(NB - 1, 1)
        gate(NB - 2, 0)
        outs(NB, 0)
        gate(NB - 1, 1)
        gate(NB, 0)

    def tensor(t):
        t.wait_ge(w_in, 5 * 16)

        def project(q, cols, w, bank):
            for k in range(KD):
                mm = t.matmul(ps[0:2 * KH, bank, 0:w], wqk[:, k, :], xnT[:, k, cols], start=(k == 0), stop=(k == KD - 1))
            mm.then_inc(qk, 1)

        for q in range(NQ):
            for j in range(4):
                n = 4 * q + j
                t.wait_ge(xr, n + 1)
                if n >= 2:
                    t.wait_ge(tev, n - 1)
                turn_tile(t, ps[:, j % 2, :], xn, n, ident).then_inc(turned, 1)
            t.wait_ge(tev, 4 * q + 4)
            if q:
                t.wait_ge(qkr, q)
                t.wait_ge(ksig, q)
            project(q, slice(q * QC, (q + 1) * QC), QC, 2)
        t.wait_ge(xr, T)
        turn_tile(t, ps[:, 0, :], xn, NB, ident).then_inc(turned, 1)
        t.wait_ge(tev, T)
        project(NQ, slice(NCOL, NTOK), NB, 3)
        t.wait_ge(cp, NBL - 1)
        t.wait_ge(kbr, NBL)
        t.wait_ge(qkr, NQ + 1)
        for n in range(NBL):
            t.matmul(ps[0:NB, n, :], kb[n][:, :, 0], qs[:, :, 1 + n * BL:1 + (n + 1) * BL], start=True, stop=True).then_inc(acp, 1)
        t.wait_ge(atcr, NBL)

        def attend(n):
            u = n % 2
            if n >= 2:
                t.wait_ge(atr, n - 1)
            if n == NB:
                t.matmul(ps[0:NB, u, 0:NB], kb0[:, :, 0], qs[:, :, 0], start=True, stop=True).then_inc(ap, 1)
                return
            for m in range(NBL):
                mm = t.matmul(ps[:, u, m * BL:(m + 1) * BL], kb[m][:, n, 1:SEQ], qs[:, n, 1 + m * BL:1 + (m + 1) * BL], start=True, stop=True)
            mm.then_inc(ap, 1)

        def outs(n):
            u, r = n % 2, tile_rows(n)
            t.wait_ge(atr, n + 1)
            if n >= 2:
                t.wait_ge(pr, n - 1)
                t.wait_ge(otr, n - 1)
            last = n == NB
            t.matmul(ps[0:r, 2 + u, :], ats[0:r, u, 0:r], xn[0:r, n, :], start=True, stop=last)
            if not last:
                t.matmul(ps[0:r, 2 + u, :], atc[:, n, :], xn[0:NB, NB, :], start=False, stop=True)
            for k in range(KD):
                ks = slice(k * P, (k + 1) * P)
                mm = t.matmul(ps[:, 4 + u, k * r:(k + 1) * r], xn[0:r, n, ks], ats[0:r, u, 0:r], start=True, stop=last)
                if not last:
                    mm = t.matmul(ps[:, 4 + u, k * r:(k + 1) * r], xn[0:NB, NB, ks], atc[:, n, :], start=False, stop=True)
            mm.then_inc(ob, 1)

        def gate(n):
            u, r = n % 2, tile_rows(n)
            cols = slice(NCOL, NTOK) if n == NB else slice(n * P, (n + 1) * P)
            t.wait_ge(otr, n + 1)
            if n >= 2:
                t.wait_ge(pr, n - 1)
            for k in range(KD):
                t.matmul(ps[0:r, 6 + u, :], xnT[:, k, cols], wig[:, k, :], start=(k == 0), stop=False)
            for k in range(KD):
                mm = t.matmul(ps[0:r, 6 + u, :], ots[:, u, k, 0:r], wog[:, k, :], start=False, stop=(k == KD - 1))
            mm.then_inc(gor, 1)

        attend(0)
        for n in range(T):
            if n + 1 < T:
                attend(n + 1)
            outs(n)
            if n:
                gate(n - 1)
        gate(NB)

    return sync, vector, gpsimd, scalar, tensor, hr


class Shared:

    def __init__(self, nc, sem, arena):
        self.h = arena.take(T, D)
        self.xn_at = arena.at
        self.xn = arena.take(T, D)
        self.y_at = arena.at
        self.y = arena.take(T, D)
        self.xnT = arena.take(KD, NTOK)
        self.scratch_at = arena.at
        self.top_at = arena.tensor.shape[1] - 340
        arena = Arena(arena.tensor, self.top_at)
        self.ident = arena.take(P)
        self.norm = Norm(arena, sem("norm_chain"))
        self.h_ready = sem("h_after_scan")


def tower(nc, d, out):
    with ExitStack() as ctx:
        def sem(name):
            return ctx.enter_context(nc.semaphore(name))

        sb = ctx.enter_context(nc.sbuf_tensor("sb", [P, 51 * 1024], F32))
        ps = ctx.enter_context(nc.psum_tensor("ps", [P, 8, 512], F32))
        h0 = nc.dram_tensor("tokens", (NB, NH, D), F32).ap()
        dram = {"xn": nc.dram_tensor("xn_rows", (NTOK, D), F32).ap(),
                "slots": nc.dram_tensor("slot_tokens", (NSLOT, 1), U32).ap(),
                "expert_out": nc.dram_tensor("expert_out", (NSLOT, D), F32).ap()}
        arena = Arena(sb)
        g = Shared(nc, sem, arena)
        tok = tokenizer(nc, sem, sb, ps, d, h0, 0)
        scan = scan_layer(nc, sem, sb, ps, d, h0, tok[5], g, g.scratch_at)
        ffn0 = ffn_layer(nc, sem, sb, ps, d, dram, g, "ffn0", 256, 2, True, lambda sp: sp.wait_ge(g.h_ready, T))
        gla = gla_layer(nc, sem, sb, ps, d, g, g.scratch_at, lambda sp: sp.wait_ge(ffn0[5], 2 * T))
        ffn1 = ffn_layer(nc, sem, sb, ps, d, dram, g, "ffn1", 352, 4, False, lambda sp: sp.wait_ge(gla[5], T))
        h_out = sem("h_stored")
        block = ctx.enter_context(nc.Block())

        @block.sync
        def _(sp):
            tok[0](sp)
            scan[0](sp)
            ffn0[0](sp)
            gla[0](sp)
            ffn1[0](sp)
            sp.wait_ge(ffn1[5], 2 * T)
            sp.dma_start(out[:, 1:SEQ, :].rearrange("b p d -> p b d"), g.h[:, 0:NB, :]).then_inc(h_out, 16)
            sp.dma_start(out[:, 0, :], g.h[0:NB, NB, :]).then_inc(h_out, 16)
            sp.wait_ge(h_out, 32)

        @block.vector
        def _(v):
            tok[1](v)
            scan[1](v)
            ffn0[1](v)
            gla[1](v)
            ffn1[1](v)

        @block.gpsimd
        def _(p):
            tok[2](p)
            scan[2](p)
            ffn0[2](p)
            gla[2](p)
            ffn1[2](p)

        @block.scalar
        def _(s):
            tok[3](s)
            scan[3](s)
            ffn0[3](s)
            gla[3](s)
            ffn1[3](s)

        @block.tensor
        def _(t):
            tok[4](t)
            scan[4](t)
            ffn0[4](t)
            gla[4](t)
            ffn1[4](t)


def laid_out(i):
    f = {k: np.asarray(v) for k, v in i.items()}
    t8 = np.arange(TB)
    k0 = np.concatenate([t8, TB * t8, TJ * t8, [0.5, 1, L // 2, L]])
    km = np.concatenate([np.repeat([TB - 1, TB * (TB - 1), TJ * (TB - 1)], TB), [0, 0, 0, 0]])

    def gate_up(gate, up):
        w = np.concatenate([gate, up], axis=2)
        n, _, c = w.shape
        return w.reshape(n, KD, P, c).transpose(0, 2, 1, 3)

    def cut(w, n):
        return w.reshape(w.shape[0], n, -1).transpose(1, 0, 2)

    def router(gate, shared):
        return np.concatenate([gate.T, shared.reshape(D, 1)], axis=1).reshape(KD, P, -1).transpose(1, 0, 2)

    T01 = (0, 2, 1)
    a = {
        "kconst": np.stack([k0, -km]).astype(np.float32),
        "lam": f["L0_tok_Lambda"],
        "log_dt": f["L0_tok_log_dt"].T,
        "x": f["x"].transpose(3, 2, 1, 0).reshape(2, NS, NH * NB),
        "ident": np.eye(P, dtype=np.float32),
        "W_in": f["L0_attn_W_in"], "W_fwd": f["L0_attn_W_fwd"], "W_bwd": f["L0_attn_W_bwd"], "W_out": f["L0_attn_W_out"],
        "gamma": f["L0_attn_gamma"], "beta": f["L0_attn_beta"],
        "iota8": np.arange(8, dtype=np.float32),
        "ffn0_router": router(f["L0_ffn_gate_w"], f["L0_ffn_se_gate_w"]),
        "ffn0_gate_up": gate_up(f["L0_ffn_w_gate"].transpose(T01), f["L0_ffn_w_up"].transpose(T01)),
        "ffn0_down": f["L0_ffn_w_down"].transpose(T01),
        "ffn0_sh_gate_up": gate_up(cut(f["L0_ffn_sh_gate"].T, 2), cut(f["L0_ffn_sh_up"].T, 2)),
        "ffn0_sh_down": f["L0_ffn_sh_down"].T.reshape(2, 256, D),
        "Wqk": np.concatenate([f["L1_attn_Wq"].T, f["L1_attn_Wk"].T], axis=1).reshape(KD, P, -1).transpose(1, 0, 2),
        "Wog": f["L1_attn_Wog"].T, "Wig": f["L1_attn_Wig"].T, "g_weight": f["L1_attn_g_weight"],
        "causal": np.triu(np.ones((P, P), np.float32)),
        "ffn1_router": router(f["L1_ffn_gate_w"], f["L1_ffn_shared_gate_w"]),
        "ffn1_gate_up": gate_up(f["L1_ffn_w_gate"], f["L1_ffn_w_up"]),
        "ffn1_down": f["L1_ffn_w_down"],
        "ffn1_sh_gate_up": gate_up(cut(f["L1_ffn_sw_gate"], 4), cut(f["L1_ffn_sw_up"], 4)),
        "ffn1_sh_down": f["L1_ffn_sw_down"].reshape(4, 352, D),
        "iota_tiles": np.arange(NTILE, dtype=np.float32),
        "valid": np.arange(T * P).reshape(T, P).T < NTOK,
        "before": np.triu(np.ones((P, P)), 1),
        "ones": np.ones((P, P)),
        "cls": np.broadcast_to(f["cls_tok"][0], (NB, D)),
    }
    a = {k: np.ascontiguousarray(v, np.float32) for k, v in a.items()}
    a["token_ids"] = np.ascontiguousarray(np.arange(T * P).reshape(T, P).T, np.int32)
    return a


def kernel(**inputs):
    import concourse.bacc as _bacc
    from concourse.bass_utils import run_bass_kernel_spmd as _run

    nc = _bacc.Bacc("TRN2", target_bir_lowering=False, num_devices=1)
    arrays, d = {}, {}
    for name, a in laid_out(inputs).items():
        arrays[f"in_{name}"] = a
        d[name] = nc.dram_tensor(f"in_{name}", a.shape, mybir.dt.from_np(a.dtype), kind="ExternalInput").ap()
    out = nc.dram_tensor("out", (NB, SEQ, D), F32, kind="ExternalOutput").ap()
    tower(nc, d, out)
    r = _run(nc, [arrays], core_ids=[0])
    return r.results[0]["out"]
```

```python
from contextlib import ExitStack

import concourse.bass as bass
import numpy as np
from concourse import mybir

F32 = mybir.dt.float32
F32R = mybir.dt.float32r
I32 = mybir.dt.int32
U32 = mybir.dt.uint32
ALU = mybir.AluOpType
ACT = mybir.ActivationFunctionType
AX = mybir.AxisListType

P = 128
NB = 16
NH = 128
NS = 64
L = 512
D = 512
KD = D // P
T = NB + 1
NCOL = NB * NH
NTOK = NB * (NH + 1)
SEQ = NH + 1
NQ = 4
QC = 512
LN_EPS = 1e-5
SILU_SCALE = 32 ** -0.5

TB = 8
TI, TJ = 8, 64
HC = 16
NHC = NH // HC
NK = 3 * TB
MAGIC = 1.5 * 2.0 ** 23
TWO_PI = 2 * np.pi


class Chain:

    def __init__(self, eng, sem, base=0):
        self.eng, self.sem, self.base, self.n = eng, sem, base, 0

    def put(self, ins):
        self.n += 1
        ins.then_inc(self.sem, 1)

    def wait(self):
        self.eng.wait_ge(self.sem, self.base + self.n)

    def link(self, ins):
        self.put(ins)
        self.wait()


def looped(eng, n, body):
    body(0)
    if n > 1:
        with eng.Fori(1, n) as i:
            body(i)


def is_first(i):
    return isinstance(i, int) and i == 0


def bc(ap, dim, n):
    shape = list(ap.shape)
    shape[dim] = n
    return ap.to_broadcast(shape)


class Arena:

    def __init__(self, tensor, at=0, origin=0):
        self.tensor, self.at, self.origin = tensor, at, origin

    def take(self, *shape, rows=P, dt=F32):
        size = int(np.prod(shape))
        flat = self.tensor[0:rows, self.at - self.origin:self.at - self.origin + size]
        self.at += size + size % 2
        assert self.at - self.origin <= self.tensor.shape[1], self.at
        if dt != F32:
            flat = flat.bitcast(dt)
        if len(shape) == 1:
            return flat
        names = [f"d{k}" for k in range(len(shape))]
        return flat.rearrange(f"p ({' '.join(names)}) -> p {' '.join(names)}",
                              **{n: s for n, s in zip(names[1:], shape[1:])})


def tokenizer(nc, sem, sb, held, ps, d, h0):
    a = Arena(sb)
    lam = a.take(2)
    ld = a.take(2, NH)
    kc = a.take(2, NK + 4)
    wre, wim = a.take(NH, NB), a.take(NH, NB)
    pos, sig, sgn = a.take(1), a.take(1), a.take(1)
    kt, kt2 = a.take(NK), a.take(4)
    ex, en, er, ep, es = (a.take(4, NH) for _ in range(5))
    eni = a.take(4 * NH, dt=I32)
    dt = a.take(2, NH)
    dre, dim = a.take(NH), a.take(NH)
    em = a.take(2, NH)
    fa, fb, p1, q, t0, fhi, flo = (a.take(NH) for _ in range(7))
    sm = [a.take(NH, 4) for _ in range(6)]
    nr, ni, dr, di, xr, xi, s0, s1, inv = (a.take(NH) for _ in range(9))
    cr, ci, c1, c2 = (a.take(NH) for _ in range(4))
    m, kl, ke, mk, re, im = (a.take(NH, NK) for _ in range(6))
    a1, a2 = a.take(2, HC, TI), a.take(2, HC, TI)
    d1, d2 = a.take(2, HC, TB), a.take(2, HC, TB)
    ta, tb = a.take(HC, TB), a.take(HC, TB)
    h_space = Arena(held)
    u1, u2 = h_space.take(2, HC, TI * NB), h_space.take(2, HC, TI * NB)
    bb, bt = a.take(2, HC, TJ), a.take(HC, TJ)
    ob = a.take(2, HC * TJ)
    LO, HI = slice(0, NS), slice(NS, P)
    INV = 1.0 / TWO_PI

    def top12(x):
        return float((np.array([x], np.float32).view(np.uint32) & np.uint32(0xFFFFF000)).view(np.float32)[0])

    V1 = top12(INV)
    V2 = top12(INV - V1)
    V3 = float(np.float32(INV - V1 - V2))
    LN2H = 355.0 / 512.0
    LN2L = float(np.log(2.0) - LN2H)

    par_in, w_in = sem("tok_params_loaded"), sem("tok_weights_loaded")
    dch = sem("tok_vector_chain")
    phase = sem("tok_phase_split")
    lin = sem("tok_linear_ready")
    sm_in, sm_out = sem("tok_small_args"), sem("tok_small_sines")
    arg, sines = sem("tok_sine_args"), sem("tok_sines")
    expd = sem("tok_decays")
    scaled = sem("tok_tables_scaled")
    ab, uw, u2r = sem("tok_factors"), sem("tok_u1_and_b"), sem("tok_u2")
    prod, evac, stored = sem("tok_products"), sem("tok_evacuated"), [sem(f"tok_stored{k}") for k in range(2)]
    H2 = NH // 2
    hs = [slice(0, H2), slice(H2, NH)]

    def sync(sp):
        for half in (LO, HI):
            sp.dma_start(lam[half, :], d["lam"]).then_inc(par_in, 16)
        for k in range(2):
            sp.dma_start(ld[:, k, :], d["log_dt"][k].partition_broadcast(P)).then_inc(par_in, 16)
            sp.dma_start(kc[:, k, :], d["kconst"][k].partition_broadcast(P)).then_inc(par_in, 16)
        for w, k in ((wre, 0), (wim, 1)):
            for half in (LO, HI):
                sp.dma_start(w[half, :, :].rearrange("p h c -> p (h c)"), d["x"][k]).then_inc(w_in, 16)
        h0v = h0.rearrange("c (g h) (i j) -> i c g h j", j=TJ, h=HC)

        def store(k, u):
            sp.wait_ge(evac, 2 * k + 2)
            for i in range(TI):
                sp.dma_start(h0v[i, :, k, :, :],
                             ob[i * NB:(i + 1) * NB, u, :].rearrange("c (h j) -> c h j", j=TJ)).then_inc(stored[u], 16)

        def pair(i):
            for u in range(2):
                store(2 * i + u, u)

        looped(sp, NHC // 2, pair)
    def all_stored(sp):
        for u in range(2):
            sp.wait_ge(stored[u], 16 * TI * NHC // 2)

    def vector(v):
        c = Chain(v, dch)
        v.wait_ge(par_in, 6 * 16)

        def exp_parts(x, w):
            X, N, R, PM, S = (t[:, 0:w, :] for t in (x, en, er, ep, es))
            NI = eni[:, 0:w * NH].rearrange("p (a b) -> p a b", b=NH)
            c.link(v.tensor_scalar(X, X, -87.0, 88.0, ALU.max, ALU.min))
            c.link(v.tensor_scalar(N, X, float(1 / np.log(2.0)), MAGIC, ALU.mult, ALU.add))
            c.link(v.tensor_scalar(N, N, -MAGIC, None, ALU.add))
            c.link(v.scalar_tensor_tensor(out=R, in0=N, scalar=-LN2H, in1=X, op0=ALU.mult, op1=ALU.add))
            c.link(v.scalar_tensor_tensor(out=R, in0=N, scalar=-LN2L, in1=R, op0=ALU.mult, op1=ALU.add))
            c.link(v.tensor_scalar(PM, R, 1.0 / 40320, None, ALU.mult))
            for f in (5040, 720, 120, 24, 6, 2, 1):
                c.link(v.scalar_tensor_tensor(out=PM, in0=PM, scalar=1.0 / f, in1=R, op0=ALU.add, op1=ALU.mult))
            c.link(v.tensor_scalar(NI, N, 127.0, None, ALU.add))
            c.link(v.tensor_scalar(S.bitcast(I32), NI, 23, None, ALU.logical_shift_left))

        c.link(v.tensor_copy(ex[:, 0:2, :], ld[:, :, :]))
        exp_parts(ex, 2)
        c.link(v.scalar_tensor_tensor(out=dt, in0=ep[:, 0:2, :], scalar=1.0, in1=es[:, 0:2, :], op0=ALU.add, op1=ALU.mult))
        c.link(v.tensor_scalar(dre, dt[:, 0, :], lam[:, 0:1], None, ALU.mult))
        c.link(v.tensor_scalar(dim, dt[:, 1, :], lam[:, 1:2], None, ALU.mult))
        c.link(v.tensor_scalar(pos, lam[:, 0:1], 0.0, None, ALU.is_gt))
        c.link(v.tensor_scalar(sig, pos, -2.0, 1.0, ALU.mult, ALU.add))
        c.link(v.memset(sgn[LO, :], 1.0))
        c.link(v.memset(sgn[HI, :], -1.0))
        c.link(v.scalar_tensor_tensor(out=kt, in0=kc[:, 1, 0:NK], scalar=pos[:, 0:1], in1=kc[:, 0, 0:NK], op0=ALU.mult, op1=ALU.add))
        c.link(v.tensor_copy(kt2, kc[:, 0, NK:NK + 4]))
        c.link(v.tensor_scalar(fa.bitcast(U32), dim.bitcast(U32), 0xFFFFF000, None, ALU.bitwise_and))
        c.link(v.tensor_tensor(fb, dim, fa, ALU.subtract))
        c.link(v.tensor_scalar(p1, fa, V1, None, ALU.mult))
        c.link(v.tensor_scalar(t0, p1, MAGIC, None, ALU.add))
        c.link(v.scalar_tensor_tensor(out=t0, in0=t0, scalar=-MAGIC, in1=p1, op0=ALU.add, op1=ALU.subtract))
        c.link(v.tensor_scalar(p1, t0, -1.0, None, ALU.mult))
        c.link(v.tensor_scalar(q, fb, V2, None, ALU.mult))
        c.link(v.scalar_tensor_tensor(out=q, in0=fa, scalar=V3, in1=q, op0=ALU.mult, op1=ALU.add))
        c.link(v.tensor_scalar(t0, fb, V1, None, ALU.mult))
        c.link(v.scalar_tensor_tensor(out=t0, in0=fa, scalar=V2, in1=t0, op0=ALU.mult, op1=ALU.add))
        c.link(v.tensor_tensor(q, q, t0, ALU.add))
        c.link(v.tensor_tensor(t0, p1, q, ALU.add))
        c.link(v.tensor_scalar(t0, t0, MAGIC / 32768, None, ALU.add))
        c.link(v.tensor_scalar(fhi, t0, -MAGIC / 32768, None, ALU.add))
        c.link(v.tensor_tensor(flo, p1, fhi, ALU.subtract))
        v.tensor_tensor(flo, flo, q, ALU.add).then_inc(phase, 1)
        v.wait_ge(phase, 1)
        c.link(v.tensor_scalar(t0, fhi, MAGIC, None, ALU.add))
        c.link(v.tensor_scalar(t0, t0, -MAGIC, None, ALU.add))
        c.link(v.tensor_tensor(fhi, fhi, t0, ALU.subtract))

        def args(out, mm, mmk, kk, ph):
            c.link(v.tensor_scalar(out, mmk, ph, MAGIC, ALU.add, ALU.add))
            c.link(v.scalar_tensor_tensor(out=out, in0=out, scalar=-MAGIC, in1=mm, op0=ALU.add, op1=ALU.subtract))
            c.link(v.scalar_tensor_tensor(out=out, in0=out, scalar=-ph, in1=kk, op0=ALU.add, op1=ALU.subtract))
            return v.tensor_scalar(out, out, -0.5, 0.5, ALU.max, ALU.min)

        def spread(x, w):
            return bc(x.unsqueeze(2), 2, w)

        k4 = bc(kt2.unsqueeze(1), 1, NH)
        ms, ks, mks, co, si, _ = sm
        c.link(v.tensor_tensor(ms, k4, spread(fhi, 4), ALU.mult))
        c.link(v.tensor_tensor(ks, k4, spread(flo, 4), ALU.mult))
        c.link(v.tensor_tensor(mks, ms, ks, ALU.add))
        args(si, ms, mks, ks, 0.0).then_inc(sm_in, 1)
        args(co, ms, mks, ks, 0.25).then_inc(sm_in, 1)
        k24 = bc(kt.unsqueeze(1), 1, H2)
        for n, h in enumerate(hs):
            c.link(v.tensor_tensor(m[:, h, :], k24, spread(fhi[:, h], NK), ALU.mult))
            v.wait_ge(lin, 2 * n + 2)
            c.link(v.tensor_tensor(mk[:, h, :], m[:, h, :], kl[:, h, :], ALU.add))
            args(re[:, h, :], m[:, h, :], mk[:, h, :], kl[:, h, :], 0.25).then_inc(arg, 1)
            args(im[:, h, :], m[:, h, :], mk[:, h, :], kl[:, h, :], 0.0).then_inc(arg, 1)
        c.link(v.tensor_scalar(ex[:, 0, :], dre, sig[:, 0:1], None, ALU.mult))
        c.link(v.tensor_scalar(ex[:, 1, :], ex[:, 0, :], float(L), None, ALU.mult))
        exp_parts(ex, 2)
        c.link(v.tensor_tensor(em, ep[:, 0:2, :], es[:, 0:2, :], ALU.mult))
        c.link(v.scalar_tensor_tensor(out=em, in0=es[:, 0:2, :], scalar=-1.0, in1=em, op0=ALU.add, op1=ALU.add))
        v.wait_ge(sm_out, 2)
        for out_r, out_i, e, kk in ((nr, ni, em[:, 0, :], 1), (dr, di, em[:, 1, :], 3)):
            c.link(v.tensor_tensor(s0, si[:, :, kk - 1], si[:, :, kk - 1], ALU.mult))
            c.link(v.tensor_tensor(out_r, e, co[:, :, kk], ALU.mult))
            c.link(v.scalar_tensor_tensor(out=out_r, in0=s0, scalar=-2.0, in1=out_r, op0=ALU.mult, op1=ALU.add))
            c.link(v.scalar_tensor_tensor(out=out_i, in0=e, scalar=1.0, in1=si[:, :, kk], op0=ALU.add, op1=ALU.mult))
            c.link(v.tensor_scalar(out_i, out_i, sig[:, 0:1], None, ALU.mult))
        c.link(v.tensor_scalar(s0, di, lam[:, 1:2], None, ALU.mult))
        c.link(v.scalar_tensor_tensor(out=xr, in0=dr, scalar=lam[:, 0:1], in1=s0, op0=ALU.mult, op1=ALU.subtract))
        c.link(v.tensor_scalar(s0, di, lam[:, 0:1], None, ALU.mult))
        c.link(v.scalar_tensor_tensor(out=xi, in0=dr, scalar=lam[:, 1:2], in1=s0, op0=ALU.mult, op1=ALU.add))
        c.link(v.tensor_tensor(s0, xr, xr, ALU.mult))
        c.link(v.tensor_tensor(s1, xi, xi, ALU.mult))
        c.link(v.scalar_tensor_tensor(out=s0, in0=s0, scalar=1e-7, in1=s1, op0=ALU.add, op1=ALU.add))
        c.link(v.reciprocal(inv, s0))
        for out, g, h, w, x, op in ((cr, nr, xr, ni, xi, ALU.add), (ci, ni, xr, nr, xi, ALU.subtract)):
            c.link(v.tensor_tensor(s0, g, h, ALU.mult))
            c.link(v.tensor_tensor(s1, w, x, ALU.mult))
            c.link(v.tensor_tensor(s0, s0, s1, op))
            c.link(v.tensor_tensor(out, s0, inv, ALU.mult))
        c.link(v.tensor_copy(c1[LO, :], cr[LO, :]))
        c.link(v.tensor_copy(c1[HI, :], ci[HI, :]))
        c.link(v.tensor_scalar(c2[LO, :], ci[LO, :], -1.0, None, ALU.mult))
        c.link(v.tensor_copy(c2[HI, :], cr[HI, :]))
        v.wait_ge(w_in, 64)
        v.wait_ge(scaled, 4)

        PER = 22

        def pair(i):
            s = Chain(v, dch, c.n + i * PER)
            for u in range(2):
                k = 2 * i + u
                hh = bass.ds(k * HC, HC)
                AR, AI = re[:, hh, 2 * TB:3 * TB], im[:, hh, 2 * TB:3 * TB]
                R1, I1 = re[:, hh, 0:TB], im[:, hh, 0:TB]
                R2, I2 = re[:, hh, TB:2 * TB], im[:, hh, TB:2 * TB]
                C1, C2 = spread(c1[:, hh], TI), spread(c2[:, hh], TI)
                if not is_first(i):
                    v.wait_ge(prod, 2 * (k - 1))
                s.put(v.tensor_tensor(a1[:, u], C1, AR, ALU.mult))
                s.put(v.tensor_tensor(ta, C2, AI, ALU.mult))
                s.put(v.tensor_tensor(a2[:, u], C2, AR, ALU.mult))
                s.link(v.tensor_tensor(tb, C1, AI, ALU.mult))
                s.put(v.tensor_tensor(a1[:, u], a1[:, u], ta, ALU.add))
                v.tensor_tensor(a2[:, u], a2[:, u], tb, ALU.subtract).then_inc(ab, 1)
                s.put(v.tensor_copy(d1[LO, u], R2[LO]))
                s.put(v.tensor_scalar(d1[HI, u], I2[HI], -1.0, None, ALU.mult))
                s.put(v.tensor_scalar(d2[LO, u], I2[LO], -1.0, None, ALU.mult))
                s.link(v.tensor_scalar(d2[HI, u], R2[HI], -1.0, None, ALU.mult))
                B4 = bb[:, u].rearrange("p h (b c) -> p h b c", c=TB)
                T4 = bt.rearrange("p h (b c) -> p h b c", c=TB)

                def outer(small, big):
                    return bc(small.unsqueeze(2), 2, TB), bc(big.unsqueeze(3), 3, TB)

                x, y = outer(R1, d1[:, u])
                s.put(v.tensor_tensor(B4, x, y, ALU.mult))
                x, y = outer(I1, d2[:, u])
                s.link(v.tensor_tensor(T4, x, y, ALU.mult))
                v.tensor_tensor(bb[:, u], bb[:, u], bt, ALU.add).then_inc(uw, 1)
                U4 = u1[:, u].rearrange("p h (i c) -> p h i c", c=NB)
                v.tensor_tensor(U4, bc(wre[:, hh, :].unsqueeze(2), 2, TI), bc(a1[:, u].unsqueeze(3), 3, NB), ALU.mult).then_inc(uw, 1)
            assert s.n == PER

        looped(v, NHC // 2, pair)

    def gpsimd(g):
        g.wait_ge(phase, 1)
        for n, h in enumerate(hs):
            k24 = bc(kt.unsqueeze(1), 1, H2)
            g.tensor_tensor(kl[:, h, :], k24, bc(flo[:, h].unsqueeze(2), 2, NK), ALU.mult).then_inc(lin, 1)
            g.tensor_tensor(ke[:, h, :], k24, bc(dre[:, h].unsqueeze(2), 2, NK), ALU.mult).then_inc(lin, 1)
        for n, h in enumerate(hs):
            g.wait_ge(expd, n + 1)
            for j, t in enumerate((re, im)):
                g.wait_ge(sines, 2 * n + j + 1)
                g.tensor_tensor(t[:, h, :], t[:, h, :], ke[:, h, :], ALU.mult).then_inc(scaled, 1)
        g.wait_ge(w_in, 64)

        def pair(i):
            for u in range(2):
                k = 2 * i + u
                hh = bass.ds(k * HC, HC)
                g.wait_ge(ab, k + 1)
                if not is_first(i):
                    g.wait_ge(prod, 2 * (k - 1))
                U4 = u2[:, u].rearrange("p h (i c) -> p h i c", c=NB)
                g.tensor_tensor(U4, bc(wim[:, hh, :].unsqueeze(2), 2, TI), bc(a2[:, u].unsqueeze(3), 3, NB), ALU.mult).then_inc(u2r, 1)
                g.wait_ge(u2r, 2 * k + 1)
                g.wait_ge(uw, 2 * k + 2)
                g.tensor_tensor(u1[:, u], u1[:, u], u2[:, u], ALU.add).then_inc(u2r, 1)

        looped(g, NHC // 2, pair)

    def scalar(s):
        for n, h in enumerate(hs):
            s.wait_ge(lin, 2 * n + 2)
            s.activation(ke[:, h, :], ke[:, h, :], ACT.Exp).then_inc(expd, 1)
        for j in (3, 4):
            t = sm[4] if j == 3 else sm[3]
            s.wait_ge(sm_in, j - 2)
            s.activation(t, t, ACT.Sin, scale=-TWO_PI).then_inc(sm_out, 1)
        for n, h in enumerate(hs):
            for j, t in enumerate((re, im)):
                s.wait_ge(arg, 2 * n + j + 1)
                s.activation(t[:, h, :], t[:, h, :], ACT.Sin, scale=-TWO_PI).then_inc(sines, 1)

        def pair(i):
            for u in range(2):
                k = 2 * i + u
                if not is_first(i):
                    s.wait_ge(stored[u], 16 * TI * i)
                for b in range(2):
                    s.wait_ge(prod, 2 * k + b + 1)
                    s.activation(ob[:, u, b * QC:(b + 1) * QC], ps[:, 2 * u + b, :], ACT.Copy).then_inc(evac, 1)

        looped(s, NHC // 2, pair)

    def tensor(t):
        def pair(i):
            for u in range(2):
                k = 2 * i + u
                t.wait_ge(uw, 2 * k + 2)
                t.wait_ge(u2r, 2 * k + 2)
                for b in range(2):
                    if not is_first(i):
                        t.wait_ge(evac, 2 * (k - 2) + b + 1)
                    for h in range(8):
                        hh = 8 * b + h
                        o = ps[:, 2 * u + b, h * TJ:(h + 1) * TJ]
                        mm = t.matmul(o, u1[:, u, hh, :], bb[:, u, hh, :], start=True, stop=True)
                    mm.then_inc(prod, 1)

        looped(t, NHC // 2, pair)

    return sync, vector, gpsimd, scalar, tensor, all_stored


def tile_rows(t):
    return NB if isinstance(t, int) and t == T - 1 else P


def over_tiles(eng, body):
    def pair(i):
        for u in range(2):
            body(2 * i + u, u)

    looped(eng, NB // 2, pair)
    body(T - 1, 0)


def each_tile(body):
    for t in range(T):
        body(t, t % 2)


def early(t):
    return isinstance(t, int) and t < 2


class Norm:

    def __init__(self, arena, chain_sem):
        self.stats = arena.take(T, 6)
        self.mv = arena.take(T, 2)
        self.rstd = arena.take(T)
        self.half = arena.take(T, 2)
        self.sem = chain_sem
        self.count = 0

    def chain(self, v):
        return Chain(v, self.sem, self.count)

    def closed(self, c):
        self.count += c.n

    def take_stats(self, v, x, t):
        r = tile_rows(t)
        v.bn_stats(self.stats[0:r, t, :], x[0:r, t, :]).then_inc(self.sem, 1)

    def clear(self, v):
        c = self.chain(v)
        c.link(v.memset(self.mv, 1.0))
        self.closed(c)

    def solve(self, v, eps=LN_EPS):
        c = self.chain(v)
        c.n += T
        c.wait()
        for t in range(T):
            r = tile_rows(t)
            c.put(v.bn_aggr(self.mv[0:r, t, :], self.stats[0:r, t, :]))
        c.wait()
        self.newton(v, c, self.mv[:, :, 1], 1.0, eps)
        self.closed(c)

    NEWTON = 12

    def newton(self, v, c, var, scale, eps, cols=slice(0, T)):
        y, a, b = self.rstd[:, cols], self.half[:, cols, 0], self.half[:, cols, 1]
        c.link(v.tensor_scalar(b, var, scale, eps, ALU.mult, ALU.add))
        c.link(v.tensor_scalar(y.bitcast(I32), b.bitcast(I32), 1, None, ALU.arith_shift_right))
        c.link(v.tensor_scalar(y.bitcast(I32), y.bitcast(I32), -1.0, float(0x5F3759DF), ALU.mult, ALU.add))
        for _ in range(3):
            c.link(v.tensor_tensor(a, y, y, ALU.mult))
            c.link(v.scalar_tensor_tensor(out=a, in0=a, scalar=-0.5, in1=b, op0=ALU.mult, op1=ALU.mult))
            c.link(v.scalar_tensor_tensor(out=y, in0=a, scalar=1.5, in1=y, op0=ALU.add, op1=ALU.mult))

    def apply(self, v, out, x, t):
        r = tile_rows(t)
        return v.tensor_scalar(out[0:r, t, :], x[0:r, t, :], self.mv[0:r, t, 0:1], self.rstd[0:r, bass.ds(t, 1)],
                               ALU.subtract, ALU.mult)


TURN_BANKS = (0, 1, 6, 7)


def turn_tile(t_eng, ps_bank, xn, t, ident):
    r = tile_rows(t)
    for k in range(KD):
        ins = t_eng.transpose(ps_bank[:, k * r:(k + 1) * r], xn[0:r, t, k * P:(k + 1) * P], ident[0:r, 0:r])
    return ins


def turned_out(s_eng, ps_bank, xnT, t):
    r = tile_rows(t)
    dst = xnT[:, :, NCOL:NTOK] if r == NB else xnT[:, :, bass.ds(t * P, P)]
    return s_eng.activation(dst, ps_bank[:, 0:KD * r].rearrange("p (k n) -> p k n", k=KD), ACT.Copy)


def scan_layer(nc, sem, sb, ps, d, h0, tok_stored, g, at):
    a = Arena(sb, at)
    hb, xn, xnT, yb, ident, norm = g.h, g.xn, g.xnT, g.y, g.ident, g.norm
    win = a.take(KD, P)
    wd, wg = a.take(P), a.take(P)
    wout, gam, bet = a.take(D), a.take(D), a.take(D)
    zb, db, gb, hs = (a.take(NB, SEQ) for _ in range(4))
    ctd, tmp, minus = a.take(2, D), a.take(2, D), a.take(T)
    F = (lambda x: x.rearrange("p b s -> p (b s)"))
    zf, df, gf, hf = F(zb), F(db), F(gb), F(hs)
    NC, CW = 6, NTOK // 6
    HALF = P // 2

    y_solved = []
    h_in = [sem(f"h_loaded{q}") for q in range(NQ + 1)]
    wz, w_in, w_fb = sem("scan_zeroed"), sem("scan_weights_loaded"), sem("scan_block_weights_loaded")
    xr, turned, tev = sem("scan_xn_ready"), sem("scan_turned"), sem("scan_xnT_ready")
    zp, zr = sem("scan_z_products"), sem("scan_z_ready")
    op, dr, gr = sem("scan_gate_products"), sem("scan_delta_ready"), sem("scan_gate_ready")
    sc = sem("scan_states")
    outp, yr = sem("scan_out_products"), sem("scan_y_ready")
    hbr, hr, tch = sem("scan_h_plus_beta"), g.h_ready, sem("scan_scaled_y")
    ctr = sem("scan_centred_y")

    def chunks(eng, body):
        looped(eng, NC // 2, lambda i: (body(2 * i, 0), body(2 * i + 1, 1)))

    def sync(sp):
        tok_stored(sp)
        for q in range(NQ):
            sp.dma_start(hb[:, 4 * q:4 * q + 4, :], h0[4 * q:4 * q + 4].rearrange("b p d -> p b d")).then_inc(h_in[q], 16)
        sp.dma_start(hb[0:NB, NB, :], d["cls"]).then_inc(h_in[NQ], 16)
        sp.dma_start(ident, d["ident"]).then_inc(w_in, 16)
        for k in range(2):
            sp.dma_start(win[:, :, k * HALF:(k + 1) * HALF], d["W_in"].rearrange("(k p) n -> p k n", p=P)).then_inc(w_in, 16)
        sp.wait_ge(wz, 2)
        for k, w in enumerate((d["W_fwd"], d["W_bwd"])):
            s = slice(k * HALF, (k + 1) * HALF)
            sp.dma_start(wd[s, s], w[:, 0:HALF]).then_inc(w_fb, 16)
            sp.dma_start(wg[s, s], w[:, HALF:P]).then_inc(w_fb, 16)
        sp.dma_start(wout, d["W_out"]).then_inc(w_fb, 16)
        sp.dma_start(gam, d["gamma"].partition_broadcast(P)).then_inc(w_fb, 16)
        sp.dma_start(bet, d["beta"].partition_broadcast(P)).then_inc(w_fb, 16)

    def vector(v):
        v.wait_ge(h_in[0], 16)
        norm.clear(v)
        for q in range(NQ):
            v.wait_ge(h_in[q], 16)
            for t in range(4 * q, 4 * q + 4):
                norm.take_stats(v, hb, t)
        v.wait_ge(h_in[NQ], 16)
        norm.take_stats(v, hb, NB)
        norm.solve(v)
        over_tiles(v, lambda t, u: norm.apply(v, xn, hb, t).then_inc(xr, 1))

        def gates(c, u):
            v.wait_ge(op, c + 1)
            cols = bass.ds(c * CW, CW)
            v.tensor_tensor(gf[:, cols], ps[:, 6 + u, 0:CW], zf[:, cols], ALU.mult).then_inc(gr, 1)

        chunks(v, gates)
        v.wait_ge(gr, NC)
        v.wait_ge(wz, 4)
        v.tensor_tensor_scan(hf[0:HALF, :], df[0:HALF, :], gf[0:HALF, :], 0.0, ALU.mult, ALU.add).then_inc(sc, 1)
        v.tensor_tensor_scan(hf[HALF:P, ::-1], df[HALF:P, ::-1], gf[HALF:P, ::-1], 0.0, ALU.mult, ALU.add).then_inc(sc, 1)

        v.wait_ge(xr, T)

        def add(t, u):
            r = tile_rows(t)
            v.wait_ge(outp, t + 1)
            v.tensor_tensor(yb[0:r, t, :], ps[0:r, 2 + u, :], xn[0:r, t, :], ALU.add).then_inc(yr, 1)
            if not (isinstance(t, int) and t == 0):
                v.wait_ge(yr, t)
                norm.take_stats(v, yb, t - 1)

        over_tiles(v, add)
        v.wait_ge(yr, T)
        norm.take_stats(v, yb, T - 1)
        norm.solve(v)
        c = norm.chain(v)
        c.link(v.tensor_scalar(minus, norm.mv[:, :, 0], -1.0, None, ALU.mult))
        norm.closed(c)
        y_solved.append(norm.count)
        v.wait_ge(hbr, 2)

        def post(t, u):
            r = tile_rows(t)
            v.wait_ge(tch, t + 1)
            v.scalar_tensor_tensor(out=hb[0:r, t, :], in0=tmp[0:r, u], scalar=norm.rstd[0:r, bass.ds(t, 1)], in1=hb[0:r, t, :], op0=ALU.mult, op1=ALU.add).then_inc(hr, 1)
            if not (isinstance(t, int) and t == 0):
                v.wait_ge(hr, t)
                norm.take_stats(v, hb, t - 1)

        over_tiles(v, post)
        v.wait_ge(hr, T)
        norm.take_stats(v, hb, NB)

    def gpsimd(p):
        p.wait_ge(h_in[0], 16)
        p.memset(wd, 0.0).then_inc(wz, 1)
        p.memset(wg, 0.0).then_inc(wz, 1)
        p.wait_ge(dr, NC)
        p.memset(db[0:HALF, :, 0], 0.0).then_inc(wz, 1)
        p.memset(db[HALF:P, :, SEQ - 1], 0.0).then_inc(wz, 1)
        p.wait_ge(wz, 4)
        p.wait_ge(w_fb, 16 * 7)
        p.wait_ge(xr, T)
        p.tensor_tensor(hb[:, 0:NB, :], hb[:, 0:NB, :], bc(bet.unsqueeze(1), 1, NB), ALU.add).then_inc(hbr, 1)
        p.wait_ge(hbr, 1)
        p.tensor_tensor(hb[0:NB, NB, :], hb[0:NB, NB, :], bet[0:NB], ALU.add).then_inc(hbr, 1)

        def scaled(t, u):
            r = tile_rows(t)
            p.wait_ge(ctr, t + 1)
            if not early(t):
                p.wait_ge(hr, t - 1)
            p.tensor_tensor(tmp[0:r, u], ctd[0:r, u], gam[0:r], ALU.mult).then_inc(tch, 1)

        over_tiles(p, scaled)

    def scalar(s):
        for n in range(T):
            s.wait_ge(turned, n + 1)
            turned_out(s, ps[:, TURN_BANKS[n % 4], :], xnT, n).then_inc(tev, 1)
        for q in range(NQ):
            s.wait_ge(zp, q + 1)
            s.activation(zb[:, 4 * q:4 * q + 4, 1:SEQ], ps[:, 2 + q, :].rearrange("p (b n) -> p b n", b=4), ACT.Copy).then_inc(zr, 1)
        s.wait_ge(zp, NQ + 1)
        s.activation(zb[:, :, 0], ps[:, 6, 0:NB], ACT.Copy).then_inc(zr, 1)

        def deltas(c, u):
            s.wait_ge(op, c + 1)
            s.activation(df[:, bass.ds(c * CW, CW)], ps[:, 4 + u, 0:CW], ACT.Sigmoid).then_inc(dr, 1)

        chunks(s, deltas)
        s.wait_ge(norm.sem, y_solved[0])

        def centred(t, u):
            r = tile_rows(t)
            if not early(t):
                s.wait_ge(tch, t - 1)
            s.activation(ctd[0:r, u], yb[0:r, t, :], ACT.Identity, bias=minus[0:r, bass.ds(t, 1)]).then_inc(ctr, 1)

        over_tiles(s, centred)

    def tensor(t):
        t.wait_ge(w_in, 3 * 16)

        def project(cols, w, bank):
            for k in range(KD):
                mm = t.matmul(ps[:, bank, 0:w], win[:, k, :], xnT[:, k, cols], start=(k == 0), stop=(k == KD - 1))
            mm.then_inc(zp, 1)

        for n in range(T):
            t.wait_ge(xr, n + 1)
            if n >= 4:
                t.wait_ge(tev, n - 3)
            turn_tile(t, ps[:, TURN_BANKS[n % 4], :], xn, n, ident).then_inc(turned, 1)
            if n == 7:
                project(slice(0, QC), QC, 2)
        t.wait_ge(tev, T)
        for q in range(1, NQ):
            project(slice(q * QC, (q + 1) * QC), QC, 2 + q)
        project(slice(NCOL, NTOK), NB, 6)
        t.wait_ge(zr, NQ + 1)
        t.wait_ge(w_fb, 16 * 7)

        def gates(c, u):
            if not early(c):
                t.wait_ge(dr, c - 1)
                t.wait_ge(gr, c - 1)
            cols = bass.ds(c * CW, CW)
            t.matmul(ps[:, 4 + u, 0:CW], wd, zf[:, cols], start=True, stop=True)
            t.matmul(ps[:, 6 + u, 0:CW], wg, zf[:, cols], start=True, stop=True).then_inc(op, 1)

        chunks(t, gates)
        t.wait_ge(sc, 2)

        def outs(n, u):
            if not early(n):
                t.wait_ge(yr, n - 1)
            r = tile_rows(n)
            lhs = hs[:, :, 0] if r == NB else hs[:, n, 1:SEQ]
            t.matmul(ps[0:r, 2 + u, :], lhs, wout, start=True, stop=True).then_inc(outp, 1)

        each_tile(outs)

    return sync, vector, gpsimd, scalar, tensor


NE = 8
NTILE = (2 * NTOK + NE * (P - 1)) // P
NSLOT = NTILE * P
CHOICE = NTOK
SPARE = 2 * CHOICE


SF = P
NU = NQ + 1


def ffn_layer(nc, sem, sb, ps, d, dram, g, name, F, NSH, stats_after, before):
    hb, ident, norm = g.h, g.ident, g.norm
    xn = Arena(g.low).take(T, D)
    NF = -(-F // P)
    FR = [min(P, F - P * f) for f in range(NF)]
    GW, DW = KD * 2 * F, NF * D
    EW = GW + DW
    SGW = KD * 2 * SF
    ex = g.experts[:, 0:NE * EW].rearrange("p (e w) -> p e w", e=NE)
    exg, exd = (lambda e, k, j, w: ex[:, e, k * 2 * F + j:k * 2 * F + j + w]), (lambda e, f, r: ex[0:r, e, GW + f * D:GW + (f + 1) * D])
    r = Arena(g.rounded, g.y_at, g.y_at)
    xnL = r.take(KD, NTOK)
    wrh, wrl = r.take(KD, NE + 1), r.take(KD, NE + 1)
    r.at = g.scratch_at - KD * NTOK
    xnT = r.take(KD, NTOK)
    whl = r.take(2, 2, SGW + D)
    hid, hidc = r.take(2, 2, QC), r.take(2, NB)
    assert r.at == g.high_at
    w = Arena(g.high, g.high_at, g.high_at)
    wraw = w.take(SGW + D)
    scT = g.high[0:NE + 1, w.at - g.high_at:w.at - g.high_at + NTOK]
    sil, silc = w.take(2, QC), w.take(NB)
    b = Arena(g.high, max(g.xn_at + NE * EW, g.high_at), g.high_at)
    xgT, esil, ehid, ehT = b.take(2, KD, P), b.take(2, F), b.take(2, F), b.take(2, NF, P)
    a = Arena(g.high, max(b.at, w.at - 2 * QC - NB + NTOK), g.high_at)
    ey = a.take(2, D)
    xg = a.take(2, D)
    wr = a.take(KD, NE + 1)
    lg, oh0, oh1, t8, mm8 = (a.take(T, NE) for _ in range(5))
    sg, m1, m2, wt = a.take(T), a.take(T), a.take(T), a.take(2, T)
    iota, iot, valid = a.take(NE), a.take(NTILE), a.take(T)
    tri, ones = xg[:, 0, 0:P], xg[:, 0, P:2 * P]
    cnt, base, incl, one8 = (a.take(NE) for _ in range(4))
    cni = a.take(NE, dt=I32)
    slot_u, pos_u, tmp_u = a.take(2, T, dt=U32), a.take(2, T, dt=U32), a.take(T, dt=U32)
    tok_u, idx_u, spare_u = a.take(2, T, dt=U32), a.take(NTILE, dt=U32), a.take(NTILE, dt=U32)
    cmp = Arena(g.high, w.at, g.high_at).take(NTILE * NE).rearrange("p (t e) -> p t e", e=NE)
    etab = a.take(NTILE)
    eti = a.take(NTILE, dt=I32)
    xd, slots, yd = dram["xn"], dram["slots"], dram["expert_out"]

    xr, turned, tev = sem(name + "_xn_ready"), sem(name + "_turned"), sem(name + "_xnT_ready")
    r_in, rp, sgm = sem(name + "_router_loaded"), sem(name + "_scores_and_ranks"), sem(name + "_sigmoids")
    w_in, whr, wlr = sem(name + "_weights_loaded"), sem(name + "_weights_hi"), sem(name + "_weights_lo")
    wrr, xl, scp, scr = sem(name + "_router_split"), sem(name + "_xnT_lo_ready"), sem(name + "_scoresT"), sem(name + "_scoresT_ready")
    gu, silr, mulr = sem(name + "_gate_up"), sem(name + "_silu"), sem(name + "_hidden_raw")
    hir, hidr = sem(name + "_hidden_hi"), sem(name + "_hidden_lo")
    dn, acc = sem(name + "_down"), sem(name + "_added")
    WD = 1 + (1 if FR[-1] == P else 2)
    DIFFERENCES, CHOICES, ROUTED = 1, 2, 3
    zs, xs, rt, scat, ix = sem(name + "_slots_cleared"), sem(name + "_xn_stored"), sem(name + "_routed"), sem(name + "_slots_filled"), sem(name + "_slots_loaded")
    e_in = [sem(f"{name}_experts_loaded{k}") for k in range(NE // 2)]
    g_in = [sem(f"{name}_rows_gathered{u}") for u in range(2)]
    tx, txr = sem(name + "_rows_turned"), sem(name + "_rowsT_ready")
    eg, esr, ehr = sem(name + "_e_gate_up"), sem(name + "_e_silu"), sem(name + "_e_hidden")
    th, thr = sem(name + "_e_hidden_turned"), sem(name + "_e_hiddenT_ready")
    ed, eyr = sem(name + "_e_down"), sem(name + "_e_out_ready")
    yst = [sem(f"{name}_e_out_stored{u}") for u in range(2)]
    cg = [(sem(f"{name}_out_gathered{u}"), 0) for u in range(2)] + [(w_in, 32 * NSH), (xs, 5 * 16)]
    cadd = sem(name + "_combined")

    def load_block(sp, name2, dst_g, dst_d, b, s):
        sp.dma_start(dst_g, d[name2 + "_gate_up"][b].rearrange("p k f -> p (k f)")).then_inc(s, 16)
        full = NF if FR[-1] == P else NF - 1
        sp.dma_start(dst_d(slice(0, P), 0, full), d[name2 + "_down"][b, 0:full * P, :].rearrange("(f p) n -> p f n", p=P)).then_inc(s, 16)
        if full < NF:
            sp.dma_start(dst_d(slice(0, FR[-1]), full, NF), d[name2 + "_down"][b, full * P:F, :].unsqueeze(1)).then_inc(s, 16)

    def load_expert(sp, e, s):
        load_block(sp, name, ex[:, e, 0:GW], lambda r, f0, f1: ex[r, e, GW + f0 * D:GW + f1 * D].rearrange("p (f n) -> p f n", n=D), e, s)

    def sync(sp):
        before(sp)
        sp.dma_start(wr, d[name + "_router"]).then_inc(r_in, 16)
        for dst, src in ((iota, d["iota8"]), (iot, d["iota_tiles"])):
            sp.dma_start(dst, src.partition_broadcast(P)).then_inc(r_in, 16)
        for dst, src in ((valid, d["valid"]), (tri, d["before"]), (ones, d["ones"])):
            sp.dma_start(dst, src).then_inc(r_in, 16)
        sp.dma_start(tok_u, d["token_ids"].bitcast(U32)).then_inc(r_in, 16)

        def shared(b):
            sp.dma_start(wraw[:, 0:SGW], d[name + "_sh_gate_up"][b].rearrange("p k f -> p (k f)")).then_inc(w_in, 16)
            sp.dma_start(wraw[:, SGW:], d[name + "_sh_down"][b]).then_inc(w_in, 16)

        shared(0)
        sp.wait_ge(zs, 1)
        sp.dma_start(slots.rearrange("(p t) o -> p (t o)", t=NTILE), spare_u).then_inc(zs, 16)
        sp.wait_ge(xr, T)
        sp.dma_start(xd[0:NCOL, :].rearrange("(t p) n -> p t n", p=P), xn[:, 0:NB, :]).then_inc(xs, 16)
        sp.dma_start(xd[NCOL:NTOK, :], xn[0:NB, NB, :]).then_inc(xs, 16)
        sp.wait_ge(wlr, 1)
        sp.wait_ge(whr, 1)
        shared(1)
        sp.dma_start(xd[CHOICE:CHOICE + NCOL, :].rearrange("(t p) n -> p t n", p=P), xn[:, 0:NB, :]).then_inc(xs, 16)
        sp.dma_start(xd[CHOICE + NCOL:CHOICE + NTOK, :], xn[0:NB, NB, :]).then_inc(xs, 16)
        sp.dma_start(xd[SPARE:SPARE + 1, :], xn[0:1, 0, :]).then_inc(xs, 16)
        sp.wait_ge(xs, 5 * 16)
        sp.wait_ge(turned, T)
        for e in range(2):
            load_expert(sp, e, e_in[0])
        sp.wait_ge(wlr, 2)
        sp.wait_ge(whr, 2)
        shared(2)
        sp.wait_ge(scat, 2 * T * 16)
        sp.dma_start(idx_u, slots.rearrange("(p t) o -> p (t o)", t=NTILE)).then_inc(ix, 16)

        def more(b):
            sp.wait_ge(wlr, b)
            sp.wait_ge(whr, b)
            shared(b)

        with sp.Fori(3, NSH) as b:
            more(b)
        sp.wait_ge(e_in[0], 2 * 16 * WD)
        sp.sem_inc(rt, 1)
        sp.wait_ge(dn, NSH * T)
        for e in range(2, NE):
            load_expert(sp, e, e_in[e // 2])
        for k in range(1, NE // 2):
            sp.wait_ge(e_in[k], 2 * 16 * WD)
            sp.sem_inc(rt, 1)

        for u in range(2):
            sp.wait_ge(yst[u], 16 * (NTILE // 2))
        sp.wait_ge(ed, NTILE)
        for i in range(NB // 2 + 1):
            if i >= CS:
                sp.wait_ge(cadd, 4 * (i - CS) + 4)
            for j in range(2):
                first = j * CHOICE + 2 * i * P
                if i < NB // 2:
                    src = yd[first:first + 2 * P, :].rearrange("(t p) n -> p t n", p=P)
                    sp.dma_start(cy[:, i % CS, :, j], src).then_inc(cg[i % CS][0], 16)
                else:
                    sp.dma_start(cy[0:NB, i % CS, 0, j], yd[first:first + NB, :]).then_inc(cg[i % CS][0], 16)

    def blocks(eng, body):
        pairs = (NSH - 2) // 2
        body(0, 0)
        with eng.Fori(0, pairs) as i:
            body(2 * i + 1, 1)
            body(2 * i + 2, 0)
        for b in range(2 * pairs + 1, NSH):
            body(b, b % 2)

    ACT_STEPS = [("silu", 0), ("silu", 1), ("hi", 0), ("hi", 1), ("silu", 2), ("hi", 2), ("split", 0),
                 ("silu", 3), ("hi", 3), ("silu", 4), ("hi", 4)]
    DVE_STEPS = [("early", 4), ("mul", 0), ("mul", 1), ("late", 4), ("lo", 0), ("lo", 1), ("early", 1), ("mul", 2), ("late", 1),
                 ("lo", 2), ("early", 2), ("split", 0), ("mul", 3), ("late", 2), ("lo", 3), ("early", 3), ("mul", 4), ("late", 3), ("lo", 4)]

    def score_bank(q):
        return 4 + q if q < NQ else 2

    def unit_cols(m):
        return (slice(NCOL, NTOK), NB) if m == 0 else (slice((m - 1) * QC, m * QC), QC)

    def unit_tiles(m, late=None):
        tiles = list(range(4 * (m - 1), 4 * m)) + ([NB] if m == 1 else [])
        return tiles if late is None else tiles[2:] if late else tiles[:2]

    def unit_rank(tile):
        return 4 if tile == NB else tile + (tile > 3)

    def unit_banks(m):
        if m == 0:
            return ps[:, 7, 0:NB], ps[:, 7, NB:2 * NB]
        p = 2 * ((m - 1) % 2)
        return ps[:, p, :], ps[:, p + 1, :]

    def unit_sil(m):
        return silc if m == 0 else sil[:, m % 2]

    def unit_hid(m, part):
        return hidc[:, part] if m == 0 else hid[:, m % 2, part]

    def unit_before(b, m):
        return b * NU + (m - 1 if m >= 3 else (1 - NU, -1, 0)[m])

    def is_last(b):
        return isinstance(b, int) and b == NSH - 1

    def vector(v):
        norm.solve(v)

        def lo(t, u):
            v.wait_ge(tev, t + 1)
            r = tile_rows(t)
            src = ps[:, u, 0:KD * r].rearrange("p (k n) -> p k n", k=KD)
            cols = slice(NCOL, NTOK) if r == NB else bass.ds(t * P, P)
            v.tensor_tensor(xnL[:, :, cols], src, xnT[:, :, cols], ALU.subtract).then_inc(xl, 1)

        def ready(t):
            norm.apply(v, xn, hb, t).then_inc(xr, 1)

        for t in range(3):
            ready(t)

        def quarter(q):
            for j in range(4):
                ready(4 * q + j + 3)
                lo(4 * q + j, j)
            if is_first(q):
                v.wait_ge(r_in, 7 * 16)
                v.wait_ge(wrr, 1)
                v.tensor_tensor(wrl, wr, wrh, ALU.subtract).then_inc(wrr, 1)

        looped(v, NQ - 1, quarter)
        ready(NB - 1)
        lo(NB - 4, 0)
        ready(NB)
        for j in range(1, 5):
            lo(NB - 4 + j, j % 4)

        def split(b, u):
            v.wait_ge(whr, b + 1)
            v.tensor_tensor(whl[:, u, 1], wraw, whl[:, u, 0], ALU.subtract).then_inc(wlr, 1)

        split(0, 0)
        c = norm.chain(v)
        c.link(v.memset(lg, 0.0))
        c.put(v.memset(sg, 0.0))
        v.memset(spare_u, SPARE).then_inc(zs, 1)
        v.wait_ge(rp, T)
        s3 = ps[:, 3, 0:T * 16].rearrange("p (t e) -> p t e", e=16)
        c.put(v.tensor_copy(lg[:, 0:NB, :], s3[:, 0:NB, 0:NE]))
        c.put(v.tensor_copy(lg[0:NB, NB, :], s3[0:NB, NB, 0:NE]))
        c.wait()
        c.put(v.tensor_copy(sg[:, 0:NB], s3[:, 0:NB, NE]))
        c.link(v.tensor_copy(sg[0:NB, NB:T], s3[0:NB, NB, NE:NE + 1]))
        io = bc(iota.unsqueeze(1), 1, T)
        wide = (lambda x: bc(x.unsqueeze(2), 2, NE))
        for m, oh in ((m1, oh0), (m2, oh1)):
            c.link(v.tensor_reduce(m, lg, AX.X, ALU.max))
            c.link(v.tensor_tensor(t8, lg, wide(m), ALU.is_ge))
            c.link(v.scalar_tensor_tensor(out=t8, in0=t8, scalar=-16.0, in1=io, op0=ALU.mult, op1=ALU.add))
            c.link(v.tensor_reduce(wt[:, 0, :], t8, AX.X, ALU.min))
            c.link(v.tensor_tensor(oh, t8, wide(wt[:, 0, :]), ALU.is_equal))
            c.link(v.scalar_tensor_tensor(out=lg, in0=oh, scalar=-3.0e38, in1=lg, op0=ALU.mult, op1=ALU.add))
        c.link(v.tensor_tensor(wt[:, 0, :], m1, m2, ALU.subtract))
        v.tensor_tensor(wt[:, 1, :], m2, m1, ALU.subtract).then_inc(rt, 1)
        for oh in (oh0, oh1):
            c.put(v.tensor_tensor(oh, oh, wide(valid), ALU.mult))
        c.wait()
        v.tensor_tensor(mm8, oh0, oh1, ALU.add).then_inc(rt, 1)
        anew = t8.rearrange("p t e -> p (t e)").rearrange("p (e t) -> p e t", e=NE)
        upto = lg.rearrange("p t e -> p (t e)").rearrange("p (e t) -> p e t", e=NE)
        c.link(v.memset(anew, 1.0))
        c.put(v.memset(anew[:, :, 0], 0.0))
        c.link(v.memset(one8, 1.0))
        v.wait_ge(rp, T + 1)
        in_tile = ps[:, 6, 256:256 + T * NE].rearrange("p (e t) -> p e t", e=NE)
        c.link(v.tensor_tensor_scan(upto.rearrange("p e t -> p (e t)"), anew.rearrange("p e t -> p (e t)"), ps[:, 6, 256:256 + T * NE], 0.0, ALU.mult, ALU.add))
        c.link(v.tensor_scalar(cni, upto[:, :, T - 1], float(P - 1), None, ALU.add))
        c.link(v.tensor_scalar(cni, cni, 7, None, ALU.arith_shift_right))
        c.link(v.tensor_copy(cnt, cni))
        c.link(v.tensor_tensor_scan(incl, one8, cnt, 0.0, ALU.mult, ALU.add))
        c.link(v.tensor_tensor(base, incl, cnt, ALU.subtract))
        c.link(v.tensor_scalar(base, base, float(P), None, ALU.mult))
        c.link(v.tensor_tensor(upto, upto, in_tile, ALU.subtract))
        c.link(v.tensor_tensor(upto, upto, bc(base.unsqueeze(2), 2, T), ALU.add))
        c.link(v.tensor_tensor(mm8, ps[:, 6, 64:64 + T * NE].rearrange("p (t e) -> p t e", e=NE), upto.rearrange("p e t -> p t e"), ALU.add))
        for j, oh in enumerate((oh0, oh1)):
            c.link(v.tensor_tensor(t8, oh, mm8, ALU.mult))
            c.link(v.tensor_reduce(m1, t8, AX.X, ALU.add))
            c.link(v.tensor_copy(slot_u[:, j], m1))
            c.link(v.tensor_scalar(tmp_u, slot_u[:, j], P - 1, None, ALU.bitwise_and))
            c.link(v.tensor_scalar(pos_u[:, j], slot_u[:, j], 7, None, ALU.logical_shift_right))
            c.link(v.scalar_tensor_tensor(out=pos_u[:, j], in0=tmp_u, scalar=float(NTILE), in1=pos_u[:, j], op0=ALU.mult, op1=ALU.add))
        c.link(v.tensor_tensor(cmp, bc(iot.unsqueeze(2), 2, NE), bc(incl.unsqueeze(1), 1, NTILE), ALU.is_ge))
        c.link(v.tensor_reduce(etab, cmp, AX.X, ALU.add))
        v.tensor_scalar(eti, etab, float(NE - 1), None, ALU.min).then_inc(rt, 1)
        norm.closed(c)
        v.wait_ge(sgm, 2)

        def block(b, u):
            for what, m in DVE_STEPS:
                if what == "mul":
                    v.wait_ge(silr, b * NU + m + 1)
                    v.tensor_tensor(unit_sil(m), unit_sil(m), unit_banks(m)[1], ALU.mult).then_inc(mulr, 1)
                elif what == "lo":
                    v.wait_ge(hir, b * NU + m + 1)
                    v.tensor_tensor(unit_hid(m, 1), unit_sil(m), unit_hid(m, 0), ALU.subtract).then_inc(hidr, 1)
                elif what == "split":
                    if not is_last(b):
                        split(b + 1, 1 - u)
                elif m < NU - 1:
                    adds(b, m, unit_tiles(m, what == "late"))
                elif not is_first(b):
                    adds(b - 1, m, unit_tiles(m, what == "late"))

        def adds(b, m, tiles):
            for t in tiles:
                rows, r = tile_rows(t), unit_rank(t)
                v.wait_ge(dn, b * T + r + 1)
                if not is_first(b):
                    v.wait_ge(acc, b * T + r + 1 - (T - 4 if m == NU - 1 else T))
                v.scalar_tensor_tensor(out=hb[0:rows, t, :], in0=ps[0:rows, 4 + r % 3, :], scalar=sg[0:rows, t:t + 1],
                                       in1=hb[0:rows, t, :], op0=ALU.mult, op1=ALU.add).then_inc(acc, 1)

        blocks(v, block)
        adds(NSH - 1, NU - 1, unit_tiles(NU - 1))

        def hidden(t, u):
            v.wait_ge(esr, t + 1)
            if not early(t):
                v.wait_ge(th, t - 1)
            v.tensor_tensor(ehid[:, u], esil[:, u], e_up(u), ALU.mult).then_inc(ehr, 1)

        def out_rows(t, u):
            v.wait_ge(ed, t + 1)
            if not early(t):
                v.wait_ge(yst[u], 16 * halves(t))
            v.tensor_copy(ey[:, u], ps[:, 6 + u, :]).then_inc(eyr, 1)

        def hidden_turned(t, u):
            v.wait_ge(th, t + 1)
            if not early(t):
                v.wait_ge(ed, t - 1)
            for f in range(NF):
                ins = v.tensor_copy(ehT[0:FR[f], u, f, :], ps[0:FR[f], 5, f * P:(f + 1) * P])
            ins.then_inc(thr, 1)

        hidden(0, 0)
        hidden_turned(0, 0)
        tiles_1_on(v, lambda t, u: (hidden(t, u), out_rows(t - 1, 1 - u), hidden_turned(t, u)))
        hidden(NTILE - 1, 1)
        out_rows(NTILE - 2, 0)
        hidden_turned(NTILE - 1, 1)
        out_rows(NTILE - 1, 1)

        v.wait_ge(acc, T * NSH)

        def combine(t):
            r, u = tile_rows(t), t // 2 % CS
            v.wait_ge(cg[u][0], cg[u][1] + 32 * (t // 2 // CS + 1))
            v.scalar_tensor_tensor(out=hb[0:r, t, :], in0=cy[0:r, u, t % 2, 0], scalar=wt[0:r, 0, t:t + 1], in1=hb[0:r, t, :], op0=ALU.mult, op1=ALU.add).then_inc(cadd, 1)
            v.wait_ge(cadd, 2 * t + 1)
            if stats_after and t:
                norm.take_stats(v, hb, t - 1)
            v.scalar_tensor_tensor(out=hb[0:r, t, :], in0=cy[0:r, u, t % 2, 1], scalar=wt[0:r, 1, t:t + 1], in1=hb[0:r, t, :], op0=ALU.mult, op1=ALU.add).then_inc(cadd, 1)

        for t in range(T):
            combine(t)
        if stats_after:
            v.wait_ge(cadd, 2 * T)
            norm.take_stats(v, hb, T - 1)

    def halves(t):
        return t // 2

    CS = 4
    cy = Arena(g.low).take(CS, 2, 2, D)
    LAG = 4

    def e_up(u):
        return ps[:, u, F:2 * F] if 2 * F <= QC else ps[:, 2 * u + 1, 0:F]

    def e_gate(u):
        return ps[:, u, 0:F] if 2 * F <= QC else ps[:, 2 * u, 0:F]

    def tiles_1_on(eng, body):
        def pair(i):
            for u in range(2):
                body(2 * i + 1 + u, 1 - u)

        looped(eng, NTILE // 2 - 1, pair)

    def gpsimd(p):
        p.wait_ge(rt, ROUTED)
        p.wait_ge(zs, 17)

        def scatter(t, u):
            r = tile_rows(t)
            for j in range(2):
                p.indirect_dma_start(out=slots, out_offset=bass.IndirectOffsetOnAxis(ap=pos_u[0:r, j, t:t + 1], axis=0),
                                     in_=tok_u[0:r, j, t:t + 1], in_offset=None).then_inc(scat, 16)

        each_tile(scatter)
        p.wait_ge(xs, 5 * 16)
        p.wait_ge(ix, 16)
        p.wait_ge(rp, T + 1)

        for t in range(NTILE + LAG):
            if t < NTILE:
                if t >= 2:
                    p.wait_ge(tx, t - 1)
                p.indirect_dma_start(out=xg[:, t % 2], out_offset=None, in_=xd,
                                     in_offset=bass.IndirectOffsetOnAxis(ap=idx_u[:, t:t + 1], axis=0)).then_inc(g_in[t % 2], 16)
            if t >= LAG:
                o = t - LAG
                p.wait_ge(eyr, o + 1)
                if o:
                    p.wait_ge(yst[1 - o % 2], 16 * ((o + 1) // 2))
                p.indirect_dma_start(out=yd, out_offset=bass.IndirectOffsetOnAxis(ap=idx_u[:, o:o + 1], axis=0),
                                     in_=ey[:, o % 2], in_offset=None).then_inc(yst[o % 2], 16)

    def scalar(s):
        def turn(t, u):
            s.wait_ge(turned, t + 1)
            turned_out(s, ps[:, u, :], xnT, t).then_inc(tev, 1)

        def split(b, u):
            s.wait_ge(w_in, 32 * (b + 1))
            if not (isinstance(b, int) and b < 2):
                s.wait_ge(dn, b * T - T)
            s.activation(whl[:, u, 0], wraw, ACT.Copy).then_inc(whr, 1)


        def quarter(q):
            for j in range(4):
                turn(4 * q + j, j)
            if is_first(q):
                s.wait_ge(r_in, 7 * 16)
                s.activation(wrh, wr, ACT.Copy).then_inc(wrr, 1)

        looped(s, NQ, quarter)
        turn(NB, 0)
        split(0, 0)

        for q in range(NU):
            s.wait_ge(scp, q + 1)
            cols, w = (slice(NCOL, NTOK), NB) if q == NQ else (slice(q * QC, (q + 1) * QC), QC)
            s.activation(scT[:, cols], ps[0:NE + 1, score_bank(q), 0:w], ACT.Copy).then_inc(scr, 1)
        s.wait_ge(rt, DIFFERENCES)
        s.activation(wt, wt, ACT.Sigmoid).then_inc(sgm, 1)
        s.activation(sg, sg, ACT.Sigmoid).then_inc(sgm, 1)

        def block(b, u):
            for what, m in ACT_STEPS:
                if what == "silu":
                    s.wait_ge(gu, b * NU + m + 1)
                    if not (is_first(b) and m < 3):
                        s.wait_ge(hidr, unit_before(b, m))
                    s.activation(unit_sil(m), unit_banks(m)[0], ACT.Silu).then_inc(silr, 1)
                elif what == "hi":
                    s.wait_ge(mulr, b * NU + m + 1)
                    if not (is_first(b) and m < 3):
                        s.wait_ge(dn, b * T + (unit_rank(unit_tiles(m - 2)[3]) + 1 if m >= 3 else (5 - T, 13 - T, 0)[m]))
                    s.activation(unit_hid(m, 0), unit_sil(m), ACT.Copy).then_inc(hir, 1)
                elif not is_last(b):
                    split(b + 1, 1 - u)

        blocks(s, block)

        def rows_turned(t, u):
            s.wait_ge(tx, t + 1)
            if not early(t):
                s.wait_ge(eg, t - 1)
            s.activation(xgT[:, u].rearrange("p k n -> p (k n)"), ps[:, 4, :], ACT.Copy).then_inc(txr, 1)

        def silu(t, u):
            s.wait_ge(eg, t + 1)
            if not early(t):
                s.wait_ge(ehr, t - 1)
            s.activation(esil[:, u], e_gate(u), ACT.Silu).then_inc(esr, 1)

        rows_turned(0, 0)
        silu(0, 0)
        rows_turned(1, 1)
        tiles_1_on(s, lambda t, u: (silu(t, u), rows_turned(t + 1, 1 - u)))
        silu(NTILE - 1, 1)

    def tensor(t):
        def split_products(out, lhs, rhs, ks):
            for k in range(ks):
                for i, (x, y) in enumerate(((0, 0), (0, 1), (1, 0))):
                    mm = t.matmul(out, lhs(k, x), rhs(k, y), start=(k == 0 and i == 0),
                                  stop=(k == ks - 1 and i == 2))
            return mm

        xT = (xnT, xnL)
        wrs = (wrh, wrl)

        def scores(q):
            cols, w = (slice(NCOL, NTOK), NB) if q == NQ else (slice(q * QC, (q + 1) * QC), QC)
            split_products(ps[0:NE + 1, score_bank(q), 0:w], lambda k, p: wrs[p][:, k, :], lambda k, p: xT[p][:, k, cols], KD).then_inc(scp, 1)

        for n in range(T):
            t.wait_ge(xr, n + 1)
            if n >= 4:
                t.wait_ge(tev, n - 3)
                t.wait_ge(xl, n - 3)
            turn_tile(t, ps[:, n % 4, :], xn, n, ident).then_inc(turned, 1)
            if n == 7:
                t.wait_ge(wrr, 2)
            if n % 4 == 3 and n > 4:
                scores((n - 7) // 4)
        t.wait_ge(tev, T)
        t.wait_ge(xl, T)
        for q in range(NQ - 1, NU):
            scores(q)
        for n in range(T):
            r = tile_rows(n)
            t.wait_ge(scr, n // 4 + 1)
            cols = slice(NCOL, NTOK) if r == NB else slice(n * P, (n + 1) * P)
            t.transpose(ps[0:r, 3, 16 * n:16 * n + NE + 1], scT[:, cols], ident[0:NE + 1, 0:NE + 1]).then_inc(rp, 1)

        def ranks():
            t.wait_ge(rt, CHOICES)
            t.matmul(ps[:, 6, 64:64 + T * NE], tri, mm8.rearrange("p t e -> p (t e)"), start=True, stop=True)
            t.matmul(ps[:, 6, 256:256 + T * NE], ones, mm8.rearrange("p t e -> p e t"), start=True, stop=True).then_inc(rp, 1)

        PARTS = ((0, 0), (0, 1), (1, 0))

        def block(b, u):
            def weights(k, p, j):
                return whl[:, u, p, k * 2 * SF + j * SF:k * 2 * SF + (j + 1) * SF]

            t.wait_ge(wlr, b + 1)
            t.wait_ge(whr, b + 1)
            for m in range(1, NU):
                units = (0, 1) if m == 1 else (m,)
                for x in units:
                    if not (is_first(b) and x < 3):
                        t.wait_ge(mulr, unit_before(b, x))
                if m > 1:
                    before = [(b, u, tile) for tile in unit_tiles(m - 1)]
                elif is_first(b):
                    before = []
                else:
                    before = [(b - 1, 1 - u, tile) for tile in unit_tiles(NU - 1)]
                step = 0
                for j in range(2):
                    for k in range(KD):
                        for i, (x, y) in enumerate(PARTS):
                            for unit in units:
                                mm = t.matmul(unit_banks(unit)[j], weights(k, x, j), xT[y][:, k, unit_cols(unit)[0]],
                                              start=(k == 0 and i == 0), stop=(k == KD - 1 and i == 2))
                                if j == 1 and k == KD - 1 and i == 2:
                                    mm.then_inc(gu, 1)
                            step += 1
                            if before and step in (16, 20):
                                down(*before.pop(0))
                for args in before:
                    down(*args)
                if m == 1 and is_first(b):
                    ranks()

        def down(b, u, tile):
            rows, r = tile_rows(tile), unit_rank(tile)
            m = 0 if tile == NB else tile // 4 + 1
            j = 0 if tile == NB else tile % 4
            if j == 0:
                t.wait_ge(hidr, b * NU + m + 1)
            if r >= 3:
                t.wait_ge(acc, b * T + r - 2)
            elif not is_first(b):
                t.wait_ge(acc, b * T - (1, 0, 2)[r])
            split_products(ps[0:rows, 4 + r % 3, :], lambda k, p: unit_hid(m, p)[:, j * P:j * P + rows],
                           lambda k, p: whl[:, u, p, SGW:], 1).then_inc(dn, 1)

        blocks(t, block)
        for tile in unit_tiles(NU - 1):
            down(NSH - 1, (NSH - 1) % 2, tile)

        def turn_rows(n, u):
            t.wait_ge(g_in[u], 16 * (halves(n) + 1))
            if not (isinstance(n, int) and n == 0):
                t.wait_ge(txr, n)
            for k in range(KD):
                ins = t.transpose(ps[:, 4, k * P:(k + 1) * P], xg[:, u, k * P:(k + 1) * P], ident)
            ins.then_inc(tx, 1)

        def gate_up(n, u):
            e = t.value_load(eti[0:1, bass.ds(n, 1)], min_val=0, max_val=NE - 1)
            t.wait_ge(rt, e // 2 + ROUTED + 1)
            t.wait_ge(txr, n + 1)
            if not early(n):
                t.wait_ge(ehr, n - 1)
            if 2 * F <= QC:
                for k in range(KD):
                    mm = t.matmul(ps[:, u, 0:2 * F], xgT[:, u, k], exg(e, k, 0, 2 * F), start=(k == 0), stop=(k == KD - 1))
            else:
                for j in range(2):
                    for k in range(KD):
                        mm = t.matmul(ps[:, 2 * u + j, 0:F], xgT[:, u, k], exg(e, k, j * F, F), start=(k == 0), stop=(k == KD - 1))
            mm.then_inc(eg, 1)

        def turn_hidden(n, u):
            t.wait_ge(ehr, n + 1)
            if not (isinstance(n, int) and n == 0):
                t.wait_ge(thr, n)
            for f in range(NF):
                ins = t.transpose(ps[0:FR[f], 5, f * P:(f + 1) * P], ehid[:, u, f * P:f * P + FR[f]], ident)
            ins.then_inc(th, 1)

        def expert_down(n, u):
            e = t.value_load(eti[0:1, bass.ds(n, 1)], min_val=0, max_val=NE - 1)
            t.wait_ge(thr, n + 1)
            if not early(n):
                t.wait_ge(eyr, n - 1)
            for f in range(NF):
                mm = t.matmul(ps[:, 6 + u, :], ehT[0:FR[f], u, f, :], exd(e, f, FR[f]), start=(f == 0), stop=(f == NF - 1))
            mm.then_inc(ed, 1)

        t.wait_ge(acc, NSH * T)
        turn_rows(0, 0)
        gate_up(0, 0)
        turn_rows(1, 1)
        turn_hidden(0, 0)

        def body(n, u):
            gate_up(n, u)
            turn_rows(n + 1, 1 - u)
            expert_down(n - 1, 1 - u)
            turn_hidden(n, u)

        tiles_1_on(t, body)
        gate_up(NTILE - 1, 1)
        expert_down(NTILE - 2, 0)
        turn_hidden(NTILE - 1, 1)
        expert_down(NTILE - 1, 1)

    return sync, vector, gpsimd, scalar, tensor, cadd, ed


def gla_layer(nc, sem, sb, ps, d, g, at, before):
    a = Arena(sb, at)
    hb, xn, xnT, ident, norm = g.h, g.xn, g.xnT, g.ident, g.norm
    KH, BL, NBL = 32, 32, 4
    wqk, wog, wig = a.take(KD, 2 * KH), a.take(KD, D), a.take(KD, D)
    gw, mask = a.take(D), a.take(P)
    ats, ots = a.take(2, P), a.take(2, KD, P)
    atc = a.take(NB, NH, rows=NB)
    sg, pb, junk = a.take(2, D), a.take(2, D), a.take(D)
    ss = a.take(T)
    qs, kb3, = (a.take(NB, SEQ, rows=KH) for _ in range(2))
    b = Arena(sb, g.y_at)
    kb0, kb1, kb2, pv = (b.take(NB, SEQ, rows=KH) for _ in range(4))
    av, bv = kb2, kb1
    sq = a.take(NB, SEQ, rows=KH)
    kb = [kb0, kb1, kb2, kb3]
    F = (lambda x: x.rearrange("p b s -> p (b s)"))

    w_in = sem("gla_weights_loaded")
    xr, turned, tev = sem("gla_xn_ready"), sem("gla_turned"), sem("gla_xnT_ready")
    qk, qsig, ksig, asig, qkr = sem("gla_qk_products"), sem("gla_q_sigmoid"), sem("gla_k_ready"), sem("gla_a_ready"), sem("gla_q_ready")
    kbr, cp = sem("gla_keys_scaled"), sem("gla_keys_copied")
    acp, atcr = sem("gla_cls_products"), sem("gla_cls_attention")
    ap, atr, ob, otr, ssr = sem("gla_attention_products"), sem("gla_attention_masked"), sem("gla_o_products"), sem("gla_oT_ready"), sem("gla_squares")
    gor, sgr, t1r, pr, gwr = sem("gla_gate_products"), sem("gla_gate_sigmoid"), sem("gla_gated"), sem("gla_gated_o"), sem("gla_weighted")
    hr = sem("gla_h_ready")

    def sync(sp):
        before(sp)
        sp.dma_start(wqk, d["Wqk"]).then_inc(w_in, 16)
        sp.dma_start(wog, d["Wog"].rearrange("(k p) n -> p k n", p=P)).then_inc(w_in, 16)
        sp.dma_start(wig, d["Wig"].rearrange("(k p) n -> p k n", p=P)).then_inc(w_in, 16)
        sp.dma_start(gw, d["g_weight"].partition_broadcast(P)).then_inc(w_in, 16)
        sp.dma_start(mask, d["causal"]).then_inc(w_in, 16)

    def vector(v):
        norm.solve(v)
        over_tiles(v, lambda t, u: norm.apply(v, xn, hb, t).then_inc(xr, 1))
        c = norm.chain(v)
        c.put(v.memset(ss, 1.0))
        c.link(v.memset(bv, 0.0))
        norm.closed(c)
        PER = 7

        def queries(q):
            v.wait_ge(qsig, q + 1)
            src = ps[0:KH, 2 + q, :].rearrange("p (b n) -> p b n", b=4)
            bs = bass.ds(4 * q, 4)
            flat = bass.ds(4 * q * SEQ, 4 * SEQ)
            v.scalar_tensor_tensor(out=qs[:, bs, 1:SEQ], in0=src, scalar=SILU_SCALE, in1=sq[:, bs, 1:SEQ], op0=ALU.mult, op1=ALU.mult).then_inc(qkr, 1)
            c = Chain(v, norm.sem, norm.count + q * PER)
            starts = slice(1, SEQ, BL)
            v.wait_ge(asig, q + 1)
            c.put(v.tensor_copy(bv[:, bs, starts], av[:, bs, starts]))
            c.put(v.memset(bv[:, bs, 0], 1.0))
            c.wait()
            c.put(v.memset(av[:, bs, starts], 0.0))
            c.link(v.memset(av[:, bs, 0], 0.0))
            c.link(v.tensor_tensor_scan(F(pv)[:, flat], F(av)[:, flat], F(bv)[:, flat], 0.0, ALU.mult, ALU.add))
            c.link(v.reciprocal(F(av)[:, flat], F(pv)[:, flat]))
            v.wait_ge(qkr, q + 1)
            c.put(v.tensor_tensor(qs[:, bs, 1:SEQ], qs[:, bs, 1:SEQ], pv[:, bs, 1:SEQ], ALU.mult))
            v.tensor_tensor(kb0[:, bs, 1:SEQ], kb0[:, bs, 1:SEQ], av[:, bs, 1:SEQ], ALU.mult).then_inc(kbr, 1)
            assert c.n == PER

        for q in range(NQ):
            queries(q)
        norm.count += NQ * PER
        v.wait_ge(qsig, NQ + 1)
        v.scalar_tensor_tensor(out=qs[:, :, 0], in0=ps[0:KH, 6, 0:NB], scalar=SILU_SCALE, in1=sq[:, :, 0], op0=ALU.mult, op1=ALU.mult).then_inc(qkr, 1)
        v.wait_ge(ksig, NQ + 1)
        v.wait_ge(norm.sem, norm.count)
        v.wait_ge(kbr, NQ)
        for n in range(1, NBL):
            w = 1 + BL * n
            total = pv[:, :, BL * n:BL * n + 1]
            if n > 1:
                v.wait_ge(cp, n - 1)
            v.tensor_tensor(kb[n][:, :, 0:w], kb[n - 1][:, :, 0:w], bc(total, 2, w), ALU.mult).then_inc(kbr, 1)
            v.wait_ge(kbr, NQ + n)
        v.wait_ge(w_in, 5 * 16)
        own = ident[0:NB, 0:NB].unsqueeze(2)
        for n in range(NBL):
            v.wait_ge(acp, n + 1)
            v.tensor_tensor(atc[:, :, n * BL:(n + 1) * BL], ps[0:NB, n, :].rearrange("p (b n) -> p b n", b=NB), bc(own, 2, BL), ALU.mult).then_inc(atcr, 1)

        def masked(t, u):
            v.wait_ge(ap, t + 1)
            if not early(t):
                v.wait_ge(ob, t - 1)
            if tile_rows(t) == NB:
                v.tensor_tensor(ats[0:NB, u, 0:NB], ps[0:NB, u, 0:NB], ident[0:NB, 0:NB], ALU.mult).then_inc(atr, 1)
            else:
                v.tensor_tensor(ats[:, u], ps[:, u, 0:P], mask, ALU.mult).then_inc(atr, 1)

        def gated(t, u):
            r = tile_rows(t)
            v.wait_ge(sgr, t + 1)
            v.tensor_tensor(sg[0:r, u], ps[0:r, 6 + u, :], sg[0:r, u], ALU.mult).then_inc(t1r, 1)
            v.wait_ge(t1r, t + 1)
            if not early(t):
                v.wait_ge(gwr, t - 1)
            v.wait_ge(ssr, t + 1)
            v.tensor_tensor(pb[0:r, u], ps[0:r, 2 + u, :], sg[0:r, u], ALU.mult).then_inc(pr, 1)

        def finish(tiles, first, base):
            c = Chain(v, norm.sem, base)
            v.wait_ge(ssr, first + len(tiles))
            norm.newton(v, c, ss[:, bass.ds(first, len(tiles))], 1.0 / D, LN_EPS, bass.ds(first, len(tiles)))
            for t in tiles:
                r = tile_rows(t)
                v.wait_ge(gwr, t + 1)
                v.scalar_tensor_tensor(out=hb[0:r, t, :], in0=xn[0:r, t, :], scalar=norm.rstd[0:r, bass.ds(t, 1)], in1=hb[0:r, t, :], op0=ALU.mult, op1=ALU.add).then_inc(hr, 1)
                v.wait_ge(hr, t + 1)
                norm.take_stats(v, hb, t)
            return c.n + len(tiles)

        done = norm.count
        PER = Norm.NEWTON + 2

        def pair(i):
            for u in range(2):
                masked(2 * i + 2 + u, u)
                gated(2 * i + u, u)
            if not is_first(i):
                finish([2 * i - 2, 2 * i - 1], 2 * i - 2, done + (i - 1) * PER)

        masked(0, 0)
        masked(1, 1)
        looped(v, NB // 2 - 1, pair)
        done += (NB // 2 - 2) * PER
        masked(NB, 0)
        gated(NB - 2, 0)
        done += finish([NB - 4, NB - 3], NB - 4, done)
        gated(NB - 1, 1)
        gated(NB, 0)
        done += finish([NB - 2, NB - 1, NB], NB - 2, done)
        norm.count = done - T

    def gpsimd(p):
        p.wait_ge(w_in, 5 * 16)

        def weigh(t, u):
            r = tile_rows(t)
            p.wait_ge(pr, t + 1)
            if isinstance(t, int) and t == NB:
                p.wait_ge(ob, T)
            p.tensor_tensor(xn[0:r, t, :], pb[0:r, u], gw[0:r], ALU.mult).then_inc(gwr, 1)

        over_tiles(p, weigh)

    def scalar(s):
        def sigmoids(q, src_q, src_k, w, out):
            s.wait_ge(qk, q + 1)
            s.activation(out(sq), src_q, ACT.Sigmoid).then_inc(qsig, 1)
            s.activation(out(kb0), src_k, ACT.Sigmoid).then_inc(ksig, 1)
            s.wait_ge(ksig, q + 1)
            if not (isinstance(q, int) and q == NQ):
                s.activation(out(av), out(kb0), ACT.Sigmoid, scale=-1.0).then_inc(asig, 1)

        def turn(n):
            s.wait_ge(turned, n + 1)
            turned_out(s, ps[:, TURN_BANKS[n % 4], :], xnT, n).then_inc(tev, 1)

        for n in range(T):
            turn(n)
        split = (lambda x: x.rearrange("p (b n) -> p b n", b=4))
        for q in range(NQ):
            sigmoids(q, split(ps[0:KH, 2 + q, :]), split(ps[KH:2 * KH, 2 + q, :]), QC, lambda x: x[:, 4 * q:4 * q + 4, 1:SEQ])
        sigmoids(NQ, ps[0:KH, 6, 0:NB], ps[KH:2 * KH, 6, 0:NB], NB, lambda x: x[:, :, 0])
        for n in range(1, NBL):
            s.wait_ge(kbr, NQ - 1 + n)
            w = 1 + BL * n
            s.activation(kb[n][:, :, w:SEQ], kb0[:, :, w:SEQ], ACT.Copy).then_inc(cp, 1)

        def outs(t, u):
            r = tile_rows(t)
            s.wait_ge(ob, t + 1)
            if not early(t):
                s.wait_ge(gor, t - 1)
            s.activation(ots[:, u, :, 0:r], ps[:, 4 + u, 0:KD * r].rearrange("p (k n) -> p k n", k=KD), ACT.Copy).then_inc(otr, 1)
            if not (isinstance(t, int) and t == 0):
                s.wait_ge(ssr, t)
            s.activation(junk[0:r], ps[0:r, 2 + u, :], ACT.Square, accum_out=ss[0:r, bass.ds(t, 1)]).then_inc(ssr, 1)

        def gate(t, u):
            r = tile_rows(t)
            s.wait_ge(gor, t + 1)
            if not early(t):
                s.wait_ge(pr, t - 1)
            s.activation(sg[0:r, u], ps[0:r, 6 + u, :], ACT.Sigmoid).then_inc(sgr, 1)

        over_tiles(s, lambda t, u: (outs(t, u), gate(t, u)))

    def tensor(t):
        t.wait_ge(w_in, 5 * 16)

        def project(q, cols, w, bank):
            for k in range(KD):
                mm = t.matmul(ps[0:2 * KH, bank, 0:w], wqk[:, k, :], xnT[:, k, cols], start=(k == 0), stop=(k == KD - 1))
            mm.then_inc(qk, 1)

        for n in range(T):
            t.wait_ge(xr, n + 1)
            if n >= 4:
                t.wait_ge(tev, n - 3)
            turn_tile(t, ps[:, TURN_BANKS[n % 4], :], xn, n, ident).then_inc(turned, 1)
            if n == 7:
                project(0, slice(0, QC), QC, 2)
        t.wait_ge(tev, T)
        for q in range(1, NQ):
            project(q, slice(q * QC, (q + 1) * QC), QC, 2 + q)
        project(NQ, slice(NCOL, NTOK), NB, 6)
        t.wait_ge(cp, NBL - 1)
        t.wait_ge(kbr, NQ - 1 + NBL)
        t.wait_ge(qkr, NQ + 1)
        for n in range(NBL):
            t.matmul(ps[0:NB, n, :], kb[n][:, :, 0], qs[:, :, 1 + n * BL:1 + (n + 1) * BL], start=True, stop=True).then_inc(acp, 1)
        t.wait_ge(atcr, NBL)

        def attend(n):
            u = n % 2
            if n >= 2:
                t.wait_ge(atr, n - 1)
            if n == NB:
                t.matmul(ps[0:NB, u, 0:NB], kb0[:, :, 0], qs[:, :, 0], start=True, stop=True).then_inc(ap, 1)
                return
            for m in range(NBL):
                mm = t.matmul(ps[:, u, m * BL:(m + 1) * BL], kb[m][:, n, 1:SEQ], qs[:, n, 1 + m * BL:1 + (m + 1) * BL], start=True, stop=True)
            mm.then_inc(ap, 1)

        def outs(n):
            u, r = n % 2, tile_rows(n)
            t.wait_ge(atr, n + 1)
            if n >= 2:
                t.wait_ge(pr, n - 1)
                t.wait_ge(otr, n - 1)
            last = n == NB
            t.matmul(ps[0:r, 2 + u, :], ats[0:r, u, 0:r], xn[0:r, n, :], start=True, stop=last)
            if not last:
                t.matmul(ps[0:r, 2 + u, :], atc[:, n, :], xn[0:NB, NB, :], start=False, stop=True)
            for k in range(KD):
                ks = slice(k * P, (k + 1) * P)
                mm = t.matmul(ps[:, 4 + u, k * r:(k + 1) * r], xn[0:r, n, ks], ats[0:r, u, 0:r], start=True, stop=last)
                if not last:
                    mm = t.matmul(ps[:, 4 + u, k * r:(k + 1) * r], xn[0:NB, NB, ks], atc[:, n, :], start=False, stop=True)
            mm.then_inc(ob, 1)

        def gate(n):
            u, r = n % 2, tile_rows(n)
            cols = slice(NCOL, NTOK) if n == NB else slice(n * P, (n + 1) * P)
            t.wait_ge(otr, n + 1)
            if n >= 2:
                t.wait_ge(pr, n - 1)
            for k in range(KD):
                t.matmul(ps[0:r, 6 + u, :], xnT[:, k, cols], wig[:, k, :], start=(k == 0), stop=False)
            for k in range(KD):
                mm = t.matmul(ps[0:r, 6 + u, :], ots[:, u, k, 0:r], wog[:, k, :], start=False, stop=(k == KD - 1))
            mm.then_inc(gor, 1)

        attend(0)
        attend(1)
        for n in range(T):
            outs(n)
            if n + 2 < T:
                attend(n + 2)
            gate(n)

    return sync, vector, gpsimd, scalar, tensor, hr


ROUNDED = 2 * KD * NTOK + 448 + 4 * (2 * KD * P + D) + 4 * QC + 2 * NB
EXPERTS = NE * (KD * 2 * 352 + 3 * D)
HELD = T * D + P + 14 * T + 8
WORDS = 51 * 1024 - HELD - HELD % 8


class Shared:

    def __init__(self, nc, sem, held, arena):
        kept = Arena(held)
        self.h = kept.take(T, D)
        self.ident = kept.take(P)
        self.norm = Norm(kept, sem("norm_chain"))
        self.xn_at = arena.at
        self.xn = arena.take(T, D)
        self.y_at = arena.at
        self.y = arena.take(T, D)
        self.xnT = arena.take(KD, NTOK)
        self.scratch_at = arena.at
        self.h_ready = sem("h_after_scan")
        self.high_at = self.y_at + ROUNDED

    def look_through(self, nc, base):
        def over(name, start, end, dt=F32):
            return nc.alloc_sbuf_tensor_at(name, [P, end - start], dt, offset=base + 4 * start)

        self.low = over("moe_xn", self.xn_at, self.y_at)
        self.rounded = over("moe_rounded", self.y_at, self.high_at, F32R)
        self.experts = over("moe_experts", self.xn_at, self.xn_at + EXPERTS)
        self.high = over("moe_scratch", self.high_at, WORDS)


def tower(nc, d, out):
    with ExitStack() as ctx:
        def sem(name):
            return ctx.enter_context(nc.semaphore(name))

        held = ctx.enter_context(nc.sbuf_tensor("held", [P, HELD], F32))
        base = -(-nc.sbuf_base // 32) * 32
        sb = ctx.enter_context(nc.sbuf_tensor("sb", [P, WORDS], F32))
        ps = ctx.enter_context(nc.psum_tensor("ps", [P, 8, 512], F32))
        h0 = nc.dram_tensor("tokens", (NB, NH, D), F32).ap()
        dram = {"xn": nc.dram_tensor("xn_rows", (SPARE + 1, D), F32).ap(),
                "slots": nc.dram_tensor("slot_tokens", (NSLOT, 1), U32).ap(),
                "expert_out": nc.dram_tensor("expert_out", (SPARE + 1, D), F32).ap()}
        arena = Arena(sb)
        g = Shared(nc, sem, held, arena)
        g.look_through(nc, base)
        tok = tokenizer(nc, sem, sb, held, ps, d, h0)
        scan = scan_layer(nc, sem, sb, ps, d, h0, tok[5], g, g.scratch_at)
        ffn0 = ffn_layer(nc, sem, sb, ps, d, dram, g, "ffn0", 256, 4, True, lambda sp: sp.wait_ge(g.h_ready, T))
        gla = gla_layer(nc, sem, sb, ps, d, g, g.scratch_at, lambda sp: sp.wait_ge(ffn0[6], NTILE))
        ffn1 = ffn_layer(nc, sem, sb, ps, d, dram, g, "ffn1", 352, 11, False, lambda sp: sp.wait_ge(gla[5], T))
        h_out = sem("h_stored")
        block = ctx.enter_context(nc.Block())

        @block.sync
        def _(sp):
            tok[0](sp)
            scan[0](sp)
            ffn0[0](sp)
            gla[0](sp)
            ffn1[0](sp)

            def store(t, u):
                sp.wait_ge(ffn1[5], 2 * t + 2)
                if tile_rows(t) == P:
                    sp.dma_start(out[bass.ds(t, 1), 1:SEQ, :].rearrange("b p d -> (b p) d"), g.h[:, t, :]).then_inc(h_out, 16)
                else:
                    sp.dma_start(out[:, 0, :], g.h[0:NB, NB, :]).then_inc(h_out, 16)

            over_tiles(sp, store)
            sp.wait_ge(h_out, 16 * T)

        @block.vector
        def _(v):
            tok[1](v)
            scan[1](v)
            ffn0[1](v)
            gla[1](v)
            ffn1[1](v)

        @block.gpsimd
        def _(p):
            tok[2](p)
            scan[2](p)
            ffn0[2](p)
            gla[2](p)
            ffn1[2](p)

        @block.scalar
        def _(s):
            tok[3](s)
            scan[3](s)
            ffn0[3](s)
            gla[3](s)
            ffn1[3](s)

        @block.tensor
        def _(t):
            tok[4](t)
            scan[4](t)
            ffn0[4](t)
            gla[4](t)
            ffn1[4](t)


def laid_out(i):
    f = {k: np.asarray(v) for k, v in i.items()}
    t8 = np.arange(TB)
    k0 = np.concatenate([t8, TB * t8, TJ * t8, [0.5, 1, L // 2, L]])
    km = np.concatenate([np.repeat([TB - 1, TB * (TB - 1), TJ * (TB - 1)], TB), [0, 0, 0, 0]])

    def gate_up(gate, up):
        w = np.concatenate([gate, up], axis=2)
        n, _, c = w.shape
        return w.reshape(n, KD, P, c).transpose(0, 2, 1, 3)

    def cut(w, n):
        return w.reshape(w.shape[0], n, -1).transpose(1, 0, 2)

    def router(gate, shared):
        return np.concatenate([gate.T, shared.reshape(D, 1)], axis=1).reshape(KD, P, -1).transpose(1, 0, 2)

    T01 = (0, 2, 1)
    a = {
        "kconst": np.stack([k0, -km]).astype(np.float32),
        "lam": f["L0_tok_Lambda"],
        "log_dt": f["L0_tok_log_dt"].T,
        "x": f["x"].transpose(3, 2, 1, 0).reshape(2, NS, NH * NB),
        "ident": np.eye(P, dtype=np.float32),
        "W_in": f["L0_attn_W_in"], "W_fwd": f["L0_attn_W_fwd"], "W_bwd": f["L0_attn_W_bwd"], "W_out": f["L0_attn_W_out"],
        "gamma": f["L0_attn_gamma"], "beta": f["L0_attn_beta"],
        "iota8": np.arange(8, dtype=np.float32),
        "ffn0_router": router(f["L0_ffn_gate_w"], f["L0_ffn_se_gate_w"]),
        "ffn0_gate_up": gate_up(f["L0_ffn_w_gate"].transpose(T01), f["L0_ffn_w_up"].transpose(T01)),
        "ffn0_down": f["L0_ffn_w_down"].transpose(T01),
        "ffn0_sh_gate_up": gate_up(cut(f["L0_ffn_sh_gate"].T, 4), cut(f["L0_ffn_sh_up"].T, 4)),
        "ffn0_sh_down": f["L0_ffn_sh_down"].T.reshape(4, P, D),
        "Wqk": np.concatenate([f["L1_attn_Wq"].T, f["L1_attn_Wk"].T], axis=1).reshape(KD, P, -1).transpose(1, 0, 2),
        "Wog": f["L1_attn_Wog"].T, "Wig": f["L1_attn_Wig"].T, "g_weight": f["L1_attn_g_weight"],
        "causal": np.triu(np.ones((P, P), np.float32)),
        "ffn1_router": router(f["L1_ffn_gate_w"], f["L1_ffn_shared_gate_w"]),
        "ffn1_gate_up": gate_up(f["L1_ffn_w_gate"], f["L1_ffn_w_up"]),
        "ffn1_down": f["L1_ffn_w_down"],
        "ffn1_sh_gate_up": gate_up(cut(f["L1_ffn_sw_gate"], 11), cut(f["L1_ffn_sw_up"], 11)),
        "ffn1_sh_down": f["L1_ffn_sw_down"].reshape(11, P, D),
        "iota_tiles": np.arange(NTILE, dtype=np.float32),
        "valid": np.arange(T * P).reshape(T, P).T < NTOK,
        "before": np.triu(np.ones((P, P)), 1),
        "ones": np.ones((P, P)),
        "cls": np.broadcast_to(f["cls_tok"][0], (NB, D)),
    }
    a = {k: np.ascontiguousarray(v, np.float32) for k, v in a.items()}
    ids = np.arange(T * P).reshape(T, P).T
    a["token_ids"] = np.ascontiguousarray(np.stack([ids, CHOICE + ids], axis=1), np.int32)
    return a


def kernel(**inputs):
    import concourse.bacc as _bacc
    from concourse.bass_utils import run_bass_kernel_spmd as _run

    nc = _bacc.Bacc("TRN2", target_bir_lowering=False, num_devices=1)
    arrays, d = {}, {}
    for name, a in laid_out(inputs).items():
        arrays[f"in_{name}"] = a
        d[name] = nc.dram_tensor(f"in_{name}", a.shape, mybir.dt.from_np(a.dtype), kind="ExternalInput").ap()
    out = nc.dram_tensor("out", (NB, SEQ, D), F32, kind="ExternalOutput").ap()
    tower(nc, d, out)
    r = _run(nc, [arrays], core_ids=[0])
    return r.results[0]["out"]
```
